# Optimizing a Trainium2 kernel written in Bass

```python
import numpy as np
import jax
import jax.numpy as jnp

def _softmax(x, axis=-1):
    return jax.nn.softmax(x, axis=axis)

def _gelu(x):
    return jax.nn.gelu(x, approximate=True)

def _silu(x):
    return jax.nn.silu(x)

def _sigmoid(x):
    return jax.nn.sigmoid(x)

def _layernorm(x, axis=-1, eps=1e-05):
    m = jnp.mean(x, axis=axis, keepdims=True)
    v = jnp.var(x, axis=axis, keepdims=True)
    return (x - m) / jnp.sqrt(v + eps)

def _scatter_add(tgt, idx, src, axis=0):
    return tgt.at[idx].add(src)

def _segment_sum(src, seg, n):
    return jax.ops.segment_sum(src, seg, n)
kernel_name = 'mk_adaln_ffn_d2_seqx_r8_b8562f'

def setup_inputs(seed: int=0):
    np.random.seed(seed)
    _w = jnp.asarray

    def _rec_inputs():
        import jax
        import jax.numpy as jnp
        _rk = jax.random.key(seed)
        x = -7.109e-05 + 0.9999 * jax.random.normal(jax.random.fold_in(_rk, 1), (128, 32, 128), jnp.float32)
        _lenS = 32 - jax.random.randint(jax.random.fold_in(_rk, 7), (128,), 0, max(1, 32 // 4) + 1, jnp.int32)
        _lenS2 = 32 - jax.random.randint(jax.random.fold_in(_rk, 8), (128,), 0, max(1, 32 // 4) + 1, jnp.int32)
        itok_B_0_15 = jax.random.randint(jax.random.fold_in(_rk, 11), (128,), 0, 16, jnp.int32)
        itok_B_0_8 = jax.random.randint(jax.random.fold_in(_rk, 12), (128,), 0, 9, jnp.int32)
        return (x, itok_B_0_15, itok_B_0_8)
    x, itok_B_0_15, itok_B_0_8 = _rec_inputs()

    def _L0_cond_setup():
        import jax, jax.numpy as jnp
        import numpy as np
        B, N, C_IN, C_OUT, S = (64, 128, 128, 128, 16)
        key = jax.random.key(seed)
        kx, ks, kw, kb = jax.random.split(key, 4)
        scale = 1.0 / np.sqrt(C_IN)
        x = jax.random.normal(kx, (B, N, C_IN), dtype=jnp.float32)
        subjects = jax.random.randint(ks, (B,), 0, S, dtype=jnp.int64)
        weights = jax.random.normal(kw, (S, C_IN, C_OUT), dtype=jnp.float32) * scale
        b = jax.random.normal(kb, (S, C_OUT), dtype=jnp.float32) * scale
        return {'x': x, 'subjects': subjects, 'weights': weights, 'b': b}
    _L0_cond_all = _L0_cond_setup()
    _L0_cond_in = {k: v for k, v in _L0_cond_all.items() if k in ('weights', 'b')}
    del _L0_cond_all

    def _L0_ffn_setup():
        import jax, jax.numpy as jnp
        import numpy as np
        E = 16
        H = 128
        F = 256
        TOP_K = 1
        B, S = (2, 128)
        key = jax.random.key(seed)
        ks = jax.random.split(key, 7)
        s = 0.02
        return {'hidden_states': jax.random.normal(ks[0], (B, S, H), jnp.float32), 'w_router': jax.random.normal(ks[1], (E, H), jnp.float32) * s, 'gate_up_proj': jax.random.normal(ks[2], (E, H, 2 * F), jnp.float32) * s, 'down_proj': jax.random.normal(ks[3], (E, F, H), jnp.float32) * s, 'w_gate': jax.random.normal(ks[4], (F, H), jnp.float32) * s, 'w_up': jax.random.normal(ks[5], (F, H), jnp.float32) * s, 'w_down': jax.random.normal(ks[6], (H, F), jnp.float32) * s}
    _L0_ffn_all = _L0_ffn_setup()
    _L0_ffn_in = {k: v for k, v in _L0_ffn_all.items() if k in ('w_router', 'gate_up_proj', 'down_proj', 'w_gate', 'w_up', 'w_down')}
    del _L0_ffn_all

    def _L1_cond_setup():
        import jax, jax.numpy as jnp
        import numpy as np
        LN_EPS = 1e-05
        key = jax.random.key(seed)
        ks = jax.random.split(key, 8)
        B, S, H, A, L = (32, 256, 128, 32, 10)
        return {'hidden_states': jax.random.normal(ks[0], (B, S, H), dtype=jnp.float32), 'language_ids': jax.random.randint(ks[1], (B,), 0, L, dtype=jnp.int64), 'W1': jax.random.normal(ks[2], (L, H, A), dtype=jnp.float32) * (1.0 / np.sqrt(H)), 'b1': jnp.zeros((L, A), dtype=jnp.float32), 'W2': jax.random.normal(ks[3], (L, A, H), dtype=jnp.float32) * (1.0 / np.sqrt(A)), 'b2': jnp.zeros((L, H), dtype=jnp.float32), 'gamma': jnp.ones((L, H), dtype=jnp.float32), 'beta': jnp.zeros((L, H), dtype=jnp.float32)}
    _L1_cond_all = _L1_cond_setup()
    _L1_cond_in = {k: v for k, v in _L1_cond_all.items() if k in ('W1', 'b1', 'W2', 'b2', 'gamma', 'beta')}
    del _L1_cond_all

    def _L1_ffn_setup():
        import math
        import jax, jax.numpy as jnp
        import numpy as np
        H = 128
        F = 512
        E = 8
        TOP_K = 2
        CAP_FACTOR = 1.25
        MIN_CAP = 4
        SHARED_SCALE = 0.1

        def _top2_gating(logits, capacity):
            N, nE = logits.shape
            gates = jax.nn.softmax(logits, axis=-1)
            idx1 = jnp.argmax(gates, axis=-1)
            mask1 = jax.nn.one_hot(idx1, nE, dtype=gates.dtype)
            idx2 = jnp.argmax(gates * (1.0 - mask1), axis=-1)
            mask2 = jax.nn.one_hot(idx2, nE, dtype=gates.dtype)
            pos1 = jnp.cumsum(mask1, axis=0) - mask1
            mask1 = mask1 * (pos1 < capacity)
            pos2 = jnp.cumsum(mask2, axis=0) - mask2 + jnp.sum(mask1, axis=0, keepdims=True)
            mask2 = mask2 * (pos2 < capacity)
            g1 = jnp.sum(gates * mask1, axis=-1)
            g2 = jnp.sum(gates * mask2, axis=-1)
            denom = jnp.maximum(g1 + g2, jnp.finfo(gates.dtype).eps)
            g1, g2 = (g1 / denom, g2 / denom)
            loc1 = jnp.sum(pos1 * mask1, axis=-1).astype(jnp.int32)
            loc2 = jnp.sum(pos2 * mask2, axis=-1).astype(jnp.int32)
            oh1 = jax.nn.one_hot(loc1, capacity, dtype=gates.dtype)
            oh2 = jax.nn.one_hot(loc2, capacity, dtype=gates.dtype)
            combine = (g1[:, None] * mask1)[:, :, None] * oh1[:, None, :] + (g2[:, None] * mask2)[:, :, None] * oh2[:, None, :]
            dispatch = (combine > 0).astype(gates.dtype)
            return (combine, dispatch)
        key = jax.random.key(seed)
        ks = jax.random.split(key, 10)
        s_h = 1.0 / math.sqrt(H)
        s_f = 1.0 / math.sqrt(F)
        return {'hidden_states': jax.random.normal(ks[0], (2, 256, H), jnp.float32), 'router_w': jax.random.uniform(ks[1], (H, E), jnp.float32, -s_h, s_h), 'w1': jax.random.uniform(ks[2], (E, H, F), jnp.float32, -s_h, s_h), 'b1': jax.random.uniform(ks[3], (E, F), jnp.float32, -s_h, s_h), 'w2': jax.random.uniform(ks[4], (E, F, H), jnp.float32, -s_f, s_f), 'b2': jax.random.uniform(ks[5], (E, H), jnp.float32, -s_f, s_f), 'sw1': jax.random.uniform(ks[6], (H, F), jnp.float32, -s_h, s_h), 'sb1': jax.random.uniform(ks[7], (F,), jnp.float32, -s_h, s_h), 'sw2': jax.random.uniform(ks[8], (F, H), jnp.float32, -s_f, s_f), 'sb2': jax.random.uniform(ks[9], (H,), jnp.float32, -s_f, s_f)}
    _L1_ffn_all = _L1_ffn_setup()
    _L1_ffn_in = {k: v for k, v in _L1_ffn_all.items() if k in ('router_w', 'w1', 'b1', 'w2', 'b2', 'sw1', 'sb1', 'sw2', 'sb2')}
    del _L1_ffn_all
    return {'x': x, 'itok_B_0_15': itok_B_0_15, 'itok_B_0_8': itok_B_0_8, 'L0_cond_weights': _L0_cond_in['weights'], 'L0_cond_b': _L0_cond_in['b'], 'L0_ffn_w_router': _L0_ffn_in['w_router'], 'L0_ffn_gate_up_proj': _L0_ffn_in['gate_up_proj'], 'L0_ffn_down_proj': _L0_ffn_in['down_proj'], 'L0_ffn_w_gate': _L0_ffn_in['w_gate'], 'L0_ffn_w_up': _L0_ffn_in['w_up'], 'L0_ffn_w_down': _L0_ffn_in['w_down'], 'L1_cond_W1': _L1_cond_in['W1'], 'L1_cond_b1': _L1_cond_in['b1'], 'L1_cond_W2': _L1_cond_in['W2'], 'L1_cond_b2': _L1_cond_in['b2'], 'L1_cond_gamma': _L1_cond_in['gamma'], 'L1_cond_beta': _L1_cond_in['beta'], 'L1_ffn_router_w': _L1_ffn_in['router_w'], 'L1_ffn_w1': _L1_ffn_in['w1'], 'L1_ffn_b1': _L1_ffn_in['b1'], 'L1_ffn_w2': _L1_ffn_in['w2'], 'L1_ffn_b2': _L1_ffn_in['b2'], 'L1_ffn_sw1': _L1_ffn_in['sw1'], 'L1_ffn_sb1': _L1_ffn_in['sb1'], 'L1_ffn_sw2': _L1_ffn_in['sw2'], 'L1_ffn_sb2': _L1_ffn_in['sb2']}

def reference(x, itok_B_0_15, itok_B_0_8, L0_cond_weights, L0_cond_b, L0_ffn_w_router, L0_ffn_gate_up_proj, L0_ffn_down_proj, L0_ffn_w_gate, L0_ffn_w_up, L0_ffn_w_down, L1_cond_W1, L1_cond_b1, L1_cond_W2, L1_cond_b2, L1_cond_gamma, L1_cond_beta, L1_ffn_router_w, L1_ffn_w1, L1_ffn_b1, L1_ffn_w2, L1_ffn_b2, L1_ffn_sw1, L1_ffn_sb1, L1_ffn_sw2, L1_ffn_sb2):
    import jax
    import jax.numpy as jnp

    def _L0_cond_ref(x, subjects, weights, b):
        import jax, jax.numpy as jnp
        import numpy as np
        B, N, C_IN, C_OUT, S = (64, 128, 128, 128, 16)
        w = weights[subjects]
        out = jnp.einsum('bnc,bcd->bnd', x, w)
        out = out + b[subjects][:, None, :]
        return out

    def _L0_ffn_ref(hidden_states, w_router, gate_up_proj, down_proj, w_gate, w_up, w_down):
        import jax, jax.numpy as jnp
        import numpy as np
        E = 16
        H = 128
        F = 256
        TOP_K = 1
        B, S = (2, 128)
        b, s, h = hidden_states.shape
        x = hidden_states.reshape(-1, h)
        logits = x @ w_router.T
        _, top_idx = jax.lax.top_k(logits, TOP_K)
        mask = jax.nn.one_hot(top_idx, E, dtype=logits.dtype).sum(axis=1)
        scores = jax.nn.sigmoid(logits) * mask
        masked_inputs = scores.T[:, :, None] * x[None, :, :]
        gate_up = jnp.einsum('eth,ehf->etf', masked_inputs, gate_up_proj)
        gate, up = jnp.split(gate_up, 2, axis=-1)
        expert_out = jnp.einsum('etf,efh->eth', up * jax.nn.silu(gate), down_proj)
        shared = jax.nn.silu(x @ w_gate.T) * (x @ w_up.T) @ w_down.T
        out = shared + expert_out.sum(axis=0)
        return out.reshape(b, s, h)

    def _L1_cond_ref(hidden_states, language_ids, W1, b1, W2, b2, gamma, beta):
        import jax, jax.numpy as jnp
        import numpy as np
        LN_EPS = 1e-05
        w1 = W1[language_ids]
        w2 = W2[language_ids]
        h = jnp.einsum('bsh,bha->bsa', hidden_states, w1) + b1[language_ids][:, None, :]
        h = jax.nn.relu(h)
        adapted = jnp.einsum('bsa,bah->bsh', h, w2) + b2[language_ids][:, None, :]
        x = hidden_states + adapted
        mean = jnp.mean(x, axis=-1, keepdims=True)
        var = jnp.mean(jnp.square(x - mean), axis=-1, keepdims=True)
        normed = (x - mean) * jax.lax.rsqrt(var + LN_EPS)
        return normed * gamma[language_ids][:, None, :] + beta[language_ids][:, None, :]

    def _L1_ffn_ref(hidden_states, router_w, w1, b1, w2, b2, sw1, sb1, sw2, sb2):
        import math
        import jax, jax.numpy as jnp
        import numpy as np
        H = 128
        F = 512
        E = 8
        TOP_K = 2
        CAP_FACTOR = 1.25
        MIN_CAP = 4
        SHARED_SCALE = 0.1

        def _top2_gating(logits, capacity):
            N, nE = logits.shape
            gates = jax.nn.softmax(logits, axis=-1)
            idx1 = jnp.argmax(gates, axis=-1)
            mask1 = jax.nn.one_hot(idx1, nE, dtype=gates.dtype)
            idx2 = jnp.argmax(gates * (1.0 - mask1), axis=-1)
            mask2 = jax.nn.one_hot(idx2, nE, dtype=gates.dtype)
            pos1 = jnp.cumsum(mask1, axis=0) - mask1
            mask1 = mask1 * (pos1 < capacity)
            pos2 = jnp.cumsum(mask2, axis=0) - mask2 + jnp.sum(mask1, axis=0, keepdims=True)
            mask2 = mask2 * (pos2 < capacity)
            g1 = jnp.sum(gates * mask1, axis=-1)
            g2 = jnp.sum(gates * mask2, axis=-1)
            denom = jnp.maximum(g1 + g2, jnp.finfo(gates.dtype).eps)
            g1, g2 = (g1 / denom, g2 / denom)
            loc1 = jnp.sum(pos1 * mask1, axis=-1).astype(jnp.int32)
            loc2 = jnp.sum(pos2 * mask2, axis=-1).astype(jnp.int32)
            oh1 = jax.nn.one_hot(loc1, capacity, dtype=gates.dtype)
            oh2 = jax.nn.one_hot(loc2, capacity, dtype=gates.dtype)
            combine = (g1[:, None] * mask1)[:, :, None] * oh1[:, None, :] + (g2[:, None] * mask2)[:, :, None] * oh2[:, None, :]
            dispatch = (combine > 0).astype(gates.dtype)
            return (combine, dispatch)
        B, S, h = hidden_states.shape
        x = hidden_states.reshape(-1, h)
        N = x.shape[0]
        capacity = min(max(MIN_CAP, math.ceil(TOP_K * CAP_FACTOR * N / E)), N)
        logits = x @ router_w
        combine, dispatch = _top2_gating(logits, capacity)
        expert_in = jnp.einsum('nec,nh->ech', dispatch, x)
        hmid = jax.nn.silu(jnp.einsum('ech,ehf->ecf', expert_in, w1) + b1[:, None, :])
        expert_out = jnp.einsum('ecf,efh->ech', hmid, w2) + b2[:, None, :]
        y = jnp.einsum('nec,ech->nh', combine, expert_out)
        shared = jax.nn.silu(x @ sw1 + sb1) @ sw2 + sb2
        out = y + SHARED_SCALE * shared
        return out.reshape(B, S, h)
    x = x + _L0_ffn_ref(_L0_cond_ref(x, itok_B_0_15, L0_cond_weights, L0_cond_b), L0_ffn_w_router, L0_ffn_gate_up_proj, L0_ffn_down_proj, L0_ffn_w_gate, L0_ffn_w_up, L0_ffn_w_down)
    x = x + _L1_ffn_ref(_L1_cond_ref(x, itok_B_0_8, L1_cond_W1, L1_cond_b1, L1_cond_W2, L1_cond_b2, L1_cond_gamma, L1_cond_beta), L1_ffn_router_w, L1_ffn_w1, L1_ffn_b1, L1_ffn_w2, L1_ffn_b2, L1_ffn_sw1, L1_ffn_sb1, L1_ffn_sw2, L1_ffn_sb2)
    return x

_drawn_inputs = setup_inputs


def setup_inputs(seed=0):
    import zlib

    import numpy as np

    out = dict(_drawn_inputs(seed))
    spreads = {'L1_cond_b1': (0.0, 2.0),
     'L1_cond_b2': (0.0, 2.0),
     'L1_cond_gamma': (1.0, 0.6),
     'L1_cond_beta': (0.0, 0.8)}
    factors = {'L0_cond_weights': 4.116,
     'L0_cond_b': 8.0,
     'L0_ffn_w_router': 8.0,
     'L0_ffn_gate_up_proj': 8.0,
     'L0_ffn_down_proj': 8.0,
     'L0_ffn_w_gate': 4.247,
     'L0_ffn_w_up': 4.282,
     'L0_ffn_w_down': 4.589,
     'L1_ffn_b1': 36.024,
     'L1_ffn_b2': 195.52,
     'L1_ffn_sw1': 24.592,
     'L1_ffn_sb1': 64.0,
     'L1_ffn_sw2': 23.552,
     'L1_ffn_sb2': 200.0,
     'L1_cond_W1': 8.0,
     'L1_cond_W2': 8.0,
     'L1_ffn_router_w': 8.0,
     'L1_ffn_w1': 8.0,
     'L1_ffn_w2': 8.0}
    for name, (base, spread) in spreads.items():
        noise = np.random.default_rng([zlib.crc32(name.encode()), seed]).standard_normal(out[name].shape)
        drawn = base * np.exp(spread * noise) if base else spread * noise
        out[name] = jnp.asarray(drawn.astype(out[name].dtype))
    for name, factor in factors.items():
        out[name] = (out[name] * factor).astype(out[name].dtype)
    return out
```

```python
import concourse.bass as bass
from concourse import mybir
from contextlib import ExitStack


def adaln_moe_two_layers(
    nc: bass.Bass,
    x: bass.AP,
    subj: bass.AP,
    lang: bass.AP,
    c0_w: bass.AP,
    c0_b: bass.AP,
    f0_router: bass.AP,
    f0_gate_up: bass.AP,
    f0_down: bass.AP,
    f0_sh_gate: bass.AP,
    f0_sh_up: bass.AP,
    f0_sh_down: bass.AP,
    c1_w1: bass.AP,
    c1_b1: bass.AP,
    c1_w2: bass.AP,
    c1_b2: bass.AP,
    c1_gamma: bass.AP,
    c1_beta: bass.AP,
    f1_router: bass.AP,
    f1_w1: bass.AP,
    f1_b1: bass.AP,
    f1_w2: bass.AP,
    f1_b2: bass.AP,
    f1_sh_w1: bass.AP,
    f1_sh_b1: bass.AP,
    f1_sh_w2: bass.AP,
    f1_sh_b2: bass.AP,
    out: bass.AP,
):
    fp32 = mybir.dt.float32
    bf16 = mybir.dt.bfloat16
    i32 = mybir.dt.int32
    ALU = mybir.AluOpType
    ACT = mybir.ActivationFunctionType
    AX = mybir.AxisListType
    ds = bass.ds

    P = 128
    T, H = x.shape
    B = subj.shape[1]
    S = T // B
    NSUB = c0_w.shape[0]
    E0, _, F0x2 = f0_gate_up.shape
    F0 = F0x2 // 2
    C0 = F0 // P
    NLANG = c1_b2.shape[0]
    A = c1_w1.shape[1] // NLANG
    E1, _, F1 = f1_w1.shape
    C1 = F1 // P
    TOP_K = 2
    CAP = min(max(4, -(-TOP_K * 5 * T // (4 * E1))), T)
    SHARED_SCALE = 0.1
    LN_EPS = 1e-5
    TINY = 1.1920929e-07

    NT = T // P
    G = 4
    NG = NT // G
    GB = G * P // S
    GP = G * P
    QB = P // S
    NBLK = NT + E0 - 1
    NBLKP = -(-NBLK // 4) * 4
    U = 2
    UP = U * P
    GPE = CAP // UP
    NQ = E1 * GPE
    ROW = H + 1
    FAR = 65536
    DROP = 16384
    HID = NLANG * A
    NCH = -(-HID // P)
    TAIL = HID - (NCH - 1) * P
    LASTK = TAIL + NLANG
    KROWS = [P] * (NCH - 1) + [LASTK]
    assert CAP % UP == 0 and TAIL % 32 == 0 and NG % 2 == 0 and E1 % 2 == 0 and GPE % 2 == 1

    rows0 = nc.dram_tensor("rows0", (NBLKP * P, ROW), fp32).ap()
    back0 = nc.dram_tensor("back0", (T, H), fp32).ap()
    rows1 = nc.dram_tensor("rows1", (E1 * CAP, ROW), fp32).ap()
    back1 = nc.dram_tensor("back1", (TOP_K * T, H), fp32).ap()

    x_g = x.rearrange("(g i p) h -> g p i h", p=P, i=G)
    out_g = out.rearrange("(g i p) h -> g p i h", p=P, i=G)
    back0_g = back0.rearrange("(g i p) h -> g p i h", p=P, i=G)
    back1_g = back1.rearrange("(k g i p) h -> k g p i h", p=P, i=G, k=TOP_K)
    rows0_b = rows0.rearrange("(j p) r -> j p r", p=P)
    rows1_q = rows1.rearrange("(q u p) r -> q p u r", p=P, u=U)

    ctx = ExitStack()
    with ctx:
        def sb(name, shape, dt=fp32):
            return ctx.enter_context(nc.sbuf_tensor(name, shape, dt))

        def sem(name):
            return ctx.enter_context(nc.semaphore(name))

        acc = sb("acc", [P, NT, H])
        featT = sb("featT", [P, T])
        disp = sb("disp", [P, NT, ROW])
        c0w = sb("c0w", [P, NSUB * H])
        w_gu = sb("w_gu", [P, E0 * F0x2])
        w_dn = sb("w_dn", [P, E0 * C0 * H])
        shg = sb("shg", [P, F0])
        shu = sb("shu", [P, F0])
        shd = sb("shd", [P, C0, H])
        rt0 = sb("rt0", [P, E0])
        rt1 = sb("rt1", [P, E1])
        c0bs = sb("c0bs", [NSUB, H])
        gam = sb("gam", [NLANG, H])
        bet = sb("bet", [NLANG, H])
        a_w1 = sb("a_w1", [P, (NCH - 1) * P + LASTK])
        a_w2 = sb("a_w2", [P, NCH, H])
        a_b1 = sb("a_b1", [P, NCH])
        sw1 = sb("sw1", [P, F1])
        sw2 = sb("sw2", [P, C1, H])
        sb1 = sb("sb1", [P, C1])
        sb2 = sb("sb2", [P, H])
        xT = [sb(f"xT{k}", [P, GP]) for k in range(2)]
        condS = sb("condS", [S, GB, H])
        act = [sb(f"act{k}", [P, C1, GP]) for k in range(2)]
        sil = sb("sil", [P, C0, GP])
        x1g = [sb(f"x1g{k}", [P, G, H]) for k in range(2)]
        y0g = [sb(f"y0g{k}", [P, G, H]) for k in range(2)]
        nrm = [sb(f"nrm{k}", [P, G, H]) for k in range(2)]
        w1r = [w_gu[:, k * F1:(k + 1) * F1] for k in range(2)]
        w2r = [w_gu[:, (2 + k) * F1:(3 + k) * F1].rearrange("p (c h) -> p c h", c=C1) for k in range(2)]
        b1r = [sb(f"b1r{k}", [P, C1]) for k in range(2)]
        b2r = [sb(f"b2r{k}", [P, H]) for k in range(2)]
        blk_x = [sb(f"blk_x{s}", [P, ROW]) for s in range(4)]
        blk_y = [sb(f"blk_y{s}", [P, H]) for s in range(4)]
        blk_i = [sb(f"blk_i{s}", [P, 1], i32) for s in range(4)]
        blk_xT = [sb(f"blk_xT{k}", [P, P]) for k in range(2)]
        blk_s = [sb(f"blk_s{k}", [P, F0]) for k in range(2)]
        blk_a = [sb(f"blk_a{k}", [P, F0]) for k in range(2)]
        blk_aT = [sb(f"blk_aT{k}", [P, F0]) for k in range(2)]
        grp_x = [sb(f"grp_x{k}", [P, U, ROW]) for k in range(2)]
        grp_y = [sb(f"grp_y{k}", [P, U, H]) for k in range(2)]
        grp_i = [sb(f"grp_i{k}", [P, U], i32) for k in range(2)]
        zrow = sb("zrow", [P, 1032])
        ident = sb("ident", [P, P])
        tri = sb("tri", [P, P], bf16)
        ones_b = sb("ones_b", [P, P], bf16)
        codes = sb("codes", [P, NT])
        subjI = sb("subjI", [NSUB, B], i32)
        langI = sb("langI", [P, B], i32)
        w0off = sb("w0off", [1, B], i32)
        rowI = sb("rowI", [P, 1], i32)
        rowL = sb("rowL", [P, NCH + 1])
        rowLi = sb("rowLi", [P, NCH + 1], i32)
        hot0 = sb("hot0", [NSUB, B])
        hot1 = sb("hot1", [NLANG, B])
        lmask = sb("lmask", [P, NCH, B])
        c0bT = sb("c0bT", [P, B])
        gamT = sb("gamT", [P, B])
        betT = sb("betT", [P, B])
        W = NT * E0
        assert W == NT * TOP_K * E1 and W == 512
        lg = sb("lg", [P, W])
        t1 = sb("t1", [P, W])
        t2 = sb("t2", [P, W])
        t3 = sb("t3", [P, W])
        mask = sb("mask", [P, W], bf16)
        rst = sb("rst", [P, W])
        incl = sb("incl", [P, W])
        revE = sb("revE", [P, E0])
        baseE = sb("baseE", [P, E1])
        m1 = sb("m1", [P, NT])
        m2 = sb("m2", [P, NT])
        m3 = sb("m3", [P, NT])
        wk = sb("wk", [P, TOP_K, NT])
        score = sb("score", [P, NT])
        slotF = sb("slotF", [P, TOP_K, NT])
        slot = sb("slot", [P, TOP_K, NT], i32)
        padI = sb("padI", [P, E0], i32)
        padF = sb("padF", [P, E0])
        endE = sb("endE", [P, E0])
        ones_f = sb("ones_f", [P, E0])
        jrow = sb("jrow", [1, NBLKP])
        cmpj = sb("cmpj", [1, NBLKP, E0 - 1])
        bexp = sb("bexp", [1, NBLKP])
        guo = sb("guo", [1, NBLKP], i32)
        dno = sb("dno", [1, NBLKP], i32)
        cnt1 = sb("cnt1", [P, E1])
        bn6 = sb("bn6", [P, G, 6])
        mv = sb("mv", [P, G, 2])
        rstd = sb("rstd", [P, G])
        epsc = sb("epsc", [P, 1])

        PS = [ctx.enter_context(nc.psum_tensor(f"PS{i}", [P, 512], fp32)) for i in range(8)]

        x_ld = [sem(f"x_ld{g}") for g in range(NG)]
        ld_small = sem("ld_small")
        ld_c0w = sem("ld_c0w")
        ld_tab = sem("ld_tab")
        ld_sh0 = sem("ld_sh0")
        ld_gu = sem("ld_gu")
        ld_dn = sem("ld_dn")
        ld_l1 = sem("ld_l1")
        zero0 = sem("zero0")
        zero1 = sem("zero1")
        poolk = sem("poolk")
        dch = sem("dch")
        dve_ready = sem("dve_ready")
        pe_tab = sem("pe_tab")
        tab_done = sem("tab_done")
        pe_xt = sem("pe_xt")
        xT_done = sem("xT_done")
        pe_c = sem("pe_c")
        condA = sem("condA")
        condD = sem("condD")
        pe_ht = sem("pe_ht")
        hT_done = sem("hT_done")
        pe_l = sem("pe_l")
        lg_done = sem("lg_done")
        pe_tok = sem("pe_tok")
        tok_done = sem("tok_done")
        mx0 = sem("mx0")
        sg0 = sem("sg0")
        mk0 = sem("mk0")
        pe_rank0 = sem("pe_rank0")
        slots0 = sem("slots0")
        blocks0 = sem("blocks0")
        scaled = sem("scaled")
        sc0 = sem("sc0")
        pe_gu = sem("pe_gu")
        sil_done = sem("sil_done")
        act_done = sem("act_done")
        pe_dn = sem("pe_dn")
        acc0 = sem("acc0")
        bx_ld = [sem(f"bx_ld{s}") for s in range(4)]
        by_st = [sem(f"by_st{s}") for s in range(4)]
        e_xt = sem("e_xt")
        e_xc = sem("e_xc")
        e_gu = sem("e_gu")
        e_sl = sem("e_sl")
        e_ac = sem("e_ac")
        e_ta = sem("e_ta")
        e_at = sem("e_at")
        e_dn = sem("e_dn")
        e_oc = sem("e_oc")
        e_ix = sem("e_ix")
        y0_ld = [sem(f"y0_ld{k}") for k in range(2)]
        x1_done = sem("x1_done")
        res_done = sem("res_done")
        b_xt = sem("b_xt")
        b_xc = sem("b_xc")
        b_w1 = sem("b_w1")
        b_rl = sem("b_rl")
        b_mk = sem("b_mk")
        b_w2 = sem("b_w2")
        b_var = sem("b_var")
        b_std = sem("b_std")
        b_nm = sem("b_nm")
        b_nt = sem("b_nt")
        b_xn = sem("b_xn")
        b_lg = sem("b_lg")
        b_lc = sem("b_lc")
        b_bt = sem("b_bt")
        b_tk = sem("b_tk")
        ex_in = sem("ex_in")
        ex_out = sem("ex_out")
        mk1 = sem("mk1")
        pe_rank1 = sem("pe_rank1")
        slots1 = sem("slots1")
        codes0 = sem("codes0")
        codes1 = sem("codes1")
        sc1 = sem("sc1")
        s_gu = sem("s_gu")
        s_sl = sem("s_sl")
        s_dn = sem("s_dn")
        s_ac = sem("s_ac")
        gx_ld = [sem(f"gx_ld{k}") for k in range(2)]
        gy_st = [sem(f"gy_st{k}") for k in range(2)]
        w_ld = [sem(f"w_ld{k}") for k in range(2)]
        q_xt = sem("q_xt")
        q_xc = sem("q_xc")
        q_gu = sem("q_gu")
        q_sl = sem("q_sl")
        q_dn = sem("q_dn")
        q_oc = sem("q_oc")
        q_ix = sem("q_ix")
        fy_ld = [sem(f"fy_ld{k}") for k in range(2)]
        f_ac = sem("f_ac")
        o_st = sem("o_st")
        pool_turn = sem("pool_turn")

        block = ctx.enter_context(nc.Block())
        mm = nc.tensor.matmul

        def at(ap, i):
            return ap[i] if isinstance(i, int) else ap[ds(i, 1)].squeeze(0)

        def tile(buf, i):
            return buf[:, i * P:(i + 1) * P]

        @block.sync
        def _(sp):
            sp.dma_start(w0off[:, :], subj).then_inc(ld_small, 16)
            sp.dma_start(subjI[:, :], subj.partition_broadcast(NSUB)).then_inc(ld_tab, 16)
            sp.dma_start(langI[:, :], lang.partition_broadcast(P)).then_inc(ld_tab, 16)
            sp.dma_start(acc[:, 0:G, :], x_g[0]).then_inc(x_ld[0], 16)
            for dst, src in ((c0bs[:, :], c0_b), (gam[:, :], c1_gamma), (bet[:, :], c1_beta),
                             (rt0[:, :], f0_router), (rt1[:, :], f1_router)):
                sp.dma_start(dst, src).then_inc(ld_tab, 16)
            for g in range(1, NG):
                sp.dma_start(acc[:, g * G:(g + 1) * G, :], x_g[g]).then_inc(x_ld[g], 16)
            sp.dma_start(shg[:, :], f0_sh_gate).then_inc(ld_sh0, 16)
            sp.dma_start(shu[:, :], f0_sh_up).then_inc(ld_sh0, 16)
            sp.dma_start(shd[:, :, :], f0_sh_down.rearrange("(c p) h -> p c h", p=P)).then_inc(ld_sh0, 16)
            sp.wait_ge(poolk, 1)
            zw = ROW * 4
            for r in range(0, NBLKP * P, P * 4):
                sp.dma_start(rows0[r:r + P * 4, :].rearrange("(p a) r -> p (a r)", p=P),
                             zrow[:, 0:zw]).then_inc(zero0, 16)
            sp.dma_start(w_gu[:, :].rearrange("p (e f) -> p e f", e=E0),
                         f0_gate_up.rearrange("e p f -> p e f")).then_inc(ld_gu, 16)
            sp.dma_start(w_dn[:, :].rearrange("p (e c h) -> p e c h", e=E0, c=C0),
                         f0_down.rearrange("e (c p) h -> p e c h", p=P)).then_inc(ld_dn, 16)
            for r in range(0, E1 * CAP, P * 4):
                sp.dma_start(rows1[r:r + P * 4, :].rearrange("(p a) r -> p (a r)", p=P),
                             zrow[:, 0:zw]).then_inc(zero1, 16)
            for r in range(0, TOP_K * T, P * 8):
                sp.dma_start(back1[r:r + P * 8, :].rearrange("(p a) h -> p (a h)", p=P),
                             zrow[:, 0:8 * H]).then_inc(zero1, 16)
            sp.wait_ge(dve_ready, 1)
            sp.dma_start(a_w1[:, 0:HID], c1_w1).then_inc(ld_l1, 16)
            for c in range(NCH - 1):
                sp.dma_start(a_w2[:, c, :], c1_w2[c * P:(c + 1) * P, :]).then_inc(ld_l1, 16)
                sp.dma_start(a_b1[:, c:c + 1], c1_b1[c * P:(c + 1) * P, :]).then_inc(ld_l1, 16)
            c = NCH - 1
            sp.dma_start(a_w2[0:TAIL, c, :], c1_w2[c * P:HID, :]).then_inc(ld_l1, 16)
            sp.dma_start(a_w2[TAIL:LASTK, c, :], c1_b2).then_inc(ld_l1, 16)
            sp.dma_start(a_b1[0:TAIL, c:c + 1], c1_b1[c * P:HID, :]).then_inc(ld_l1, 16)
            sp.dma_start(sw1[:, :], f1_sh_w1).then_inc(ld_l1, 16)
            sp.dma_start(sw2[:, :, :], f1_sh_w2.rearrange("(c p) h -> p c h", p=P)).then_inc(ld_l1, 16)
            sp.dma_start(sb1[:, :], f1_sh_b1).then_inc(ld_l1, 16)
            sp.dma_start(sb2[:, :], f1_sh_b2.partition_broadcast(P)).then_inc(ld_l1, 16)

            def load_block(j, s, first=False):
                if not first:
                    sp.wait_ge(e_xt, j - 3)
                    sp.wait_ge(e_ix, j - 3)
                sp.dma_start(blk_x[s][:, :], at(rows0_b, j)).then_inc(bx_ld[s], 16)

            sp.wait_ge(sc0, 16 * NT)
            for j in range(4):
                load_block(j, j, first=True)
            with sp.Fori(0, NBLKP // 4 - 1) as it:
                for s in range(4):
                    load_block(it * 4 + (4 + s), s)
            for s in range(4):
                sp.wait_ge(by_st[s], 16 * (NBLKP // 4))
            for g in range(NG):
                if g >= 2:
                    sp.wait_ge(x1_done, g - 1)
                sp.dma_start(y0g[g % 2][:, :, :], back0_g[g]).then_inc(y0_ld[g % 2], 16)

            def load_weights(e, k, free_at=None):
                if free_at is not None:
                    sp.wait_ge(q_oc, free_at)
                sp.dma_start(w1r[k], at(f1_w1, e)).then_inc(w_ld[k], 16)
                sp.dma_start(w2r[k], at(f1_w2, e).rearrange("(c p) h -> p c h", p=P)).then_inc(w_ld[k], 16)
                sp.dma_start(b1r[k][:, :], at(f1_b1, e)).then_inc(w_ld[k], 16)
                sp.dma_start(b2r[k][:, :], f1_b2[ds(e, 1), :].partition_broadcast(P)).then_inc(w_ld[k], 16)

            def load_group(m, k, first=False):
                if not first:
                    sp.wait_ge(q_xt, m - 1)
                    sp.wait_ge(q_ix, m - 1)
                sp.dma_start(grp_x[k][:, :, :], at(rows1_q, m)).then_inc(gx_ld[k], 16)

            load_weights(0, 0)
            load_weights(1, 1)
            sp.wait_ge(sc1, 16 * TOP_K * NT)
            load_group(0, 0, first=True)
            load_group(1, 1, first=True)
            load_group(2, 0)
            load_group(3, 1)
            with sp.Fori(0, E1 // 2 - 1) as it:
                for u in range(2 * GPE):
                    m = it * (2 * GPE) + (4 + u)
                    load_group(m, u % 2)
                    if u == GPE - 1:
                        load_weights(it * 2 + 2, 0, it * (2 * GPE) + GPE)
                    if u == 2 * GPE - 1:
                        load_weights(it * 2 + 3, 1, it * (2 * GPE) + 2 * GPE)
            for m in range(4 + (E1 // 2 - 1) * 2 * GPE, NQ):
                load_group(m, m % 2)

            for k in range(2):
                sp.wait_ge(gy_st[k], 16 * U * (NQ // 2))
            for g in range(NG + 2):
                if g < NG:
                    k = g % 2
                    if g >= 2:
                        sp.wait_ge(f_ac, g - 1)
                    sp.dma_start(x1g[k][:, :, :], back1_g[0, g]).then_inc(fy_ld[k], 16)
                    sp.dma_start(y0g[k][:, :, :], back1_g[1, g]).then_inc(fy_ld[k], 16)
                if g >= 2:
                    sp.wait_ge(f_ac, g - 1)
                    sp.dma_start(out_g[g - 2], acc[:, (g - 2) * G:(g - 1) * G, :]).then_inc(o_st, 16)
            sp.wait_ge(o_st, 16 * NG)

        @block.gpsimd
        def _(pool):
            gp = nc.gpsimd
            gp.memset(zrow[:, :], 0.0).then_inc(poolk, 1)
            gp.memset(ident[:, :], 0.0).then_inc(poolk, 1)
            gp.memset(tri[:, :], 1.0).then_inc(poolk, 1)
            gp.memset(ones_b[:, :], 1.0).then_inc(poolk, 1)
            gp.memset(rst[:, :], 1.0).then_inc(poolk, 1)
            pool.wait_ge(poolk, 5)
            gp.affine_select(out=ident[:, :], in_=ident[:, :], compare_op=ALU.not_equal, fill=1.0,
                             base=0, pattern=[[-1, P]], channel_multiplier=1).then_inc(poolk, 1)
            gp.affine_select(out=tri[:, :], in_=tri[:, :], compare_op=ALU.is_gt, fill=0.0,
                             base=0, pattern=[[1, P]], channel_multiplier=-1).then_inc(poolk, 1)
            gp.memset(rst[:, :].rearrange("p (e i) -> p e i", i=NT)[:, :, 0:1], 0.0).then_inc(poolk, 1)
            gp.iota(rowI[:, :], pattern=[[1, 1]], base=0, channel_multiplier=1).then_inc(poolk, 1)
            gp.iota(codes[:, :], pattern=[[-P, NT]], base=FAR, channel_multiplier=-1,
                    allow_small_or_imprecise_dtypes=True).then_inc(poolk, 1)
            gp.iota(revE[:, :], pattern=[[-1, E0]], base=E0, channel_multiplier=0,
                    allow_small_or_imprecise_dtypes=True).then_inc(poolk, 1)
            gp.iota(baseE[:, :], pattern=[[CAP, E1]], base=-DROP, channel_multiplier=0,
                    allow_small_or_imprecise_dtypes=True).then_inc(poolk, 1)
            gp.iota(jrow[:, :], pattern=[[P, NBLKP]], base=0, channel_multiplier=0,
                    allow_small_or_imprecise_dtypes=True).then_inc(poolk, 1)
            gp.memset(ones_f[:, :], 1.0).then_inc(poolk, 1)
            gp.memset(epsc[:, :], LN_EPS).then_inc(poolk, 1)
            pool.wait_ge(poolk, 15)
            gp.tensor_copy(disp[:, :, H:ROW], codes[:, :].unsqueeze(2)).then_inc(codes0, 1)

            pool.wait_ge(zero0, 16 * (NBLKP // 4))
            pool.wait_ge(slots0, 1)
            pool.wait_ge(codes0, 1)
            for t in range(NT):
                if t % G == 0:
                    pool.wait_ge(scaled, t + G)
                gp.indirect_dma_start(rows0, bass.IndirectOffsetOnAxis(ap=slot[:, 0, t:t + 1], axis=0),
                                      disp[:, t, :], None, bounds_check=NBLKP * P - 1,
                                      oob_is_err=False).then_inc(sc0, 16)

            last_token = pool.to_reg(T - 1)
            with pool.Fori(0, NBLKP // 4) as it:
                for s in range(4):
                    pool.wait_ge(e_oc, it * 4 + (s + 1))
                    pool.sem_inc(pool_turn)
                    gp.indirect_dma_start(back0, bass.IndirectOffsetOnAxis(ap=blk_i[s][:, 0:1], axis=0),
                                          blk_y[s][:, :], None, bounds_check=last_token,
                                          oob_is_err=False).then_inc(by_st[s], 16)

            for g in range(NG):
                pool.wait_ge(x1_done, g + 1)
                if g == 0:
                    pool.wait_ge(ld_l1, 16 * (2 * (NCH - 1) + 8))
                    pool.wait_ge(acc0, NG)
                gp.tensor_copy(acc[:, g * G:(g + 1) * G, :], x1g[g % 2][:, :, :]).then_inc(res_done, 1)

            pool.wait_ge(zero1, 16 * (E1 * CAP // (4 * P) + TOP_K * T // (8 * P)))
            pool.wait_ge(b_tk, NG)
            pool.wait_ge(slots1, 1)
            for k in range(TOP_K):
                if k:
                    pool.wait_ge(sc1, 16 * NT)
                    gp.tensor_scalar(disp[:, :, H:ROW], codes[:, :].unsqueeze(2), float(-T), None,
                                     ALU.add).then_inc(codes1, 1)
                    pool.wait_ge(codes1, 1)
                for t in range(NT):
                    gp.indirect_dma_start(rows1, bass.IndirectOffsetOnAxis(ap=slot[:, k, t:t + 1], axis=0),
                                          disp[:, t, :], None, bounds_check=E1 * CAP - 1,
                                          oob_is_err=False).then_inc(sc1, 16)
            last_row = pool.to_reg(TOP_K * T - 1)
            with pool.Fori(0, NQ // 2) as it:
                for k in range(2):
                    pool.wait_ge(q_oc, it * 2 + (k + 1))
                    pool.sem_inc(pool_turn)
                    for u in range(U):
                        gp.indirect_dma_start(back1, bass.IndirectOffsetOnAxis(ap=grp_i[k][:, u:u + 1], axis=0),
                                              grp_y[k][:, u, :], None, bounds_check=last_row,
                                              oob_is_err=False).then_inc(gy_st[k], 16)

        @block.scalar
        def _(eng):
            sc = nc.scalar

            def cp(dst, src):
                return sc.activation(dst, src, ACT.Copy)

            eng.dma_start(c0w[:, :].rearrange("p (s h) -> p s h", s=NSUB),
                          c0_w.rearrange("s p h -> p s h")).then_inc(ld_c0w, 16)
            eng.preload_act_table(ACT.Sigmoid)
            for n in range(NG + 1):
                if n < NG:
                    eng.wait_ge(pe_xt, n + 1)
                    cp(xT[n % 2][:, :], PS[0][:, :]).then_inc(xT_done, 1)
                    for b in range(2):
                        eng.wait_ge(pe_c, 4 * n + b + 1)
                        cp(condS[:, 4 * b:4 * b + 4, :], PS[1 + b][0:S, :].rearrange("p (b h) -> p b h", h=H)
                           ).then_inc(condA, 1)
                if n >= 1:
                    eng.wait_ge(pe_tok, n)
                    cp(disp[:, (n - 1) * G:n * G, 0:H],
                       PS[7][:, :].rearrange("p (i h) -> p i h", h=H)).then_inc(tok_done, 1)
            eng.wait_ge(mx0, 1)
            sc.activation(score[:, :], m1[:, :], ACT.Sigmoid).then_inc(sg0, 1)
            eng.preload_act_table(ACT.Silu)
            eng.wait_ge(sg0, 1)
            eng.wait_ge(tok_done, NG)
            for n in range(NG):
                for c in range(C0):
                    eng.wait_ge(pe_gu, 2 * C0 * n + 2 * c + 1)
                    if n >= 1:
                        eng.wait_ge(act_done, C0 * (n - 1) + c + 1)
                    sc.activation(sil[:, c, :], PS[2 * c][:, :], ACT.Silu).then_inc(sil_done, 1)
                for i in range(G):
                    t = n * G + i
                    sc.activation(disp[:, t, 0:H], disp[:, t, 0:H], ACT.Copy,
                                  scale=score[:, t:t + 1]).then_inc(scaled, 1)

            def copy_xT(j, k):
                eng.wait_ge(e_xt, j + 1)
                cp(blk_xT[k][:, :], PS[5 + k][:, 0:P]).then_inc(e_xc, 1)

            def silu(j, k):
                eng.wait_ge(e_gu, j + 1)
                sc.activation(blk_s[k][:, :], PS[k][:, 0:F0], ACT.Silu).then_inc(e_sl, 1)

            def copy_aT(j, k):
                eng.wait_ge(e_ta, j + 1)
                cp(blk_aT[k][:, :], PS[2 + k][:, 0:F0]).then_inc(e_at, 1)

            def act_stage(j, k, first=False, last=False):
                if not last:
                    copy_xT(j + 1, 1 - k)
                silu(j, k)
                if not first:
                    copy_aT(j - 1, 1 - k)

            copy_xT(0, 0)
            for j in range(4):
                act_stage(j, j % 2, first=j == 0)
            with eng.Fori(0, NBLKP // 4 - 2) as it:
                for s in range(4):
                    act_stage(it * 4 + (4 + s), s % 2)
            for j in range(NBLKP - 4, NBLKP):
                act_stage(j, j % 2, last=j == NBLKP - 1)
            copy_aT(NBLKP - 1, (NBLKP - 1) % 2)

            eng.wait_ge(ld_l1, 16 * (2 * (NCH - 1) + 8))
            for n in range(NG + 3):
                if 3 <= n:
                    m = n - 3
                    eng.wait_ge(b_bt, m + 1)
                    cp(disp[:, m * G:(m + 1) * G, 0:H],
                       PS[6][:, :].rearrange("p (i h) -> p i h", h=H)).then_inc(b_tk, 1)
                if n < NG:
                    eng.wait_ge(b_xt, n + 1)
                    cp(xT[n % 2][:, :], PS[0][:, :]).then_inc(b_xc, 1)
                    for c in range(NCH):
                        eng.wait_ge(b_w1, NCH * n + c + 1)
                        if n >= 2:
                            eng.wait_ge(b_w2, n - 1)
                        sc.activation(act[n % 2][0:KROWS[c], c, :], PS[1 + c][0:KROWS[c], :], ACT.Relu,
                                      bias=a_b1[0:KROWS[c], c:c + 1]).then_inc(b_rl, 1)
                if 1 <= n < NG + 1:
                    eng.wait_ge(b_var, n)
                    sc.activation(rstd[:, :], mv[:, :, 1], ACT.Sqrt, bias=epsc[:, :]).then_inc(b_std, 1)
            eng.wait_ge(ex_in, 1)
            sc.activation(t1[:, 0:NT * E1], t1[:, 0:NT * E1], ACT.Exp).then_inc(ex_out, 1)
            eng.preload_act_table(ACT.Silu)
            for n in range(NG):
                for c in range(C1):
                    eng.wait_ge(s_gu, C1 * n + c + 1)
                    if n >= 2:
                        eng.wait_ge(s_dn, n - 1)
                    sc.activation(act[n % 2][:, c, :], PS[c][:, :], ACT.Silu,
                                  bias=sb1[:, c:c + 1]).then_inc(s_sl, 1)

            def q_copy(q):
                eng.wait_ge(q_xt, q + 1)
                cp(xT[0][:, 0:UP], PS[0][:, 0:UP]).then_inc(q_xc, 1)

            def q_silu(q, k, e):
                for c in range(C1):
                    if c % 2 == 0:
                        eng.wait_ge(q_gu, q * (C1 // 2) + (c // 2 + 1))
                    sc.activation(act[k][:, c, 0:UP], PS[1 + k * (C1 // 2) + c // 2][:, (c % 2) * UP:(c % 2 + 1) * UP],
                                  ACT.Silu, bias=b1r[e][:, c:c + 1]).then_inc(q_sl, 1)

            def q_stage(q, k, e, last=False):
                q_silu(q, k, e)
                if not last:
                    q_copy(q + 1)

            q_copy(0)
            q_stage(0, 0, 0)
            with eng.Fori(0, E1 // 2 - 1) as it:
                for u in range(2 * GPE):
                    q_stage(it * (2 * GPE) + (1 + u), (1 + u) % 2, (1 + u) // GPE % 2)
            for q in range(1 + (E1 // 2 - 1) * 2 * GPE, NQ):
                q_stage(q, q % 2, q // GPE % 2, last=q == NQ - 1)

        @block.vector
        def _(dve):
            v = nc.vector
            chain = [0]

            def link(ins):
                chain[0] += 1
                ins.then_inc(dch, 1)
                dve.wait_ge(dch, chain[0])

            def bc(ap, shape):
                return ap.to_broadcast(shape)

            v.memset(a_w1[:, HID:(NCH - 1) * P + LASTK], 0.0)
            v.memset(a_b1[TAIL:LASTK, NCH - 1:NCH], 1.0).then_inc(dve_ready, 1)
            dve.wait_ge(ld_small, 16)
            link(v.tensor_scalar(w0off[:, :], w0off[:, :], float(H), None, ALU.mult))
            dve.wait_ge(poolk, 15)
            link(v.tensor_copy(rowLi[:, NCH:NCH + 1], rowI[:, :]))
            for c in range(NCH):
                link(v.tensor_scalar(rowLi[:, c:c + 1], rowI[:, :], A.bit_length() - 1, None,
                                     ALU.arith_shift_right))
            link(v.tensor_copy(rowL[:, :], rowLi[:, :]))
            for c in range(1, NCH):
                link(v.tensor_scalar(rowL[:, c:c + 1], rowL[:, c:c + 1], float(c * P // A), None, ALU.add))
            link(v.tensor_scalar(rowL[TAIL:P, NCH - 1:NCH], rowL[TAIL:P, NCH:NCH + 1], float(-TAIL), None,
                                 ALU.add))
            dve.wait_ge(ld_tab, 16 * 7)
            link(v.tensor_scalar(hot0[:, :], subjI[:, :], rowL[0:NSUB, NCH:NCH + 1], None, ALU.is_equal))
            link(v.tensor_scalar(hot1[:, :], langI[0:NLANG, :], rowL[0:NLANG, NCH:NCH + 1], None, ALU.is_equal))
            for c in range(NCH):
                link(v.tensor_scalar(lmask[:, c, :], langI[:, :], rowL[:, c:c + 1], None, ALU.is_equal))
            v.engine_nop().then_inc(dve_ready, 1)
            dve.wait_ge(pe_tab, 1)
            link(v.tensor_copy(c0bT[:, :], PS[6][:, 0:B]))
            link(v.tensor_copy(gamT[:, :], PS[6][:, B:2 * B]))
            link(v.tensor_copy(betT[:, :], PS[6][:, 2 * B:3 * B]))
            v.engine_nop().then_inc(tab_done, 1)

            for n in range(NG + 1):
                if n >= 1:
                    m = n - 1
                    dve.wait_ge(pe_ht, n)
                    v.tensor_tensor(featT[:, m * GP:n * GP].rearrange("p (b s) -> p b s", s=S),
                                    PS[5][:, :].rearrange("p (b s) -> p b s", s=S),
                                    bc(c0bT[:, m * GB:n * GB].unsqueeze(2), [P, GB, S]),
                                    ALU.add).then_inc(hT_done, 1)
                if n < NG:
                    for b in range(2, 4):
                        dve.wait_ge(pe_c, 4 * n + b + 1)
                        v.tensor_copy(condS[:, 4 * b:4 * b + 4, :],
                                      PS[1 + b][0:S, :].rearrange("p (b h) -> p b h", h=H)).then_inc(condD, 1)
                if n >= 1:
                    dve.wait_ge(pe_l, n)
                    v.tensor_copy(lg[:, m * G * E0:n * G * E0], PS[6][:, 0:G * E0]).then_inc(lg_done, 1)

            def first_max(vals, ne, keys, out_mask, top, top_sem=None):
                shape = [P, NT, ne]
                w3 = lambda a: a.rearrange("p (i e) -> p i e", e=ne)
                link(v.tensor_reduce(top[:, :], w3(vals), AX.X, ALU.max))
                if top_sem is not None:
                    v.engine_nop().then_inc(top_sem, 1)
                link(v.tensor_tensor(w3(keys), w3(vals), bc(top[:, :].unsqueeze(2), shape), ALU.is_equal))
                link(v.tensor_tensor(w3(keys), w3(keys), bc(revE[:, E0 - ne:E0].unsqueeze(1), shape), ALU.mult))
                link(v.tensor_reduce(m3[:, :], w3(keys), AX.X, ALU.max))
                link(v.tensor_tensor(w3(out_mask), w3(keys), bc(m3[:, :].unsqueeze(2), shape), ALU.is_equal))

            dve.wait_ge(lg_done, NG)
            first_max(lg[:, :], E0, t1[:, :], mask[:, :], m1, top_sem=mx0)
            v.engine_nop().then_inc(mk0, 1)
            te = lambda a, ne: a.rearrange("p (i e) -> p i e", e=ne)
            et = lambda a: a.rearrange("p (e i) -> p e i", i=NT)
            dve.wait_ge(pe_rank0, 1)
            link(v.tensor_copy(et(t1[:, :]), te(PS[6][:, :], E0).rearrange("p i e -> p e i")))
            link(v.tensor_tensor_scan(incl[:, :], rst[:, :], t1[:, :], 0.0, ALU.mult, ALU.add))
            link(v.tensor_scalar(padI[:, :], et(incl[:, :])[:, :, NT - 1], float(P - 1), None, ALU.add))
            link(v.tensor_scalar(padI[:, :], padI[:, :], P.bit_length() - 1, P.bit_length() - 1,
                                 ALU.arith_shift_right, ALU.arith_shift_left))
            link(v.tensor_copy(padF[:, :], padI[:, :]))
            link(v.tensor_tensor_scan(endE[:, :], ones_f[:, :], padF[:, :], 0.0, ALU.mult, ALU.add))
            link(v.tensor_tensor(padF[:, :], endE[:, :], padF[:, :], ALU.subtract))
            link(v.tensor_tensor(t2[:, :], incl[:, :], t1[:, :], ALU.subtract))
            link(v.tensor_tensor(te(t3[:, :], E0), et(t2[:, :]).rearrange("p e i -> p i e"),
                                 te(PS[5][:, :], E0), ALU.add))
            link(v.tensor_tensor(te(t3[:, :], E0), te(t3[:, :], E0),
                                 bc(padF[:, :].unsqueeze(1), [P, NT, E0]), ALU.add))
            link(v.tensor_tensor(t3[:, :], t3[:, :], mask[:, :], ALU.mult))
            link(v.tensor_reduce(slotF[:, 0, :], te(t3[:, :], E0), AX.X, ALU.add))
            v.tensor_copy(slot[:, 0, :], slotF[:, 0, :]).then_inc(slots0, 1)
            link(v.tensor_tensor(cmpj[:, :, :], bc(jrow[:, :].unsqueeze(2), [1, NBLKP, E0 - 1]),
                                 bc(endE[0:1, 0:E0 - 1].unsqueeze(1), [1, NBLKP, E0 - 1]), ALU.is_ge))
            link(v.tensor_reduce(bexp[:, :], cmpj[:, :, :], AX.X, ALU.add))
            v.tensor_scalar(guo[:, :], bexp[:, :], float(F0x2), None, ALU.mult)
            v.tensor_scalar(dno[:, :], bexp[:, :], float(C0 * H), None, ALU.mult).then_inc(blocks0, 1)

            for n in range(NG + 1):
                if n < NG:
                    for c in range(C0):
                        dve.wait_ge(sil_done, C0 * n + c + 1)
                        dve.wait_ge(pe_gu, 2 * C0 * n + 2 * c + 2)
                        if n >= 2:
                            dve.wait_ge(pe_dn, n - 1)
                        v.tensor_tensor(act[n % 2][:, c, :], PS[2 * c + 1][:, :], sil[:, c, :],
                                        ALU.mult).then_inc(act_done, 1)
                if n >= 1:
                    dve.wait_ge(pe_dn, n)
                    a = acc[:, (n - 1) * G:n * G, :]
                    v.tensor_tensor(a, a, PS[4][:, :].rearrange("p (i h) -> p i h", h=H),
                                    ALU.add).then_inc(acc0, 1)

            def index(j, s, turn, first=False):
                dve.wait_ge(bx_ld[s], turn * 16 + 16)
                if not first:
                    dve.wait_ge(by_st[s], turn * 16)
                v.tensor_scalar(blk_i[s][:, :], blk_x[s][:, H:ROW], -1.0, float(FAR), ALU.mult,
                                ALU.add).then_inc(e_ix, 1)

            def glu(j, k):
                dve.wait_ge(e_sl, j + 1)
                v.tensor_tensor(blk_a[k][:, :], PS[k][:, F0:F0x2], blk_s[k][:, :], ALU.mult).then_inc(e_ac, 1)

            def result(j, s):
                dve.wait_ge(e_dn, j + 1)
                v.tensor_copy(blk_y[s][:, :], PS[4 if s % 2 == 0 else 7][:, 0:H]).then_inc(e_oc, 1)

            def dve_stage(j, s, turn, first=False):
                index(j, s, turn, first)
                glu(j, s % 2)
                if not (isinstance(j, int) and j < 2):
                    result(j - 2, (s - 2) % 4)

            for j in range(4):
                dve_stage(j, j, 0, first=True)
            with dve.Fori(0, NBLKP // 4 - 1) as it:
                for s in range(4):
                    dve_stage(it * 4 + (4 + s), s, it + 1)
            for j in range(NBLKP - 2, NBLKP):
                result(j, j % 4)

            dve.wait_ge(acc0, NG)
            for n in range(NG + 2):
                if n < NG:
                    k = n % 2
                    dve.wait_ge(y0_ld[k], 16 * (n // 2 + 1))
                    if n >= 2:
                        dve.wait_ge(res_done, n - 1)
                    v.tensor_tensor(x1g[k][:, :, :], acc[:, n * G:(n + 1) * G, :], y0g[k][:, :, :],
                                    ALU.add).then_inc(x1_done, 1)
                if n >= 2:
                    m = n - 2
                    dve.wait_ge(b_nt, m + 1)
                    f3 = featT[:, m * GP:(m + 1) * GP].rearrange("p (b s) -> p b s", s=S)
                    link(v.tensor_tensor(f3, PS[5][:, :].rearrange("p (b s) -> p b s", s=S),
                                         bc(gamT[:, m * GB:(m + 1) * GB].unsqueeze(2), [P, GB, S]), ALU.mult))
                    v.tensor_tensor(f3, f3, bc(betT[:, m * GB:(m + 1) * GB].unsqueeze(2), [P, GB, S]),
                                    ALU.add).then_inc(b_xn, 1)
                if n < NG:
                    for c in range(NCH):
                        dve.wait_ge(b_rl, NCH * n + c + 1)
                        a3 = act[k][0:KROWS[c], c, :].rearrange("p (b s) -> p b s", s=S)
                        v.tensor_tensor(a3, a3, bc(lmask[0:KROWS[c], c, n * GB:(n + 1) * GB].unsqueeze(2),
                                                   [KROWS[c], GB, S]), ALU.mult).then_inc(b_mk, 1)
                if 1 <= n < NG + 1:
                    m = n - 1
                    k = m % 2
                    dve.wait_ge(b_w2, n)
                    dve.wait_ge(x1_done, n)
                    if m >= 2:
                        dve.wait_ge(b_nt, m - 1)
                    link(v.tensor_tensor(nrm[k][:, :, :], PS[4][:, :].rearrange("p (i h) -> p i h", h=H),
                                         x1g[k][:, :, :], ALU.add))
                    for i in range(G):
                        ins = v.bn_stats(bn6[:, i, :], nrm[k][:, i, :])
                    link(ins)
                    for i in range(G):
                        ins = v.bn_aggr(mv[:, i, :], bn6[:, i, :])
                    ins.then_inc(b_var, 1)
                    dve.wait_ge(b_std, n)
                    link(v.reciprocal(rstd[:, :], rstd[:, :]))
                    for i in range(G):
                        ins = v.tensor_scalar(nrm[k][:, i, :], nrm[k][:, i, :], mv[:, i, 0:1], rstd[:, i:i + 1],
                                              ALU.subtract, ALU.mult)
                    ins.then_inc(b_nm, 1)
                if n >= 2:
                    m = n - 2
                    dve.wait_ge(b_lg, m + 1)
                    v.tensor_copy(lg[:, m * G * E1:(m + 1) * G * E1], PS[7][:, 0:G * E1]).then_inc(b_lc, 1)

            WE = NT * E1
            L3 = [P, NT, E1]
            dve.wait_ge(b_lc, NG)
            link(v.tensor_reduce(m1[:, :], te(lg[:, 0:WE], E1), AX.X, ALU.max))
            v.tensor_tensor(te(t1[:, 0:WE], E1), te(lg[:, 0:WE], E1), bc(m1[:, :].unsqueeze(2), L3),
                            ALU.subtract).then_inc(ex_in, 1)
            dve.wait_ge(ex_out, 1)
            link(v.tensor_reduce(m1[:, :], te(t1[:, 0:WE], E1), AX.X, ALU.add))
            link(v.reciprocal(m1[:, :], m1[:, :]))
            link(v.tensor_tensor(te(lg[:, 0:WE], E1), te(t1[:, 0:WE], E1), bc(m1[:, :].unsqueeze(2), L3), ALU.mult))
            first_max(lg[:, 0:WE], E1, t1[:, 0:WE], mask[:, 0:WE], m1)
            link(v.tensor_scalar(t2[:, 0:WE], mask[:, 0:WE], -1.0, 1.0, ALU.mult, ALU.add))
            link(v.tensor_tensor(t2[:, 0:WE], lg[:, 0:WE], t2[:, 0:WE], ALU.mult))
            first_max(t2[:, 0:WE], E1, t1[:, 0:WE], mask[:, WE:2 * WE], m1)
            v.engine_nop().then_inc(mk1, 1)
            k4 = lambda a: a.rearrange("p (k i e) -> p k i e", k=TOP_K, e=E1)
            dve.wait_ge(pe_rank1, 1)
            for k in range(TOP_K):
                link(v.tensor_copy(et(t1[:, k * WE:(k + 1) * WE]),
                                   te(PS[6][:, k * WE:(k + 1) * WE], E1).rearrange("p i e -> p e i")))
            link(v.tensor_tensor_scan(incl[:, :], rst[:, :], t1[:, :], 0.0, ALU.mult, ALU.add))
            link(v.tensor_tensor(t2[:, :], incl[:, :], t1[:, :], ALU.subtract))
            link(v.tensor_scalar(cnt1[:, :], et(incl[:, 0:WE])[:, :, NT - 1], float(CAP), None, ALU.min))
            for k in range(TOP_K):
                r = slice(k * WE, (k + 1) * WE)
                link(v.tensor_tensor(te(t3[:, r], E1), et(t2[:, r]).rearrange("p e i -> p i e"),
                                     te(PS[5][:, r], E1), ALU.add))
            link(v.tensor_tensor(te(t3[:, WE:2 * WE], E1), te(t3[:, WE:2 * WE], E1),
                                 bc(cnt1[:, :].unsqueeze(1), L3), ALU.add))
            link(v.tensor_scalar(t1[:, :], t3[:, :], float(CAP), None, ALU.is_lt))
            link(v.tensor_tensor(t1[:, :], t1[:, :], mask[:, :], ALU.mult))
            for k in range(TOP_K):
                r = slice(k * WE, (k + 1) * WE)
                link(v.tensor_tensor(te(t3[:, r], E1), te(t3[:, r], E1), bc(baseE[:, :].unsqueeze(1), L3), ALU.add))
            link(v.tensor_tensor(t3[:, :], t3[:, :], t1[:, :], ALU.mult))
            link(v.tensor_reduce(slotF[:, :, :], k4(t3[:, :]), AX.X, ALU.add))
            v.tensor_scalar(slot[:, :, :], slotF[:, :, :], float(DROP), None, ALU.add).then_inc(slots1, 1)
            for k in range(TOP_K):
                r = slice(k * WE, (k + 1) * WE)
                link(v.tensor_tensor(t2[:, r], t1[:, r], lg[:, 0:WE], ALU.mult))
            link(v.tensor_reduce(wk[:, :, :], k4(t2[:, :]), AX.X, ALU.add))
            link(v.tensor_tensor(m1[:, :], wk[:, 0, :], wk[:, 1, :], ALU.add))
            link(v.tensor_scalar(m1[:, :], m1[:, :], TINY, None, ALU.max))
            link(v.reciprocal(m1[:, :], m1[:, :]))
            link(v.tensor_tensor(wk[:, :, :], wk[:, :, :], bc(m1[:, :].unsqueeze(1), [P, TOP_K, NT]), ALU.mult))
            link(v.tensor_scalar(sb2[:, :], sb2[:, :], SHARED_SCALE, None, ALU.mult))

            dve.wait_ge(res_done, NG)
            for n in range(NG):
                dve.wait_ge(s_dn, n + 1)
                a = acc[:, n * G:(n + 1) * G, :]
                link(v.scalar_tensor_tensor(out=a, in0=PS[4][:, :].rearrange("p (i h) -> p i h", h=H),
                                            scalar=SHARED_SCALE, in1=a, op0=ALU.mult, op1=ALU.add))
                v.tensor_tensor(a, a, bc(sb2[:, :].unsqueeze(1), [P, G, H]), ALU.add).then_inc(s_ac, 1)

            def q_index(q, k, turn, first=False):
                dve.wait_ge(gx_ld[k], turn * 16 + 16)
                if not first:
                    dve.wait_ge(gy_st[k], turn * (16 * U))
                v.tensor_scalar(grp_i[k][:, :], grp_x[k][:, :, H], -1.0, float(FAR), ALU.mult,
                                ALU.add).then_inc(q_ix, 1)

            def q_result(q, k, e):
                dve.wait_ge(q_dn, q + 1)
                v.tensor_tensor(grp_y[k][:, :, :], PS[5 + k][:, 0:UP].rearrange("p (u h) -> p u h", h=H),
                                bc(b2r[e][:, :].unsqueeze(1), [P, U, H]), ALU.add).then_inc(q_oc, 1)

            for q in range(2):
                q_index(q, q, 0, first=True)
                q_result(q, q, 0)
            with dve.Fori(0, E1 // 2 - 1) as it:
                for u in range(2 * GPE):
                    q = it * (2 * GPE) + (2 + u)
                    q_index(q, u % 2, it * GPE + (1 + u // 2))
                    q_result(q, u % 2, (2 + u) // GPE % 2)
            for q in range(2 + (E1 // 2 - 1) * 2 * GPE, NQ):
                q_index(q, q % 2, q // 2)
                q_result(q, q % 2, q // GPE % 2)

            for g in range(NG):
                dve.wait_ge(fy_ld[g % 2], 32 * (g // 2 + 1))
                for i in range(G):
                    t = g * G + i
                    link(v.scalar_tensor_tensor(out=acc[:, t, :], in0=x1g[g % 2][:, i, :], scalar=wk[:, 0, t:t + 1],
                                                in1=acc[:, t, :], op0=ALU.mult, op1=ALU.add))
                    ins = v.scalar_tensor_tensor(out=acc[:, t, :], in0=y0g[g % 2][:, i, :],
                                                 scalar=wk[:, 1, t:t + 1], in1=acc[:, t, :],
                                                 op0=ALU.mult, op1=ALU.add)
                ins.then_inc(f_ac, 1)

        @block.tensor
        def _(pe):
            idn = ident[:, :]

            def tr(dst, src, k=P):
                return nc.tensor.transpose(dst, src, ident[0:k, 0:k])

            pe.wait_ge(dve_ready, 2)
            pe.wait_ge(ld_tab, 16 * 7)
            pe.wait_ge(poolk, 15)
            mm(PS[6][:, 0:B], c0bs[:, :], hot0[:, :], start=True, stop=True)
            mm(PS[6][:, B:2 * B], gam[:, :], hot1[:, :], start=True, stop=True)
            mm(PS[6][:, 2 * B:3 * B], bet[:, :], hot1[:, :], start=True, stop=True).then_inc(pe_tab, 1)

            for n in range(NG + 1):
                if n < NG:
                    pe.wait_ge(x_ld[n], 16)
                    for i in range(G):
                        last = tr(tile(PS[0], i), acc[:, n * G + i, :])
                    last.then_inc(pe_xt, 1)
                if n >= 1:
                    pe.wait_ge(condA, 2 * n)
                    pe.wait_ge(condD, 2 * n)
                    if n == 1:
                        pe.wait_ge(tab_done, 1)
                    for b in range(GB):
                        last = tr(PS[5][:, b * S:(b + 1) * S], condS[:, b, :], S)
                    last.then_inc(pe_ht, 1)
                if n < NG:
                    pe.wait_ge(xT_done, n + 1)
                    if n == 0:
                        pe.wait_ge(ld_c0w, 16)
                    _, offs = nc.values_load_multi_w_load_instructions(
                        w0off[0:1, n * GB:(n + 1) * GB], engines=(mybir.EngineType.PE,), min_val=0,
                        max_val=(NSUB - 1) * H, skip_runtime_bounds_check_because="subjects are under NSUB")
                    for b in range(GB):
                        last = mm(PS[1 + b // 4][0:S, (b % 4) * H:(b % 4 + 1) * H],
                                  xT[n % 2][:, b * S:(b + 1) * S], c0w[:, ds(offs[b], H)],
                                  start=True, stop=True)
                        if b % 4 == 3:
                            last.then_inc(pe_c, 1)
                if n >= 1:
                    m = n - 1
                    pe.wait_ge(hT_done, n)
                    if m >= 1:
                        pe.wait_ge(lg_done, m)
                        pe.wait_ge(tok_done, m)
                    for i in range(G):
                        last = mm(PS[6][:, i * E0:(i + 1) * E0], tile(featT, m * G + i), rt0[:, :],
                                  start=True, stop=True)
                    last.then_inc(pe_l, 1)
                    for i in range(G):
                        last = tr(tile(PS[7], i), tile(featT, m * G + i))
                    last.then_inc(pe_tok, 1)

            def shared0_up(n):
                for c in range(C0):
                    for w, b in ((shg, 2 * c), (shu, 2 * c + 1)):
                        if n >= 1:
                            pe.wait_ge(act_done, C0 * (n - 1) + c + 1)
                        mm(PS[b][:, :], w[:, c * P:(c + 1) * P], featT[:, n * GP:(n + 1) * GP],
                           start=True, stop=True).then_inc(pe_gu, 1)

            def shared0_down(n):
                pe.wait_ge(act_done, C0 * (n + 1))
                if n >= 1:
                    pe.wait_ge(acc0, n)
                for i in range(G):
                    for c in range(C0):
                        last = mm(tile(PS[4], i), tile(act[n % 2][:, c, :], i), shd[:, c, :],
                                  start=c == 0, stop=c == C0 - 1)
                last.then_inc(pe_dn, 1)

            pe.wait_ge(ld_sh0, 48)
            shared0_up(0)
            pe.wait_ge(mk0, 1)
            mm(PS[5][:, :], tri[:, :], mask[:, :], start=True, stop=True)
            mm(PS[6][:, :], ones_b[:, :], mask[:, :], start=True, stop=True).then_inc(pe_rank0, 1)
            for n in range(1, NG):
                shared0_up(n)
                shared0_down(n - 1)
            shared0_down(NG - 1)

            def x_tr(j, s, turn, k):
                pe.wait_ge(bx_ld[s], turn * 16 + 16)
                tr(PS[5 + k][:, 0:P], blk_x[s][:, 0:H]).then_inc(e_xt, 1)

            def gate_up(j, k, off):
                pe.wait_ge(e_xc, j + 1)
                mm(PS[k][:, :], blk_xT[k][:, :], w_gu[:, ds(off, F0x2)], start=True, stop=True).then_inc(e_gu, 1)

            def a_tr(j, k):
                pe.wait_ge(e_ac, j + 1)
                for c in range(C0):
                    last = tr(tile(PS[2 + k], c), tile(blk_a[k], c))
                last.then_inc(e_ta, 1)

            def down(j, k, off, first=False):
                pe.wait_ge(e_at, j + 1)
                if not first:
                    pe.wait_ge(e_oc, j - 1)
                for c in range(C0):
                    last = mm(PS[4 if k == 0 else 7][:, 0:H], blk_aT[k][:, c * P:(c + 1) * P],
                              w_dn[:, ds(off + c * H, H)], start=c == 0, stop=c == C0 - 1)
                last.then_inc(e_dn, 1)

            def offsets(tab, at, n, most):
                _, vals = nc.values_load_multi_w_load_instructions(
                    tab[0:1, ds(at, n)], engines=(mybir.EngineType.PE,), min_val=0, max_val=most,
                    skip_runtime_bounds_check_because="a count of at most E0 - 1, times the stride")
                return vals

            GU_MAX = (E0 - 1) * F0x2
            DN_MAX = (E0 - 1) * C0 * H
            pe.wait_ge(acc0, NG)
            pe.wait_ge(blocks0, 1)
            pe.wait_ge(slots0, 1)
            pe.wait_ge(tok_done, NG)
            pe.wait_ge(ld_gu, 16)
            pe.wait_ge(ld_dn, 16)

            def pe_stages(j0, turn, s_off, stages, offs_g, offs_d, lo=None):
                for i in range(stages):
                    s = i % 4
                    j = j0 + i
                    static = isinstance(j, int)
                    if not (static and j == NBLKP - 1):
                        x_tr(j + 1, (s + 1) % 4, turn + (1 if s == 3 else 0), (s + 1) % 2)
                    gate_up(j, s % 2, offs_g[i])
                    if not (static and j < 2):
                        down(j - 2, s % 2, offs_d[i], first=static and j < 4)
                    if not (static and j < 1):
                        a_tr(j - 1, (s + 1) % 2)

            x_tr(0, 0, 0, 0)
            og = offsets(guo, 0, 4, GU_MAX)
            od = offsets(dno, 0, 2, DN_MAX)
            pe_stages(0, 0, 0, 4, og, [None, None] + list(od))
            with pe.Fori(0, NBLKP // 4 - 2) as it:
                og = offsets(guo, it * 4 + 4, 4, GU_MAX)
                od = offsets(dno, it * 4 + 2, 4, DN_MAX)
                pe_stages(it * 4 + 4, it + 1, 0, 4, og, od)
            og = offsets(guo, NBLKP - 4, 4, GU_MAX)
            od = offsets(dno, NBLKP - 6, 6, DN_MAX)
            pe_stages(NBLKP - 4, NBLKP // 4 - 1, 0, 4, og, od)
            down(NBLKP - 2, 0, od[4])
            a_tr(NBLKP - 1, 1)
            down(NBLKP - 1, 1, od[5])

            pe.wait_ge(e_oc, NBLKP)
            pe.wait_ge(ld_l1, 16 * (2 * (NCH - 1) + 8))
            for n in range(NG + 3):
                if n >= 3:
                    m = n - 3
                    pe.wait_ge(b_xn, m + 1)
                    if m >= 1:
                        pe.wait_ge(b_lc, m)
                        pe.wait_ge(b_tk, m)
                    for i in range(G):
                        last = mm(PS[7][:, i * E1:(i + 1) * E1], tile(featT, m * G + i), rt1[:, :],
                                  start=True, stop=True)
                    last.then_inc(b_lg, 1)
                    for i in range(G):
                        last = tr(tile(PS[6], i), tile(featT, m * G + i))
                    last.then_inc(b_bt, 1)
                if n < NG:
                    pe.wait_ge(x1_done, n + 1)
                    if n >= 1:
                        pe.wait_ge(b_xc, n)
                    for i in range(G):
                        last = tr(tile(PS[0], i), x1g[n % 2][:, i, :])
                    last.then_inc(b_xt, 1)
                    pe.wait_ge(b_xc, n + 1)
                    if n >= 1:
                        pe.wait_ge(b_rl, NCH * n)
                    for c in range(NCH):
                        mm(PS[1 + c][0:KROWS[c], :], a_w1[:, c * P:c * P + KROWS[c]], xT[n % 2][:, :],
                           start=True, stop=True).then_inc(b_w1, 1)
                if 1 <= n < NG + 1:
                    m = n - 1
                    pe.wait_ge(b_mk, NCH * n)
                    if m >= 1:
                        pe.wait_ge(b_var, m)
                    for i in range(G):
                        for c in range(NCH):
                            last = mm(tile(PS[4], i), tile(act[m % 2][0:KROWS[c], c, :], i),
                                      a_w2[0:KROWS[c], c, :], start=c == 0, stop=c == NCH - 1)
                    last.then_inc(b_w2, 1)
                if 2 <= n < NG + 2:
                    m = n - 2
                    pe.wait_ge(b_nm, m + 1)
                    if m >= 1:
                        pe.wait_ge(b_xn, m)
                    for i in range(G):
                        last = tr(tile(PS[5], i), nrm[m % 2][:, i, :])
                    last.then_inc(b_nt, 1)

            def shared1_up(n):
                for c in range(C1):
                    if n >= 1:
                        pe.wait_ge(s_sl, C1 * (n - 1) + c + 1)
                    mm(PS[c][:, :], sw1[:, c * P:(c + 1) * P], featT[:, n * GP:(n + 1) * GP],
                       start=True, stop=True).then_inc(s_gu, 1)

            def shared1_down(n):
                pe.wait_ge(s_sl, C1 * (n + 1))
                if n >= 1:
                    pe.wait_ge(s_ac, n)
                for i in range(G):
                    for c in range(C1):
                        last = mm(tile(PS[4], i), tile(act[n % 2][:, c, :], i), sw2[:, c, :],
                                  start=c == 0, stop=c == C1 - 1)
                last.then_inc(s_dn, 1)

            shared1_up(0)
            pe.wait_ge(b_tk, NG)
            pe.wait_ge(mk1, 1)
            mm(PS[5][:, :], tri[:, :], mask[:, :], start=True, stop=True)
            mm(PS[6][:, :], ones_b[:, :], mask[:, :], start=True, stop=True).then_inc(pe_rank1, 1)
            for n in range(1, NG):
                shared1_up(n)
                shared1_down(n - 1)
            shared1_down(NG - 1)

            def q_tr(q, k, turn):
                pe.wait_ge(gx_ld[k], turn * 16 + 16)
                for u in range(U):
                    last = tr(tile(PS[0], u), grp_x[k][:, u, 0:H])
                last.then_inc(q_xt, 1)

            def q_up(q, k, e):
                for c in range(C1):
                    last = mm(PS[1 + k * (C1 // 2) + c // 2][:, (c % 2) * UP:(c % 2 + 1) * UP],
                              w1r[e][:, c * P:(c + 1) * P], xT[0][:, 0:UP], start=True, stop=True)
                    if c % 2 == 1:
                        last.then_inc(q_gu, 1)

            def q_down(q, k, e, first=False):
                pe.wait_ge(q_sl, q * C1 + C1)
                if not first:
                    pe.wait_ge(q_oc, q - 1)
                for u in range(U):
                    for c in range(C1):
                        last = mm(PS[5 + k][:, u * P:(u + 1) * P], act[k][:, c, u * P:(u + 1) * P],
                                  w2r[e][:, c, :], start=c == 0, stop=c == C1 - 1)
                last.then_inc(q_dn, 1)

            def q_stage(q, w, e, we, turn, weights=None, first=False, last=False):
                pe.wait_ge(q_xc, q + 1)
                if not last:
                    q_tr(q + 1, 1 - w, turn)
                if weights is not None:
                    pe.wait_ge(w_ld[e], weights)
                q_up(q, w, e)
                if not (isinstance(q, int) and q == 0):
                    q_down(q - 1, 1 - w, we, first=first)

            pe.wait_ge(s_ac, NG)
            q_tr(0, 0, 0)
            q_stage(0, 0, 0, 0, 0, weights=64)
            q_stage(1, 1, 0, 0, 1, first=True)
            q_stage(2, 0, 0, 0, 1, first=True)
            with pe.Fori(0, E1 // 2 - 1) as it:
                for u in range(2 * GPE):
                    b = 3 + u
                    q_stage(it * (2 * GPE) + b, b % 2, b // GPE % 2, (b - 1) // GPE % 2, it * GPE + (b + 1) // 2,
                            weights=(it * 64 + (b // (2 * GPE) + 1) * 64) if b % GPE == 0 else None)
            for q in range(3 + (E1 // 2 - 1) * 2 * GPE, NQ):
                q_stage(q, q % 2, q // GPE % 2, (q - 1) // GPE % 2, (q + 1) // 2,
                        weights=64 * (q // (2 * GPE) + 1) if q % GPE == 0 else None, last=q == NQ - 1)
            q_down(NQ - 1, (NQ - 1) % 2, (E1 - 1) % 2)


def kernel(**inputs):
    import numpy as np
    import concourse.bacc as bacc
    from concourse import mybir
    from concourse.bass_utils import run_bass_kernel_spmd

    i = {k: np.asarray(a) for k, a in inputs.items()}
    x = i["x"]
    nb, ns, h = x.shape
    lw1 = i["L1_cond_W1"]
    nl, _, na = lw1.shape
    e1, f1 = i["L1_ffn_b1"].shape
    arrays = {
        "x": x.reshape(nb * ns, h),
        "subj": i["itok_B_0_15"].reshape(1, nb),
        "lang": i["itok_B_0_8"].reshape(1, nb),
        "c0_w": i["L0_cond_weights"],
        "c0_b": i["L0_cond_b"],
        "f0_router": i["L0_ffn_w_router"].T,
        "f0_gate_up": i["L0_ffn_gate_up_proj"],
        "f0_down": i["L0_ffn_down_proj"],
        "f0_sh_gate": i["L0_ffn_w_gate"].T,
        "f0_sh_up": i["L0_ffn_w_up"].T,
        "f0_sh_down": i["L0_ffn_w_down"].T,
        "c1_w1": lw1.transpose(1, 0, 2).reshape(h, nl * na),
        "c1_b1": i["L1_cond_b1"].reshape(nl * na, 1),
        "c1_w2": i["L1_cond_W2"].reshape(nl * na, h),
        "c1_b2": i["L1_cond_b2"],
        "c1_gamma": i["L1_cond_gamma"],
        "c1_beta": i["L1_cond_beta"],
        "f1_router": i["L1_ffn_router_w"],
        "f1_w1": i["L1_ffn_w1"],
        "f1_b1": i["L1_ffn_b1"].reshape(e1, f1 // 128, 128).transpose(0, 2, 1),
        "f1_w2": i["L1_ffn_w2"],
        "f1_b2": i["L1_ffn_b2"],
        "f1_sh_w1": i["L1_ffn_sw1"],
        "f1_sh_b1": i["L1_ffn_sb1"].reshape(f1 // 128, 128).T,
        "f1_sh_w2": i["L1_ffn_sw2"],
        "f1_sh_b2": i["L1_ffn_sb2"].reshape(1, h),
    }
    arrays = {k: np.ascontiguousarray(a) for k, a in arrays.items()}
    nc = bacc.Bacc("TRN2", target_bir_lowering=False, num_devices=1)
    args = [nc.dram_tensor(f"in_{k}", a.shape, mybir.dt.from_np(a.dtype), kind="ExternalInput").ap()
            for k, a in arrays.items()]
    res = nc.dram_tensor("out_x", (nb * ns, h), mybir.dt.float32, kind="ExternalOutput").ap()
    adaln_moe_two_layers(nc, *args, res)
    r = run_bass_kernel_spmd(nc, [{f"in_{k}": a for k, a in arrays.items()}], core_ids=[0])
    return r.results[0]["out_x"].reshape(nb, ns, h)
```

```python
import concourse.bass as bass
from concourse import mybir
from contextlib import ExitStack


def adaln_moe_two_layers(
    nc: bass.Bass,
    x: bass.AP,
    subj: bass.AP,
    lang: bass.AP,
    c0_w: bass.AP,
    c0_b: bass.AP,
    f0_router: bass.AP,
    f0_gate_up: bass.AP,
    f0_down: bass.AP,
    f0_sh_gate: bass.AP,
    f0_sh_up: bass.AP,
    f0_sh_down: bass.AP,
    c1_w1: bass.AP,
    c1_b1: bass.AP,
    c1_w2: bass.AP,
    c1_b2: bass.AP,
    c1_gamma: bass.AP,
    c1_beta: bass.AP,
    f1_router: bass.AP,
    f1_w1: bass.AP,
    f1_b1: bass.AP,
    f1_w2: bass.AP,
    f1_b2: bass.AP,
    f1_sh_w1: bass.AP,
    f1_sh_b1: bass.AP,
    f1_sh_w2: bass.AP,
    f1_sh_b2: bass.AP,
    out: bass.AP,
):
    fp32 = mybir.dt.float32
    bf16 = mybir.dt.bfloat16
    i32 = mybir.dt.int32
    ALU = mybir.AluOpType
    ACT = mybir.ActivationFunctionType
    AX = mybir.AxisListType
    ds = bass.ds

    P = 128
    T, H = x.shape
    B = subj.shape[1]
    S = T // B
    NSUB = c0_w.shape[0]
    E0, _, F0x2 = f0_gate_up.shape
    F0 = F0x2 // 2
    C0 = F0 // P
    NLANG = c1_b2.shape[0]
    A = c1_w1.shape[1] // NLANG
    E1, _, F1 = f1_w1.shape
    C1 = F1 // P
    TOP_K = 2
    CAP = min(max(4, -(-TOP_K * 5 * T // (4 * E1))), T)
    SHARED_SCALE = 0.1
    LN_EPS = 1e-5
    BIG = 2.0 ** 120
    TINY = 1.1920929e-07

    NT = T // P
    G = 4
    NG = NT // G
    GB = G * P // S
    GP = G * P
    QB = P // S
    NBLK = NT + E0 - 1
    NBLKP = -(-NBLK // 4) * 4
    U = 2
    UP = U * P
    GPE = CAP // UP
    NQ = E1 * GPE
    ROW = H + 1
    FAR = 65536
    DROP = 16384
    HID = NLANG * A
    NCH = -(-HID // P)
    TAIL = HID - (NCH - 1) * P
    LASTK = TAIL + NLANG
    KROWS = [P] * (NCH - 1) + [LASTK]
    assert CAP % UP == 0 and TAIL % 32 == 0 and NG % 2 == 0 and E1 % 2 == 0 and GPE % 2 == 1

    rows0 = nc.dram_tensor("rows0", (NBLKP * P, ROW), fp32).ap()
    back0 = nc.dram_tensor("back0", (T, H), fp32).ap()
    rows1 = nc.dram_tensor("rows1", (E1 * CAP, ROW), fp32).ap()
    back1 = nc.dram_tensor("back1", (TOP_K * T, H), fp32).ap()

    x_g = x.rearrange("(g i p) h -> g p i h", p=P, i=G)
    out_g = out.rearrange("(g i p) h -> g p i h", p=P, i=G)
    back0_g = back0.rearrange("(g i p) h -> g p i h", p=P, i=G)
    back1_g = back1.rearrange("(k g i p) h -> k g p i h", p=P, i=G, k=TOP_K)
    rows0_b = rows0.rearrange("(j p) r -> j p r", p=P)
    rows1_q = rows1.rearrange("(q u p) r -> q p u r", p=P, u=U)

    ctx = ExitStack()
    with ctx:
        def sb(name, shape, dt=fp32):
            return ctx.enter_context(nc.sbuf_tensor(name, shape, dt))

        def sem(name):
            return ctx.enter_context(nc.semaphore(name))

        acc = sb("acc", [P, NT, H])
        featT = sb("featT", [P, T])
        disp = sb("disp", [P, NT, ROW])
        c0w = sb("c0w", [P, NSUB * H])
        w_gu = sb("w_gu", [P, E0 * F0x2])
        w_dn = sb("w_dn", [P, E0 * C0 * H])
        shg = sb("shg", [P, F0])
        shu = sb("shu", [P, F0])
        shd = sb("shd", [P, C0, H])
        rt0 = sb("rt0", [P, E0])
        rt1 = sb("rt1", [P, E1])
        c0bs = sb("c0bs", [NSUB, H])
        gam = sb("gam", [NLANG, H])
        bet = sb("bet", [NLANG, H])
        a_w1 = sb("a_w1", [P, (NCH - 1) * P + LASTK])
        a_w2 = sb("a_w2", [P, NCH, H])
        a_b1 = sb("a_b1", [P, NCH])
        sw1 = sb("sw1", [P, F1])
        sw2 = sb("sw2", [P, C1, H])
        sb1 = sb("sb1", [P, C1])
        sb2 = sb("sb2", [P, H])
        xT = [sb(f"xT{k}", [P, GP]) for k in range(2)]
        condS = sb("condS", [P, G, H])
        act = [sb(f"act{k}", [P, C1, GP]) for k in range(2)]
        sil = sb("sil", [P, C0, GP])
        y0g = [sb(f"y0g{k}", [P, G, H]) for k in range(4)]
        nrm = [sb(f"nrm{k}", [P, G, H]) for k in range(2)]
        w1r = [w_gu[:, k * F1:(k + 1) * F1] for k in range(2)]
        w2r = [w_gu[:, (2 + k) * F1:(3 + k) * F1].rearrange("p (c h) -> p c h", c=C1) for k in range(2)]
        NX = GPE
        GX = 4 * F1
        grp_x = [w_gu[:, GX + k * U * ROW:GX + (k + 1) * U * ROW].rearrange("p (u r) -> p u r", r=ROW)
                 for k in range(NX)]
        FX = GX + NX * U * ROW
        back = [[a[:, o + g * GP:o + (g + 1) * GP].rearrange("p (i h) -> p i h", h=H) for g in range(NG)]
                for a, o in ((w_dn, 0), (w_gu, FX))]
        b1r = [sb(f"b1r{k}", [P, C1]) for k in range(2)]
        b2r = [sb(f"b2r{k}", [P, H]) for k in range(2)]
        blk_x = [sb(f"blk_x{s}", [P, ROW]) for s in range(4)]
        blk_y = [sb(f"blk_y{s}", [P, H]) for s in range(4)]
        blk_i = [sb(f"blk_i{s}", [P, 1], i32) for s in range(4)]
        blk_xT = [sb(f"blk_xT{k}", [P, P]) for k in range(2)]
        blk_s = [sb(f"blk_s{k}", [P, F0]) for k in range(2)]
        blk_a = [sb(f"blk_a{k}", [P, F0]) for k in range(2)]
        blk_aT = [sb(f"blk_aT{k}", [P, F0]) for k in range(2)]
        grp_y = [sb(f"grp_y{k}", [P, U, H]) for k in range(2)]
        grp_i = [sb(f"grp_i{k}", [P, U], i32) for k in range(NX)]
        zrow = sb("zrow", [P, 1032])
        ident = sb("ident", [P, P])
        tri = sb("tri", [P, P], bf16)
        ones_b = sb("ones_b", [P, P], bf16)
        codes = sb("codes", [P, NT])
        subjI = sb("subjI", [NSUB, B], i32)
        langI = sb("langI", [NLANG, B], i32)
        w0off = sb("w0off", [1, B], i32)
        rowI = sb("rowI", [P, 1], i32)
        rowF = sb("rowF", [P, 1])
        colL = sb("colL", [NLANG, HID + NLANG])
        other = sb("other", [NLANG, HID + NLANG], bf16)
        hot0 = sb("hot0", [NSUB, B])
        hot1 = sb("hot1", [NLANG, B])
        hot1b = sb("hot1b", [NLANG, B], bf16)
        c0bT = sb("c0bT", [P, B])
        gamT = sb("gamT", [P, B])
        betT = sb("betT", [P, B])
        RT = NT // 4
        assert RT % G == 0
        W = NT * E0
        assert W == NT * TOP_K * E1 and W == 512
        lg = sb("lg", [P, W])
        t1 = sb("t1", [P, W])
        t2 = sb("t2", [P, W])
        t3 = sb("t3", [P, W])
        mask = sb("mask", [P, W], bf16)
        seen = sb("seen", [P, W], bf16)
        before = sb("before", [P, E1], bf16)
        keep = sb("keep", [P, W])
        rst = sb("rst", [P, W])
        rst1 = sb("rst1", [P, E1 * RT])
        revE = sb("revE", [P, E0])
        baseE = sb("baseE", [P, E1])
        m1 = sb("m1", [P, NT])
        m2 = sb("m2", [P, NT])
        m3 = sb("m3", [P, NT])
        wk = sb("wk", [P, TOP_K, NT])
        score = sb("score", [P, NT])
        slotF = sb("slotF", [P, TOP_K, NT])
        slot = sb("slot", [P, TOP_K, NT], i32)
        padI = sb("padI", [P, E0], i32)
        padF = sb("padF", [P, E0])
        endE = sb("endE", [P, E0])
        ones_f = sb("ones_f", [P, E0])
        jrow = sb("jrow", [1, NBLKP])
        cmpj = sb("cmpj", [1, NBLKP, E0 - 1])
        bexp = sb("bexp", [1, NBLKP])
        guo = sb("guo", [1, NBLKP], i32)
        dno = sb("dno", [1, NBLKP], i32)
        cnt1 = sb("cnt1", [P, E1])
        bn6 = sb("bn6", [P, G, 6])
        mv = sb("mv", [P, G, 2])
        rstd = [sb(f"rstd{k}", [P, G]) for k in range(2)]
        nmr = [sb(f"nmr{k}", [P, G]) for k in range(2)]
        epsc = sb("epsc", [P, 1])

        PS = [ctx.enter_context(nc.psum_tensor(f"PS{i}", [P, 512], fp32)) for i in range(8)]

        x_ld = [sem(f"x_ld{g}") for g in range(NG)]
        ld_small = sem("ld_small")
        ld_c0w = sem("ld_c0w")
        ld_tab = sem("ld_tab")
        ld_sh0 = sem("ld_sh0")
        ld_gu = sem("ld_gu")
        ld_dn = sem("ld_dn")
        ld_l1 = sem("ld_l1")
        zero0 = sem("zero0")
        zero1 = sem("zero1")
        poolk = sem("poolk")
        dch = sem("dch")
        dve_ready = sem("dve_ready")
        pe_tab = sem("pe_tab")
        tab_done = sem("tab_done")
        pe_xt = sem("pe_xt")
        xT_done = sem("xT_done")
        pe_c = sem("pe_c")
        condA = sem("condA")
        condD = sem("condD")
        pe_ht = sem("pe_ht")
        hT_done = sem("hT_done")
        pe_l = sem("pe_l")
        lg_done = sem("lg_done")
        pe_tok = sem("pe_tok")
        tok_done = sem("tok_done")
        mx0 = sem("mx0")
        sg0 = sem("sg0")
        mk0 = sem("mk0")
        pe_rank0 = sem("pe_rank0")
        slots0 = sem("slots0")
        blocks0 = sem("blocks0")
        scaled = sem("scaled")
        sc0 = sem("sc0")
        pe_gu = sem("pe_gu")
        sil_done = sem("sil_done")
        act_done = sem("act_done")
        pe_dn = sem("pe_dn")
        acc0 = sem("acc0")
        bx_ld = [sem(f"bx_ld{s}") for s in range(4)]
        by_st = [sem(f"by_st{s}") for s in range(4)]
        e_xt = sem("e_xt")
        e_xc = sem("e_xc")
        e_gu = sem("e_gu")
        e_sl = sem("e_sl")
        e_ac = sem("e_ac")
        e_ta = sem("e_ta")
        e_at = sem("e_at")
        e_dn = sem("e_dn")
        e_oc = sem("e_oc")
        e_ix = sem("e_ix")
        y0_ld = [sem(f"y0_ld{k}") for k in range(4)]
        x1_done = sem("x1_done")
        b_xt = sem("b_xt")
        b_xc = sem("b_xc")
        b_w1 = sem("b_w1")
        b_rl = sem("b_rl")
        b_w2 = sem("b_w2")
        b_var = sem("b_var")
        b_std = sem("b_std")
        b_nb = sem("b_nb")
        b_nm = sem("b_nm")
        b_nt = sem("b_nt")
        b_xn = sem("b_xn")
        b_lg = sem("b_lg")
        b_lc = sem("b_lc")
        b_rk = sem("b_rk")
        b_bt = sem("b_bt")
        b_tk = sem("b_tk")
        ex_in = sem("ex_in")
        ex_out = sem("ex_out")
        mk1 = sem("mk1")
        pe_rank1 = sem("pe_rank1")
        slots1 = sem("slots1")
        codes0 = sem("codes0")
        codes1 = sem("codes1")
        sc1 = [[sem(f"sc1_{k}{h}") for h in range(2)] for k in range(2)]
        s_gu = sem("s_gu")
        s_sl = sem("s_sl")
        s_dn = sem("s_dn")
        s_ac = sem("s_ac")
        gx_ld = [sem(f"gx_ld{k}") for k in range(NX)]
        gy_st = [sem(f"gy_st{k}") for k in range(2)]
        w_ld = [sem(f"w_ld{k}") for k in range(2)]
        q_xt = sem("q_xt")
        q_xc = sem("q_xc")
        q_gu = sem("q_gu")
        q_sl = sem("q_sl")
        q_dn = sem("q_dn")
        q_oc = sem("q_oc")
        q_ix = sem("q_ix")
        fy_ld = [sem(f"fy_ld{g}") for g in range(NG)]
        f_sc = sem("f_sc")
        f_ac = sem("f_ac")
        o_st = sem("o_st")
        pool_turn = sem("pool_turn")

        block = ctx.enter_context(nc.Block())
        mm = nc.tensor.matmul

        def at(ap, i):
            return ap[i] if isinstance(i, int) else ap[ds(i, 1)].squeeze(0)

        def tile(buf, i):
            return buf[:, i * P:(i + 1) * P]

        @block.sync
        def _(sp):
            sp.dma_start(w0off[:, :], subj).then_inc(ld_small, 16)
            sp.dma_start(subjI[:, :], subj.partition_broadcast(NSUB)).then_inc(ld_tab, 16)
            sp.dma_start(langI[:, :], lang.partition_broadcast(NLANG)).then_inc(ld_tab, 16)
            sp.dma_start(acc[:, 0:G, :], x_g[0]).then_inc(x_ld[0], 16)
            for dst, src in ((c0bs[:, :], c0_b), (gam[:, :], c1_gamma), (bet[:, :], c1_beta),
                             (rt0[:, :], f0_router), (rt1[:, :], f1_router)):
                sp.dma_start(dst, src).then_inc(ld_tab, 16)
            for g in range(1, NG):
                sp.dma_start(acc[:, g * G:(g + 1) * G, :], x_g[g]).then_inc(x_ld[g], 16)
            sp.dma_start(shg[:, :], f0_sh_gate).then_inc(ld_sh0, 16)
            sp.dma_start(shu[:, :], f0_sh_up).then_inc(ld_sh0, 16)
            sp.dma_start(shd[:, :, :], f0_sh_down.rearrange("(c p) h -> p c h", p=P)).then_inc(ld_sh0, 16)
            sp.wait_ge(poolk, 1)
            zw = ROW * 4
            for r in range(0, NBLKP * P, P * 4):
                sp.dma_start(rows0[r:r + P * 4, :].rearrange("(p a) r -> p (a r)", p=P),
                             zrow[:, 0:zw]).then_inc(zero0, 16)
            sp.dma_start(w_gu[:, :].rearrange("p (e f) -> p e f", e=E0),
                         f0_gate_up.rearrange("e p f -> p e f")).then_inc(ld_gu, 16)
            sp.dma_start(w_dn[:, :].rearrange("p (e c h) -> p e c h", e=E0, c=C0),
                         f0_down.rearrange("e (c p) h -> p e c h", p=P)).then_inc(ld_dn, 16)
            for r in range(0, E1 * CAP, P * 4):
                sp.dma_start(rows1[r:r + P * 4, :].rearrange("(p a) r -> p (a r)", p=P),
                             zrow[:, 0:zw]).then_inc(zero1, 16)
            for r in range(0, TOP_K * T, P * 8):
                sp.dma_start(back1[r:r + P * 8, :].rearrange("(p a) h -> p (a h)", p=P),
                             zrow[:, 0:8 * H]).then_inc(zero1, 16)
            sp.wait_ge(dve_ready, 1)
            sp.dma_start(a_w1[:, 0:HID], c1_w1).then_inc(ld_l1, 16)
            for c in range(NCH - 1):
                sp.dma_start(a_w2[:, c, :], c1_w2[c * P:(c + 1) * P, :]).then_inc(ld_l1, 16)
                sp.dma_start(a_b1[:, c:c + 1], c1_b1[c * P:(c + 1) * P, :]).then_inc(ld_l1, 16)
            c = NCH - 1
            sp.dma_start(a_w2[0:TAIL, c, :], c1_w2[c * P:HID, :]).then_inc(ld_l1, 16)
            sp.dma_start(a_w2[TAIL:LASTK, c, :], c1_b2).then_inc(ld_l1, 16)
            sp.dma_start(a_b1[0:TAIL, c:c + 1], c1_b1[c * P:HID, :]).then_inc(ld_l1, 16)
            sp.dma_start(sw1[:, :], f1_sh_w1).then_inc(ld_l1, 16)
            sp.dma_start(sw2[:, :, :], f1_sh_w2.rearrange("(c p) h -> p c h", p=P)).then_inc(ld_l1, 16)
            sp.dma_start(sb1[:, :], f1_sh_b1).then_inc(ld_l1, 16)
            sp.dma_start(sb2[:, :], f1_sh_b2.partition_broadcast(P)).then_inc(ld_l1, 16)

            def load_block(j, s, first=False):
                if not first:
                    sp.wait_ge(e_xt, j - 3)
                    sp.wait_ge(e_ix, j - 3)
                sp.dma_start(blk_x[s][:, :], at(rows0_b, j)).then_inc(bx_ld[s], 16)

            sp.wait_ge(sc0, 16 * NT)
            for j in range(4):
                load_block(j, j, first=True)
            with sp.Fori(0, NBLKP // 4 - 1) as it:
                for s in range(4):
                    load_block(it * 4 + (4 + s), s)
            for s in range(4):
                sp.wait_ge(by_st[s], 16 * (NBLKP // 4))
            for g in range(NG):
                if g >= 4:
                    sp.wait_ge(x1_done, g - 3)
                sp.dma_start(y0g[g % 4][:, :, :], back0_g[g]).then_inc(y0_ld[g % 4], 16)

            def load_weights(e, k, free_at=None):
                if free_at is not None:
                    sp.wait_ge(q_oc, free_at)
                sp.dma_start(w1r[k], at(f1_w1, e)).then_inc(w_ld[k], 16)
                sp.dma_start(w2r[k], at(f1_w2, e).rearrange("(c p) h -> p c h", p=P)).then_inc(w_ld[k], 16)
                sp.dma_start(b1r[k][:, :], at(f1_b1, e)).then_inc(w_ld[k], 16)
                sp.dma_start(b2r[k][:, :], f1_b2[ds(e, 1), :].partition_broadcast(P)).then_inc(w_ld[k], 16)

            def load_group(m, k, first=False):
                if not first:
                    sp.wait_ge(q_xt, m - (NX - 1))
                    sp.wait_ge(q_ix, m - (NX - 1))
                sp.dma_start(grp_x[k], at(rows1_q, m)).then_inc(gx_ld[k], 16)

            load_weights(0, 0)
            load_weights(1, 1)
            for k in range(TOP_K):
                for h in range(2):
                    sp.wait_ge(sc1[k][h], 16 * (NT // 2))
            for m in range(NX):
                load_group(m, m, first=True)
            with sp.Fori(0, E1 // 2 - 1) as it:
                for u in range(2 * GPE):
                    load_group(it * (2 * GPE) + (NX + u), u % NX)
                    if u == GPE:
                        load_weights(it * 2 + 2, 0, it * (2 * GPE) + GPE)
                    if u == 2 * GPE - 1:
                        load_weights(it * 2 + 3, 1, it * (2 * GPE) + 2 * GPE)
            for m in range(NX + (E1 // 2 - 1) * 2 * GPE, NQ):
                load_group(m, m % NX)

            for k in range(2):
                sp.wait_ge(gy_st[k], 16 * U * (NQ // 2))
            for g in range(NG):
                for k in range(TOP_K):
                    sp.dma_start(back[k][g], back1_g[k, g]).then_inc(fy_ld[g], 16)
            for g in range(NG):
                sp.wait_ge(f_ac, g + 1)
                sp.dma_start(out_g[g], acc[:, g * G:(g + 1) * G, :]).then_inc(o_st, 16)
            sp.wait_ge(o_st, 16 * NG)

        @block.gpsimd
        def _(pool):
            gp = nc.gpsimd
            gp.memset(zrow[:, :], 0.0).then_inc(poolk, 1)
            gp.memset(ident[:, :], 0.0).then_inc(poolk, 1)
            gp.memset(tri[:, :], -1.0).then_inc(poolk, 1)
            gp.memset(ones_b[:, :], 1.0).then_inc(poolk, 1)
            gp.memset(rst[:, :], 1.0).then_inc(poolk, 1)
            gp.memset(rst1[:, :], 1.0).then_inc(poolk, 1)
            pool.wait_ge(poolk, 6)
            gp.affine_select(out=ident[:, :], in_=ident[:, :], compare_op=ALU.not_equal, fill=1.0,
                             base=0, pattern=[[-1, P]], channel_multiplier=1).then_inc(poolk, 1)
            gp.affine_select(out=tri[:, :], in_=tri[:, :], compare_op=ALU.is_ge, fill=0.0,
                             base=0, pattern=[[-1, P]], channel_multiplier=1).then_inc(poolk, 1)
            gp.memset(rst[:, :].rearrange("p (e i) -> p e i", i=NT)[:, :, 0:1], 0.0).then_inc(poolk, 1)
            gp.memset(rst1[:, :].rearrange("p (e i) -> p e i", i=RT)[:, :, 0:1], 0.0).then_inc(poolk, 1)
            gp.iota(rowI[:, :], pattern=[[1, 1]], base=0, channel_multiplier=1).then_inc(poolk, 1)
            gp.iota(codes[:, :], pattern=[[-P, NT]], base=FAR, channel_multiplier=-1,
                    allow_small_or_imprecise_dtypes=True).then_inc(poolk, 1)
            gp.iota(revE[:, :], pattern=[[-1, E0]], base=E0, channel_multiplier=0,
                    allow_small_or_imprecise_dtypes=True).then_inc(poolk, 1)
            gp.iota(baseE[:, :], pattern=[[CAP, E1]], base=-DROP, channel_multiplier=0,
                    allow_small_or_imprecise_dtypes=True).then_inc(poolk, 1)
            gp.iota(jrow[:, :], pattern=[[P, NBLKP]], base=0, channel_multiplier=0,
                    allow_small_or_imprecise_dtypes=True).then_inc(poolk, 1)
            gp.iota(colL[:, 0:HID], pattern=[[1, NLANG], [0, A]], base=0, channel_multiplier=0,
                    allow_small_or_imprecise_dtypes=True).then_inc(poolk, 1)
            gp.iota(colL[:, HID:HID + NLANG], pattern=[[1, NLANG]], base=0, channel_multiplier=0,
                    allow_small_or_imprecise_dtypes=True).then_inc(poolk, 1)
            gp.memset(ones_f[:, :], 1.0).then_inc(poolk, 1)
            gp.memset(epsc[:, :], LN_EPS).then_inc(poolk, 1)
            pool.wait_ge(poolk, 19)
            gp.tensor_copy(disp[:, :, H:ROW], codes[:, :].unsqueeze(2)).then_inc(codes0, 1)

            pool.wait_ge(zero0, 16 * (NBLKP // 4))
            pool.wait_ge(slots0, 1)
            pool.wait_ge(codes0, 1)
            for t in range(NT):
                if t % G == 0:
                    pool.wait_ge(scaled, t + G)
                gp.indirect_dma_start(rows0, bass.IndirectOffsetOnAxis(ap=slot[:, 0, t:t + 1], axis=0),
                                      disp[:, t, :], None, bounds_check=NBLKP * P - 1,
                                      oob_is_err=False).then_inc(sc0, 16)

            last_token = pool.to_reg(T - 1)
            with pool.Fori(0, NBLKP // 4) as it:
                for s in range(4):
                    pool.wait_ge(e_oc, it * 4 + (s + 1))
                    pool.sem_inc(pool_turn)
                    gp.indirect_dma_start(back0, bass.IndirectOffsetOnAxis(ap=blk_i[s][:, 0:1], axis=0),
                                          blk_y[s][:, :], None, bounds_check=last_token,
                                          oob_is_err=False).then_inc(by_st[s], 16)

            pool.wait_ge(zero1, 16 * (E1 * CAP // (4 * P) + TOP_K * T // (8 * P)))
            HT = NT // 2
            for k in range(TOP_K):
                for t in range(NT):
                    if k == 0 and t % RT == 0:
                        pool.wait_ge(slots1, t // RT + 1)
                        pool.wait_ge(b_tk, (t + RT) // G)
                    if k == 1 and t == 0:
                        pool.wait_ge(slots1, NT // RT + 1)
                    gp.indirect_dma_start(rows1, bass.IndirectOffsetOnAxis(ap=slot[:, k, t:t + 1], axis=0),
                                          disp[:, t, :], None, bounds_check=E1 * CAP - 1,
                                          oob_is_err=False).then_inc(sc1[k][t // HT], 16)
                    if (k, t) in ((0, NT - 8), (1, HT - 8)):
                        h = k
                        pool.wait_ge(sc1[0][h], 16 * HT)
                        half = slice(h * HT, (h + 1) * HT)
                        gp.tensor_scalar(disp[:, half, H:ROW], codes[:, half].unsqueeze(2), float(-T), None,
                                         ALU.add).then_inc(codes1, 1)
                        pool.wait_ge(codes1, h + 1)
            last_row = pool.to_reg(TOP_K * T - 1)
            with pool.Fori(0, E1 // 2) as it:
                for v in range(2 * GPE):
                    k = v % 2
                    pool.wait_ge(q_oc, it * (2 * GPE) + (v + 1))
                    pool.sem_inc(pool_turn)
                    for u in range(U):
                        gp.indirect_dma_start(back1, bass.IndirectOffsetOnAxis(ap=grp_i[v % NX][:, u:u + 1], axis=0),
                                              grp_y[k][:, u, :], None, bounds_check=last_row,
                                              oob_is_err=False).then_inc(gy_st[k], 16)

        @block.scalar
        def _(eng):
            sc = nc.scalar

            def cp(dst, src):
                return sc.activation(dst, src, ACT.Copy)

            eng.dma_start(c0w[:, :].rearrange("p (s h) -> p s h", s=NSUB),
                          c0_w.rearrange("s p h -> p s h")).then_inc(ld_c0w, 16)
            eng.preload_act_table(ACT.Sigmoid)
            def copy_x(n):
                eng.wait_ge(pe_xt, n + 1)
                cp(xT[n % 2][:, :], PS[0][:, :]).then_inc(xT_done, 1)

            copy_x(0)
            for n in range(NG + 1):
                if n < NG:
                    if n + 1 < NG:
                        copy_x(n + 1)
                    for b in range(2):
                        eng.wait_ge(pe_c, QB * n + b + 1)
                        cp(condS[b * S:(b + 1) * S, :, :],
                           PS[1 + b][0:S, :].rearrange("p (i h) -> p i h", h=H)).then_inc(condA, 1)
                if n >= 1:
                    eng.wait_ge(pe_tok, n)
                    cp(disp[:, (n - 1) * G:n * G, 0:H],
                       PS[7][:, :].rearrange("p (i h) -> p i h", h=H)).then_inc(tok_done, 1)
            eng.wait_ge(mx0, 1)
            sc.activation(score[:, :], m1[:, :], ACT.Sigmoid).then_inc(sg0, 1)
            eng.preload_act_table(ACT.Silu)
            eng.wait_ge(sg0, 1)
            eng.wait_ge(tok_done, NG)
            for n in range(NG):
                for c in range(C0):
                    eng.wait_ge(pe_gu, 2 * C0 * n + 2 * c + 1)
                    if n >= 1:
                        eng.wait_ge(act_done, C0 * (n - 1) + c + 1)
                    sc.activation(sil[:, c, :], PS[2 * c][:, :], ACT.Silu).then_inc(sil_done, 1)
                for i in range(G):
                    t = n * G + i
                    sc.activation(disp[:, t, 0:H], disp[:, t, 0:H], ACT.Copy,
                                  scale=score[:, t:t + 1]).then_inc(scaled, 1)

            def copy_xT(j, k):
                eng.wait_ge(e_xt, j + 1)
                cp(blk_xT[k][:, :], PS[5 + k][:, 0:P]).then_inc(e_xc, 1)

            def silu(j, k):
                eng.wait_ge(e_gu, j + 1)
                sc.activation(blk_s[k][:, :], PS[k][:, 0:F0], ACT.Silu).then_inc(e_sl, 1)

            def copy_aT(j, k):
                eng.wait_ge(e_ta, j + 1)
                cp(blk_aT[k][:, :], PS[2 + k][:, 0:F0]).then_inc(e_at, 1)

            def act_stage(j, k, first=False, last=False):
                if not last:
                    copy_xT(j + 1, 1 - k)
                silu(j, k)
                if not first:
                    copy_aT(j - 1, 1 - k)

            copy_xT(0, 0)
            for j in range(4):
                act_stage(j, j % 2, first=j == 0)
            with eng.Fori(0, NBLKP // 4 - 2) as it:
                for s in range(4):
                    act_stage(it * 4 + (4 + s), s % 2)
            for j in range(NBLKP - 4, NBLKP):
                act_stage(j, j % 2, last=j == NBLKP - 1)
            copy_aT(NBLKP - 1, (NBLKP - 1) % 2)

            eng.wait_ge(ld_l1, 16 * (2 * (NCH - 1) + 8))
            def copy_x1(n):
                eng.wait_ge(b_xt, n + 1)
                cp(xT[n % 2][:, :], PS[0][:, :]).then_inc(b_xc, 1)

            def copy_rows(m):
                eng.wait_ge(b_bt, m + 1)
                cp(disp[:, m * G:(m + 1) * G, 0:H],
                   PS[6][:, :].rearrange("p (i h) -> p i h", h=H)).then_inc(b_tk, 1)

            def shared1_silu(n):
                for c in range(C1):
                    eng.wait_ge(s_gu, C1 * n + c + 1)
                    eng.wait_ge(b_w2, NG)
                    if n >= 2:
                        eng.wait_ge(s_dn, n - 1)
                    sc.activation(act[n % 2][:, c, :], PS[c][:, :], ACT.Silu,
                                  bias=sb1[:, c:c + 1]).then_inc(s_sl, 1)

            copy_x1(0)
            for n in range(NG + 2):
                if n + 1 < NG:
                    copy_x1(n + 1)
                if n < NG:
                    for c in range(NCH):
                        eng.wait_ge(b_w1, NCH * n + c + 1)
                        if n >= 2:
                            eng.wait_ge(b_w2, n - 1)
                        sc.activation(act[n % 2][0:KROWS[c], c, :], PS[1 + c][0:KROWS[c], :], ACT.Relu,
                                      bias=a_b1[0:KROWS[c], c:c + 1]).then_inc(b_rl, 1)
                if 1 <= n < NG + 1:
                    k = (n - 1) % 2
                    eng.wait_ge(b_var, n)
                    sc.activation(rstd[k][:, :], mv[:, :, 1], ACT.Sqrt, bias=epsc[:, :]).then_inc(b_std, 1)
                if 3 <= n:
                    copy_rows(n - 3)
                if 1 <= n < NG + 1:
                    eng.wait_ge(b_nb, n)
                    for i in range(G):
                        ins = sc.activation(nrm[k][:, i, :], nrm[k][:, i, :], ACT.Identity,
                                            scale=rstd[k][:, i:i + 1], bias=nmr[k][:, i:i + 1])
                    ins.then_inc(b_nm, 1)
            shared1_silu(0)
            copy_rows(NG - 1)
            eng.wait_ge(ex_in, 1)
            sc.activation(t1[:, 0:NT * E1], t1[:, 0:NT * E1], ACT.Exp).then_inc(ex_out, 1)
            eng.preload_act_table(ACT.Silu)
            for n in range(1, NG):
                shared1_silu(n)

            def q_copy(q, q_slot):
                eng.wait_ge(q_xt, q + 1)
                cp(xT[q_slot][:, 0:UP], PS[0][:, 0:UP]).then_inc(q_xc, 1)

            def q_silu(q, k, e):
                for c in range(C1):
                    if c % 2 == 0:
                        eng.wait_ge(q_gu, q * (C1 // 2) + (c // 2 + 1))
                    sc.activation(act[k][:, c, 0:UP], PS[1 + k * (C1 // 2) + c // 2][:, (c % 2) * UP:(c % 2 + 1) * UP],
                                  ACT.Silu, bias=b1r[e][:, c:c + 1]).then_inc(q_sl, 1)

            def q_stage(q, k, e, last=False):
                if not last:
                    q_copy(q + 1, 1 - k)
                q_silu(q, k, e)

            q_copy(0, 0)
            q_stage(0, 0, 0)
            with eng.Fori(0, E1 // 2 - 1) as it:
                for u in range(2 * GPE):
                    q_stage(it * (2 * GPE) + (1 + u), (1 + u) % 2, (1 + u) // GPE % 2)
            for q in range(1 + (E1 // 2 - 1) * 2 * GPE, NQ):
                q_stage(q, q % 2, q // GPE % 2, last=q == NQ - 1)

            for g in range(NG):
                eng.wait_ge(fy_ld[g], 16 * TOP_K)
                for i in range(G):
                    ins = sc.activation(back[1][g][:, i, :], back[1][g][:, i, :], ACT.Copy,
                                        scale=wk[:, 1, g * G + i:g * G + i + 1])
                ins.then_inc(f_sc, 1)

        @block.vector
        def _(dve):
            v = nc.vector
            chain = [0]

            def link(ins):
                chain[0] += 1
                ins.then_inc(dch, 1)
                dve.wait_ge(dch, chain[0])

            def bc(ap, shape):
                return ap.to_broadcast(shape)

            v.memset(a_w1[:, HID:(NCH - 1) * P + LASTK], 0.0)
            v.memset(a_b1[TAIL:LASTK, NCH - 1:NCH], 1.0).then_inc(dve_ready, 1)
            dve.wait_ge(ld_small, 16)
            link(v.tensor_scalar(w0off[:, :], w0off[:, :], float(H), None, ALU.mult))
            dve.wait_ge(poolk, 19)
            link(v.tensor_copy(rowF[:, :], rowI[:, :]))
            link(v.tensor_scalar(other[:, :], colL[:, :], rowF[0:NLANG, :], -BIG, ALU.not_equal, ALU.mult))
            dve.wait_ge(ld_tab, 16 * 7)
            link(v.tensor_scalar(hot0[:, :], subjI[:, :], rowF[0:NSUB, :], None, ALU.is_equal))
            link(v.tensor_scalar(hot1[:, :], langI[:, :], rowF[0:NLANG, :], None, ALU.is_equal))
            link(v.tensor_copy(hot1b[:, :], hot1[:, :]))
            v.engine_nop().then_inc(dve_ready, 1)
            dve.wait_ge(pe_tab, 1)
            link(v.tensor_copy(c0bT[:, :], PS[6][:, 0:B]))
            link(v.tensor_copy(gamT[:, :], PS[6][:, B:2 * B]))
            link(v.tensor_copy(betT[:, :], PS[6][:, 2 * B:3 * B]))
            v.engine_nop().then_inc(tab_done, 1)

            def first_max(vals, ne, keys, out, i0, n):
                shape = [P, n, ne]
                w3 = lambda a: a[:, i0 * ne:(i0 + n) * ne].rearrange("p (i e) -> p i e", e=ne)
                top, best = m1[:, i0:i0 + n], m3[:, i0:i0 + n]
                link(v.tensor_reduce(top, w3(vals), AX.X, ALU.max))
                link(v.tensor_tensor(w3(keys), w3(vals), bc(top.unsqueeze(2), shape), ALU.is_equal))
                link(v.tensor_tensor(w3(keys), w3(keys), bc(revE[:, E0 - ne:E0].unsqueeze(1), shape), ALU.mult))
                link(v.tensor_reduce(best, w3(keys), AX.X, ALU.max))
                link(v.tensor_tensor(out, w3(keys), bc(best.unsqueeze(2), shape), ALU.is_equal))

            te = lambda a, ne: a.rearrange("p (i e) -> p i e", e=ne)
            et = lambda a, n: a.rearrange("p (e i) -> p e i", i=n)
            by_t = lambda a, n: a.rearrange("p (e i) -> p i e", i=n)

            for n in range(NG + 1):
                if n >= 1:
                    m = n - 1
                    dve.wait_ge(pe_ht, n)
                    v.tensor_tensor(featT[:, m * GP:n * GP].rearrange("p (b s) -> p b s", s=S),
                                    PS[5][:, :].rearrange("p (b s) -> p b s", s=S),
                                    bc(c0bT[:, m * GB:n * GB].unsqueeze(2), [P, GB, S]),
                                    ALU.add).then_inc(hT_done, 1)
                if n < NG:
                    for b in range(2, 4):
                        dve.wait_ge(pe_c, QB * n + b + 1)
                        v.tensor_copy(condS[b * S:(b + 1) * S, :, :],
                                      PS[1 + b][0:S, :].rearrange("p (i h) -> p i h", h=H)).then_inc(condD, 1)
                if n >= 1:
                    dve.wait_ge(pe_l, n)
                    v.tensor_copy(lg[:, m * G * E0:n * G * E0], PS[6][:, 0:G * E0]).then_inc(lg_done, 1)
                    if n * G % RT == 0:
                        dve.wait_ge(lg_done, n)
                        first_max(lg, E0, t1, by_t(mask[:, :], NT)[:, n * G - RT:n * G, :], n * G - RT, RT)

            def glu0(n):
                for c in range(C0):
                    dve.wait_ge(sil_done, C0 * n + c + 1)
                    dve.wait_ge(pe_gu, 2 * C0 * n + 2 * c + 2)
                    if n >= 2:
                        dve.wait_ge(pe_dn, n - 1)
                    v.tensor_tensor(act[n % 2][:, c, :], PS[2 * c + 1][:, :], sil[:, c, :],
                                    ALU.mult).then_inc(act_done, 1)

            def add0(n):
                dve.wait_ge(pe_dn, n + 1)
                a = acc[:, n * G:(n + 1) * G, :]
                v.tensor_tensor(a, a, PS[4][:, :].rearrange("p (i h) -> p i h", h=H), ALU.add).then_inc(acc0, 1)

            v.engine_nop().then_inc(mx0, 1)
            link(v.tensor_tensor_scan(seen[:, :], rst[:, :], mask[:, :], 0.0, ALU.mult, ALU.add))
            v.engine_nop().then_inc(mk0, 1)
            glu0(0)
            dve.wait_ge(pe_rank0, 1)
            link(v.tensor_scalar(padI[:, :], PS[6][:, 0:E0], float(P - 1), None, ALU.add))
            link(v.tensor_scalar(padI[:, :], padI[:, :], P.bit_length() - 1, P.bit_length() - 1,
                                 ALU.arith_shift_right, ALU.arith_shift_left))
            link(v.tensor_copy(padF[:, :], padI[:, :]))
            link(v.tensor_tensor_scan(endE[:, :], ones_f[:, :], padF[:, :], 0.0, ALU.mult, ALU.add))
            link(v.tensor_tensor(padF[:, :], endE[:, :], padF[:, :], ALU.subtract))
            link(v.tensor_tensor(et(t3[:, :], NT), et(PS[5][:, :], NT),
                                 bc(padF[:, :].unsqueeze(2), [P, E0, NT]), ALU.add))
            link(v.tensor_tensor(t3[:, :], t3[:, :], mask[:, :], ALU.mult))
            link(v.tensor_reduce(slotF[:, 0, :], by_t(t3[:, :], NT), AX.X, ALU.add))
            v.tensor_copy(slot[:, 0, :], slotF[:, 0, :]).then_inc(slots0, 1)
            link(v.tensor_tensor(cmpj[:, :, :], bc(jrow[:, :].unsqueeze(2), [1, NBLKP, E0 - 1]),
                                 bc(endE[0:1, 0:E0 - 1].unsqueeze(1), [1, NBLKP, E0 - 1]), ALU.is_ge))
            link(v.tensor_reduce(bexp[:, :], cmpj[:, :, :], AX.X, ALU.add))
            v.tensor_scalar(guo[:, :], bexp[:, :], float(F0x2), None, ALU.mult)
            v.tensor_scalar(dno[:, :], bexp[:, :], float(C0 * H), None, ALU.mult).then_inc(blocks0, 1)

            for n in range(1, NG + 1):
                if n < NG:
                    glu0(n)
                add0(n - 1)

            def index(j, s, turn, first=False):
                dve.wait_ge(bx_ld[s], turn * 16 + 16)
                if not first:
                    dve.wait_ge(by_st[s], turn * 16)
                v.tensor_scalar(blk_i[s][:, :], blk_x[s][:, H:ROW], -1.0, float(FAR), ALU.mult,
                                ALU.add).then_inc(e_ix, 1)

            def glu(j, k):
                dve.wait_ge(e_sl, j + 1)
                v.tensor_tensor(blk_a[k][:, :], PS[k][:, F0:F0x2], blk_s[k][:, :], ALU.mult).then_inc(e_ac, 1)

            def result(j, s):
                dve.wait_ge(e_dn, j + 1)
                v.tensor_copy(blk_y[s][:, :], PS[4 if s % 2 == 0 else 7][:, 0:H]).then_inc(e_oc, 1)

            def dve_stage(j, s, turn, first=False):
                index(j, s, turn, first)
                glu(j, s % 2)
                if not (isinstance(j, int) and j < 2):
                    result(j - 2, (s - 2) % 4)

            for j in range(4):
                dve_stage(j, j, 0, first=True)
            with dve.Fori(0, NBLKP // 4 - 1) as it:
                for s in range(4):
                    dve_stage(it * 4 + (4 + s), s, it + 1)
            for j in range(NBLKP - 2, NBLKP):
                result(j, j % 4)

            dve.wait_ge(acc0, NG)

            def residual(n):
                dve.wait_ge(y0_ld[n % 4], 16 * (n // 4 + 1))
                a = acc[:, n * G:(n + 1) * G, :]
                v.tensor_tensor(a, a, y0g[n % 4][:, :, :], ALU.add).then_inc(x1_done, 1)

            WE = NT * E1
            L3 = [P, NT, E1]

            def choice_slots(k, i0, n, pos):
                cols = slice(k * WE + i0 * E1, k * WE + (i0 + n) * E1)
                link(v.scalar_tensor_tensor(out=keep[:, cols], in0=pos, scalar=float(CAP), in1=mask[:, cols],
                                            op0=ALU.is_lt, op1=ALU.mult))
                link(v.tensor_tensor(et(t3[:, cols], n), et(pos, n), bc(baseE[:, :].unsqueeze(2), [P, E1, n]),
                                     ALU.add))
                if k == 0:
                    v.engine_nop().then_inc(b_rk, 1)
                link(v.tensor_tensor(t3[:, cols], t3[:, cols], keep[:, cols], ALU.mult))
                link(v.tensor_reduce(slotF[:, k, i0:i0 + n], by_t(t3[:, cols], n), AX.X, ALU.add))
                v.tensor_scalar(slot[:, k, i0:i0 + n], slotF[:, k, i0:i0 + n], float(DROP), None,
                                ALU.add).then_inc(slots1, 1)

            def first_choices(r):
                cols = slice(r * RT * E1, (r + 1) * RT * E1)
                first_max(lg, E1, t2, by_t(mask[:, cols], RT), r * RT, RT)
                link(v.tensor_tensor_scan(seen[:, cols], rst1[:, :], mask[:, cols], 0.0, ALU.mult, ALU.add))
                v.engine_nop().then_inc(mk1, 1)

            def first_slots(r):
                dve.wait_ge(pe_rank1, r + 1)
                last = et(seen[:, r * RT * E1:(r + 1) * RT * E1], RT)[:, :, RT - 1]
                if r == 0:
                    link(v.tensor_copy(before[:, :], last))
                else:
                    link(v.tensor_tensor(before[:, :], before[:, :], last, ALU.add))
                choice_slots(0, r * RT, RT, PS[7][:, WE:WE + RT * E1])

            residual(0)
            residual(1)
            for n in range(NG + 3):
                if n + 2 < NG:
                    residual(n + 2)
                if (n - 3) * G % RT == 0 and n > 3:
                    first_slots((n - 3) * G // RT - 1)
                if 1 <= n < NG + 1:
                    m = n - 1
                    k = m % 2
                    dve.wait_ge(b_w2, n)
                    dve.wait_ge(x1_done, n)
                    if m >= 2:
                        dve.wait_ge(b_nt, m - 1)
                    link(v.tensor_tensor(nrm[k][:, :, :], PS[4][:, :].rearrange("p (i h) -> p i h", h=H),
                                         acc[:, m * G:(m + 1) * G, :], ALU.add))
                    for i in range(G):
                        ins = v.bn_stats(bn6[:, i, :], nrm[k][:, i, :])
                    link(ins)
                    for i in range(G):
                        ins = v.bn_aggr(mv[:, i, :], bn6[:, i, :])
                    ins.then_inc(b_var, 1)
                if 2 <= n < NG + 2:
                    g = n - 2
                    dve.wait_ge(b_nt, g + 1)
                    f3 = featT[:, g * GP:(g + 1) * GP].rearrange("p (b s) -> p b s", s=S)
                    link(v.tensor_tensor(f3, PS[5][:, :].rearrange("p (b s) -> p b s", s=S),
                                         bc(gamT[:, g * GB:(g + 1) * GB].unsqueeze(2), [P, GB, S]), ALU.mult))
                    v.tensor_tensor(f3, f3, bc(betT[:, g * GB:(g + 1) * GB].unsqueeze(2), [P, GB, S]),
                                    ALU.add).then_inc(b_xn, 1)
                if 1 <= n < NG + 1:
                    dve.wait_ge(b_std, n)
                    link(v.reciprocal(rstd[k][:, :], rstd[k][:, :]))
                    v.scalar_tensor_tensor(out=nmr[k][:, :], in0=mv[:, :, 0], scalar=-1.0, in1=rstd[k][:, :],
                                           op0=ALU.mult, op1=ALU.mult).then_inc(b_nb, 1)
                if n >= 3:
                    m = n - 3
                    dve.wait_ge(b_lg, m + 1)
                    v.tensor_copy(lg[:, m * G * E1:(m + 1) * G * E1], PS[7][:, 0:G * E1]).then_inc(b_lc, 1)
                    if (m + 1) * G % RT == 0:
                        dve.wait_ge(b_lc, m + 1)
                        first_choices((m + 1) * G // RT - 1)

            def add1(n):
                dve.wait_ge(s_dn, n + 1)
                a = acc[:, n * G:(n + 1) * G, :]
                link(v.scalar_tensor_tensor(out=a, in0=PS[4][:, :].rearrange("p (i h) -> p i h", h=H),
                                            scalar=SHARED_SCALE, in1=a, op0=ALU.mult, op1=ALU.add))
                v.tensor_tensor(a, a, bc(sb2[:, :].unsqueeze(1), [P, G, H]), ALU.add).then_inc(s_ac, 1)

            link(v.tensor_reduce(m1[:, :], te(lg[:, 0:WE], E1), AX.X, ALU.max))
            v.tensor_tensor(te(t1[:, 0:WE], E1), te(lg[:, 0:WE], E1), bc(m1[:, :].unsqueeze(2), L3),
                            ALU.subtract).then_inc(ex_in, 1)
            first_slots(NT // RT - 1)
            dve.wait_ge(ex_out, 1)
            link(v.tensor_reduce(m1[:, :], te(t1[:, 0:WE], E1), AX.X, ALU.add))
            link(v.reciprocal(m1[:, :], m1[:, :]))
            link(v.tensor_tensor(te(lg[:, 0:WE], E1), te(t1[:, 0:WE], E1), bc(m1[:, :].unsqueeze(2), L3), ALU.mult))
            parts = lambda a: a.rearrange("p (r e i) -> p r i e", e=E1, i=RT)
            rie = lambda a: a.rearrange("p (r i e) -> p r i e", e=E1, i=RT)
            link(v.tensor_scalar(rie(t2[:, 0:WE]), parts(mask[:, 0:WE]), -1.0, 1.0, ALU.mult, ALU.add))
            link(v.tensor_tensor(t2[:, 0:WE], lg[:, 0:WE], t2[:, 0:WE], ALU.mult))
            first_max(t2, E1, t1, by_t(mask[:, WE:2 * WE], NT), 0, NT)
            link(v.tensor_tensor_scan(seen[:, WE:2 * WE], rst[:, 0:WE], mask[:, WE:2 * WE], 0.0, ALU.mult, ALU.add))
            v.engine_nop().then_inc(mk1, 1)
            link(v.tensor_scalar(sb2[:, :], sb2[:, :], SHARED_SCALE, None, ALU.mult))
            add1(0)
            dve.wait_ge(pe_rank1, NT // RT + 1)
            link(v.tensor_scalar(cnt1[:, :], PS[6][:, 0:E1], float(CAP), None, ALU.min))
            link(v.tensor_tensor(et(t1[:, 0:WE], NT), et(PS[5][:, 0:WE], NT), bc(cnt1[:, :].unsqueeze(2), [P, E1, NT]),
                                 ALU.add))
            choice_slots(1, 0, NT, t1[:, 0:WE])
            add1(1)
            add1(2)
            link(v.tensor_tensor(rie(t2[:, 0:WE]), parts(keep[:, 0:WE]), rie(lg[:, 0:WE]), ALU.mult))
            link(v.tensor_tensor(te(t2[:, WE:2 * WE], E1), by_t(keep[:, WE:2 * WE], NT), te(lg[:, 0:WE], E1), ALU.mult))
            link(v.tensor_reduce(wk[:, :, :], t2[:, :].rearrange("p (k i e) -> p k i e", k=TOP_K, e=E1), AX.X, ALU.add))
            link(v.tensor_tensor(m1[:, :], wk[:, 0, :], wk[:, 1, :], ALU.add))
            link(v.tensor_scalar(m1[:, :], m1[:, :], TINY, None, ALU.max))
            link(v.reciprocal(m1[:, :], m1[:, :]))
            link(v.tensor_tensor(wk[:, :, :], wk[:, :, :], bc(m1[:, :].unsqueeze(1), [P, TOP_K, NT]), ALU.mult))
            for n in range(3, NG):
                add1(n)

            def q_index(k, turn):
                dve.wait_ge(gx_ld[k], turn * 16 + 16)
                v.tensor_scalar(grp_i[k][:, :], grp_x[k][:, :, H], -1.0, float(FAR), ALU.mult,
                                ALU.add).then_inc(q_ix, 1)

            def q_result(q, k, e, turn=None):
                dve.wait_ge(q_dn, q + 1)
                if turn is not None:
                    dve.wait_ge(gy_st[k], turn * (16 * U))
                v.tensor_tensor(grp_y[k][:, :, :], PS[5 + k][:, 0:UP].rearrange("p (u h) -> p u h", h=H),
                                bc(b2r[e][:, :].unsqueeze(1), [P, U, H]), ALU.add).then_inc(q_oc, 1)

            q_index(0, 0)
            q_index(1, 0)
            for q in range(2):
                q_index(q + 2, 0)
                q_result(q, q, 0)
            with dve.Fori(0, E1 // 2 - 1) as it:
                for u in range(2 * GPE):
                    b = 2 + u
                    q_index((b + 2) % NX, it * 2 + (b + 2) // NX)
                    q_result(it * (2 * GPE) + b, b % 2, b // GPE % 2, it * GPE + b // 2)
            for q in range(2 + (E1 // 2 - 1) * 2 * GPE, NQ):
                if q + 2 < NQ:
                    q_index((q + 2) % NX, (q + 2) // NX)
                q_result(q, q % 2, q // GPE % 2, q // 2)

            for g in range(NG):
                dve.wait_ge(fy_ld[g], 16 * TOP_K)
                for i in range(G):
                    t = g * G + i
                    ins = v.scalar_tensor_tensor(out=acc[:, t, :], in0=back[0][g][:, i, :], scalar=wk[:, 0, t:t + 1],
                                                 in1=acc[:, t, :], op0=ALU.mult, op1=ALU.add)
                link(ins)
                dve.wait_ge(f_sc, g + 1)
                a = acc[:, g * G:(g + 1) * G, :]
                v.tensor_tensor(a, a, back[1][g], ALU.add).then_inc(f_ac, 1)

        @block.tensor
        def _(pe):
            def tr(dst, src, k=P):
                return nc.tensor.transpose(dst, src, ident[0:k, 0:k])

            pe.wait_ge(dve_ready, 2)
            pe.wait_ge(ld_tab, 16 * 7)
            pe.wait_ge(poolk, 19)
            mm(PS[6][:, 0:B], c0bs[:, :], hot0[:, :], start=True, stop=True)
            mm(PS[6][:, B:2 * B], gam[:, :], hot1[:, :], start=True, stop=True)
            mm(PS[6][:, 2 * B:3 * B], bet[:, :], hot1[:, :], start=True, stop=True).then_inc(pe_tab, 1)

            def x_in(n):
                pe.wait_ge(x_ld[n], 16)
                if n >= 1:
                    pe.wait_ge(xT_done, n)
                for i in range(G):
                    last = tr(tile(PS[0], i), acc[:, n * G + i, :])
                last.then_inc(pe_xt, 1)

            x_in(0)
            for n in range(NG + 1):
                if n + 1 < NG:
                    x_in(n + 1)
                if n >= 1:
                    pe.wait_ge(condA, 2 * n)
                    pe.wait_ge(condD, 2 * n)
                    if n == 1:
                        pe.wait_ge(tab_done, 1)
                    else:
                        pe.wait_ge(hT_done, n - 1)
                    for i in range(G):
                        last = tr(tile(PS[5], i), condS[:, i, :])
                    last.then_inc(pe_ht, 1)
                if n < NG:
                    pe.wait_ge(xT_done, n + 1)
                    if n == 0:
                        pe.wait_ge(ld_c0w, 16)
                    _, offs = nc.values_load_multi_w_load_instructions(
                        w0off[0:1, n * GB:(n + 1) * GB], engines=(mybir.EngineType.PE,), min_val=0,
                        max_val=(NSUB - 1) * H, skip_runtime_bounds_check_because="subjects are under NSUB")
                    for b in range(QB):
                        for i in range(G):
                            t = i * QB + b
                            last = mm(PS[1 + b][0:S, i * H:(i + 1) * H],
                                      xT[n % 2][:, t * S:(t + 1) * S], c0w[:, ds(offs[t], H)],
                                      start=True, stop=True)
                        last.then_inc(pe_c, 1)
                if n >= 1:
                    m = n - 1
                    pe.wait_ge(hT_done, n)
                    if m >= 1:
                        pe.wait_ge(lg_done, m)
                        pe.wait_ge(tok_done, m)
                    for i in range(G):
                        last = mm(PS[6][:, i * E0:(i + 1) * E0], tile(featT, m * G + i), rt0[:, :],
                                  start=True, stop=True)
                    last.then_inc(pe_l, 1)
                    for i in range(G):
                        last = tr(tile(PS[7], i), tile(featT, m * G + i))
                    last.then_inc(pe_tok, 1)

            def shared0_up(n):
                for c in range(C0):
                    for w, b in ((shg, 2 * c), (shu, 2 * c + 1)):
                        if n >= 1:
                            pe.wait_ge(act_done, C0 * (n - 1) + c + 1)
                        mm(PS[b][:, :], w[:, c * P:(c + 1) * P], featT[:, n * GP:(n + 1) * GP],
                           start=True, stop=True).then_inc(pe_gu, 1)

            def shared0_down(n):
                pe.wait_ge(act_done, C0 * (n + 1))
                if n >= 1:
                    pe.wait_ge(acc0, n)
                for i in range(G):
                    for c in range(C0):
                        last = mm(tile(PS[4], i), tile(act[n % 2][:, c, :], i), shd[:, c, :],
                                  start=c == 0, stop=c == C0 - 1)
                last.then_inc(pe_dn, 1)

            pe.wait_ge(ld_sh0, 48)
            shared0_up(0)
            pe.wait_ge(mk0, 1)
            mm(PS[6][:, 0:E0], ones_b[:, :], seen[:, :].rearrange("p (e i) -> p e i", i=NT)[:, :, NT - 1],
               start=True, stop=True)
            mm(PS[5][:, :], tri[:, :], mask[:, :], start=True, stop=False)
            mm(PS[5][:, :], ones_b[:, :], seen[:, :], start=False, stop=True).then_inc(pe_rank0, 1)
            for n in range(1, NG):
                shared0_up(n)
                shared0_down(n - 1)
            shared0_down(NG - 1)

            def x_tr(j, s, turn, k):
                pe.wait_ge(bx_ld[s], turn * 16 + 16)
                tr(PS[5 + k][:, 0:P], blk_x[s][:, 0:H]).then_inc(e_xt, 1)

            def gate_up(j, k, off):
                pe.wait_ge(e_xc, j + 1)
                mm(PS[k][:, :], blk_xT[k][:, :], w_gu[:, ds(off, F0x2)], start=True, stop=True).then_inc(e_gu, 1)

            def a_tr(j, k):
                pe.wait_ge(e_ac, j + 1)
                for c in range(C0):
                    last = tr(tile(PS[2 + k], c), tile(blk_a[k], c))
                last.then_inc(e_ta, 1)

            def down(j, k, off, first=False):
                pe.wait_ge(e_at, j + 1)
                if not first:
                    pe.wait_ge(e_oc, j - 1)
                for c in range(C0):
                    last = mm(PS[4 if k == 0 else 7][:, 0:H], blk_aT[k][:, c * P:(c + 1) * P],
                              w_dn[:, ds(off + c * H, H)], start=c == 0, stop=c == C0 - 1)
                last.then_inc(e_dn, 1)

            def offsets(tab, at, n, most):
                _, vals = nc.values_load_multi_w_load_instructions(
                    tab[0:1, ds(at, n)], engines=(mybir.EngineType.PE,), min_val=0, max_val=most,
                    skip_runtime_bounds_check_because="a count of at most E0 - 1, times the stride")
                return vals

            GU_MAX = (E0 - 1) * F0x2
            DN_MAX = (E0 - 1) * C0 * H
            pe.wait_ge(acc0, NG)
            pe.wait_ge(blocks0, 1)
            pe.wait_ge(slots0, 1)
            pe.wait_ge(tok_done, NG)
            pe.wait_ge(ld_gu, 16)
            pe.wait_ge(ld_dn, 16)

            def pe_stages(j0, turn, s_off, stages, offs_g, offs_d, lo=None):
                for i in range(stages):
                    s = i % 4
                    j = j0 + i
                    static = isinstance(j, int)
                    if not (static and j == NBLKP - 1):
                        x_tr(j + 1, (s + 1) % 4, turn + (1 if s == 3 else 0), (s + 1) % 2)
                    gate_up(j, s % 2, offs_g[i])
                    if not (static and j < 2):
                        down(j - 2, s % 2, offs_d[i], first=static and j < 4)
                    if not (static and j < 1):
                        a_tr(j - 1, (s + 1) % 2)

            x_tr(0, 0, 0, 0)
            og = offsets(guo, 0, 4, GU_MAX)
            od = offsets(dno, 0, 2, DN_MAX)
            pe_stages(0, 0, 0, 4, og, [None, None] + list(od))
            with pe.Fori(0, NBLKP // 4 - 2) as it:
                og = offsets(guo, it * 4 + 4, 4, GU_MAX)
                od = offsets(dno, it * 4 + 2, 4, DN_MAX)
                pe_stages(it * 4 + 4, it + 1, 0, 4, og, od)
            og = offsets(guo, NBLKP - 4, 4, GU_MAX)
            od = offsets(dno, NBLKP - 6, 6, DN_MAX)
            pe_stages(NBLKP - 4, NBLKP // 4 - 1, 0, 4, og, od)
            down(NBLKP - 2, 0, od[4])
            a_tr(NBLKP - 1, 1)
            down(NBLKP - 1, 1, od[5])

            pe.wait_ge(e_oc, NBLKP)
            pe.wait_ge(ld_l1, 16 * (2 * (NCH - 1) + 8))
            def x1_in(n):
                pe.wait_ge(x1_done, n + 1)
                if n >= 1:
                    pe.wait_ge(b_xc, n)
                for i in range(G):
                    last = tr(tile(PS[0], i), acc[:, n * G + i, :])
                last.then_inc(b_xt, 1)

            WE = NT * E1

            def rank1(r):
                cols = slice(r * RT * E1, (r + 1) * RT * E1)
                pos = PS[7][:, WE:WE + RT * E1]
                pe.wait_ge(mk1, r + 1)
                pe.wait_ge(b_lc, (r + 1) * RT // G)
                mm(pos, tri[:, :], mask[:, cols], start=True, stop=False)
                last = mm(pos, ones_b[:, :], seen[:, cols], start=False, stop=r == 0)
                if r:
                    last = mm(pos.rearrange("p (e i) -> p e i", i=RT), ones_b[:, :],
                              before[:, :].unsqueeze(2).to_broadcast([P, E1, RT]), start=False, stop=True)
                last.then_inc(pe_rank1, 1)

            def shared1_up(n):
                for c in range(C1):
                    if n >= 1:
                        pe.wait_ge(s_sl, C1 * (n - 1) + c + 1)
                    mm(PS[c][:, :], sw1[:, c * P:(c + 1) * P], featT[:, n * GP:(n + 1) * GP],
                       start=True, stop=True).then_inc(s_gu, 1)

            x1_in(0)
            for n in range(NG + 3):
                if n == NG + 1:
                    pe.wait_ge(b_xc, NG)
                    pe.wait_ge(b_rl, NCH * NG)
                    pe.wait_ge(b_var, NG)
                    shared1_up(0)
                if n + 1 < NG:
                    x1_in(n + 1)
                if n < NG:
                    pe.wait_ge(b_xc, n + 1)
                    if n >= 1:
                        pe.wait_ge(b_rl, NCH * n)
                    for c in range(NCH):
                        cols = slice(c * P, c * P + KROWS[c])
                        mm(PS[1 + c][0:KROWS[c], :], a_w1[:, cols], xT[n % 2][:, :], start=True, stop=False)
                        mm(PS[1 + c][0:KROWS[c], :].rearrange("p (b s) -> p b s", s=S), other[:, cols],
                           hot1b[:, n * GB:(n + 1) * GB].unsqueeze(2).to_broadcast([NLANG, GB, S]),
                           start=False, stop=True).then_inc(b_w1, 1)
                if (n - 3) * G % RT == 0 and n > 3:
                    rank1((n - 3) * G // RT - 1)
                if 1 <= n < NG + 1:
                    m = n - 1
                    pe.wait_ge(b_rl, NCH * n)
                    if m >= 1:
                        pe.wait_ge(b_var, m)
                    for i in range(G):
                        for c in range(NCH):
                            last = mm(tile(PS[4], i), tile(act[m % 2][0:KROWS[c], c, :], i),
                                      a_w2[0:KROWS[c], c, :], start=c == 0, stop=c == NCH - 1)
                    last.then_inc(b_w2, 1)
                if 2 <= n < NG + 2:
                    m = n - 2
                    pe.wait_ge(b_nm, m + 1)
                    if m >= 1:
                        pe.wait_ge(b_xn, m)
                    for i in range(G):
                        last = tr(tile(PS[5], i), nrm[m % 2][:, i, :])
                    last.then_inc(b_nt, 1)
                if n >= 3:
                    m = n - 3
                    pe.wait_ge(b_xn, m + 1)
                    if m >= 1:
                        pe.wait_ge(b_lc, m)
                        if m * G >= RT:
                            pe.wait_ge(b_rk, m * G // RT)
                        pe.wait_ge(b_tk, m)
                    for i in range(G):
                        last = mm(PS[7][:, i * E1:(i + 1) * E1], tile(featT, m * G + i), rt1[:, :],
                                  start=True, stop=True)
                    last.then_inc(b_lg, 1)
                    for i in range(G):
                        last = tr(tile(PS[6], i), tile(featT, m * G + i))
                    last.then_inc(b_bt, 1)

            def shared1_down(n):
                pe.wait_ge(s_sl, C1 * (n + 1))
                if n >= 1:
                    pe.wait_ge(s_ac, n)
                for i in range(G):
                    for c in range(C1):
                        last = mm(tile(PS[4], i), tile(act[n % 2][:, c, :], i), sw2[:, c, :],
                                  start=c == 0, stop=c == C1 - 1)
                last.then_inc(s_dn, 1)

            shared1_down(0)
            rank1(NT // RT - 1)
            shared1_up(1)
            shared1_up(2)
            shared1_down(1)
            pe.wait_ge(b_tk, NG)
            pe.wait_ge(mk1, NT // RT + 1)
            mm(PS[6][:, 0:E1], ones_b[:, :], before[:, :], start=True, stop=True)
            mm(PS[5][:, 0:WE], tri[:, :], mask[:, WE:2 * WE], start=True, stop=False)
            mm(PS[5][:, 0:WE], ones_b[:, :], seen[:, WE:2 * WE], start=False, stop=True).then_inc(pe_rank1, 1)
            for n in range(3, NG):
                shared1_up(n)
                shared1_down(n - 1)
            shared1_down(NG - 1)

            def q_tr(k, turn):
                pe.wait_ge(gx_ld[k], turn * 16 + 16)
                for u in range(U):
                    last = tr(tile(PS[0], u), grp_x[k][:, u, 0:H])
                last.then_inc(q_xt, 1)

            def q_up(q, k, e):
                for c in range(C1):
                    last = mm(PS[1 + k * (C1 // 2) + c // 2][:, (c % 2) * UP:(c % 2 + 1) * UP],
                              w1r[e][:, c * P:(c + 1) * P], xT[k][:, 0:UP], start=True, stop=True)
                    if c % 2 == 1:
                        last.then_inc(q_gu, 1)

            def q_down(q, k, e, first=False):
                pe.wait_ge(q_sl, q * C1 + C1)
                if not first:
                    pe.wait_ge(q_oc, q - 1)
                for u in range(U):
                    for c in range(C1):
                        last = mm(PS[5 + k][:, u * P:(u + 1) * P], act[k][:, c, u * P:(u + 1) * P],
                                  w2r[e][:, c, :], start=c == 0, stop=c == C1 - 1)
                last.then_inc(q_dn, 1)

            def q_stage(q, w, e, we, k, turn, weights=None, first=False, last=False):
                pe.wait_ge(q_xc, q + 1)
                if not last:
                    q_tr(k, turn)
                if weights is not None:
                    pe.wait_ge(w_ld[e], weights)
                q_up(q, w, e)
                if not (isinstance(q, int) and q == 0):
                    q_down(q - 1, 1 - w, we, first=first)

            def q_args(b, it2=0, it64=0):
                return (b % 2, b // GPE % 2, (b - 1) // GPE % 2, (b + 1) % NX, it2 + (b + 1) // NX,
                        (it64 + (b // (2 * GPE) + 1) * 64) if b % GPE == 0 else None)

            pe.wait_ge(s_ac, NG)
            q_tr(0, 0)
            for q in range(3):
                q_stage(q, *q_args(q), first=True)
            with pe.Fori(0, E1 // 2 - 1) as it:
                for u in range(2 * GPE):
                    q_stage(it * (2 * GPE) + (3 + u), *q_args(3 + u, it * 2, it * 64))
            for q in range(3 + (E1 // 2 - 1) * 2 * GPE, NQ):
                q_stage(q, *q_args(q), last=q == NQ - 1)
            q_down(NQ - 1, (NQ - 1) % 2, (E1 - 1) % 2)


def kernel(**inputs):
    import numpy as np
    import concourse.bacc as bacc
    from concourse import mybir
    from concourse.bass_utils import run_bass_kernel_spmd

    i = {k: np.asarray(a) for k, a in inputs.items()}
    x = i["x"]
    nb, ns, h = x.shape
    lw1 = i["L1_cond_W1"]
    nl, _, na = lw1.shape
    e1, f1 = i["L1_ffn_b1"].shape
    arrays = {
        "x": x.reshape(nb * ns, h),
        "subj": i["itok_B_0_15"].reshape(1, nb),
        "lang": i["itok_B_0_8"].reshape(1, nb),
        "c0_w": i["L0_cond_weights"],
        "c0_b": i["L0_cond_b"],
        "f0_router": i["L0_ffn_w_router"].T,
        "f0_gate_up": i["L0_ffn_gate_up_proj"],
        "f0_down": i["L0_ffn_down_proj"],
        "f0_sh_gate": i["L0_ffn_w_gate"].T,
        "f0_sh_up": i["L0_ffn_w_up"].T,
        "f0_sh_down": i["L0_ffn_w_down"].T,
        "c1_w1": lw1.transpose(1, 0, 2).reshape(h, nl * na),
        "c1_b1": i["L1_cond_b1"].reshape(nl * na, 1),
        "c1_w2": i["L1_cond_W2"].reshape(nl * na, h),
        "c1_b2": i["L1_cond_b2"],
        "c1_gamma": i["L1_cond_gamma"],
        "c1_beta": i["L1_cond_beta"],
        "f1_router": i["L1_ffn_router_w"],
        "f1_w1": i["L1_ffn_w1"],
        "f1_b1": i["L1_ffn_b1"].reshape(e1, f1 // 128, 128).transpose(0, 2, 1),
        "f1_w2": i["L1_ffn_w2"],
        "f1_b2": i["L1_ffn_b2"],
        "f1_sh_w1": i["L1_ffn_sw1"],
        "f1_sh_b1": i["L1_ffn_sb1"].reshape(f1 // 128, 128).T,
        "f1_sh_w2": i["L1_ffn_sw2"],
        "f1_sh_b2": i["L1_ffn_sb2"].reshape(1, h),
    }
    arrays = {k: np.ascontiguousarray(a) for k, a in arrays.items()}
    nc = bacc.Bacc("TRN2", target_bir_lowering=False, num_devices=1)
    args = [nc.dram_tensor(f"in_{k}", a.shape, mybir.dt.from_np(a.dtype), kind="ExternalInput").ap()
            for k, a in arrays.items()]
    res = nc.dram_tensor("out_x", (nb * ns, h), mybir.dt.float32, kind="ExternalOutput").ap()
    adaln_moe_two_layers(nc, *args, res)
    r = run_bass_kernel_spmd(nc, [{f"in_{k}": a for k, a in arrays.items()}], core_ids=[0])
    return r.results[0]["out_x"].reshape(nb, ns, h)
```

```python
import concourse.bass as bass
from concourse import mybir
from contextlib import ExitStack


def adaln_moe_two_layers(
    nc: bass.Bass,
    x: bass.AP,
    subj: bass.AP,
    lang: bass.AP,
    c0_w: bass.AP,
    c0_b: bass.AP,
    f0_router: bass.AP,
    f0_gate_up: bass.AP,
    f0_down: bass.AP,
    f0_sh_gate: bass.AP,
    f0_sh_up: bass.AP,
    f0_sh_down: bass.AP,
    c1_w1: bass.AP,
    c1_b1: bass.AP,
    c1_w2: bass.AP,
    c1_b2: bass.AP,
    c1_gamma: bass.AP,
    c1_beta: bass.AP,
    f1_router: bass.AP,
    f1_w1: bass.AP,
    f1_b1: bass.AP,
    f1_w2: bass.AP,
    f1_b2: bass.AP,
    f1_sh_w1: bass.AP,
    f1_sh_b1: bass.AP,
    f1_sh_w2: bass.AP,
    f1_sh_b2: bass.AP,
    out: bass.AP,
):
    fp32 = mybir.dt.float32
    bf16 = mybir.dt.bfloat16
    i32 = mybir.dt.int32
    fp32r = mybir.dt.float32r
    ALU = mybir.AluOpType
    ACT = mybir.ActivationFunctionType
    AX = mybir.AxisListType
    ds = bass.ds

    P = 128
    T, H = x.shape
    B = subj.shape[1]
    S = T // B
    NSUB = c0_w.shape[0]
    E0, _, F0x2 = f0_gate_up.shape
    F0 = F0x2 // 2
    C0 = F0 // P
    NLANG = c1_b2.shape[0]
    A = c1_w1.shape[1] // NLANG
    E1, _, F1 = f1_w1.shape
    C1 = F1 // P
    TOP_K = 2
    CAP = min(max(4, -(-TOP_K * 5 * T // (4 * E1))), T)
    SHARED_SCALE = 0.1
    LN_EPS = 1e-5
    BIG = 2.0 ** 120
    TINY = 1.1920929e-07

    NT = T // P
    G = 4
    NG = NT // G
    GB = G * P // S
    GP = G * P
    QB = P // S
    NBLK = NT + E0 - 1
    NBLKP = -(-NBLK // 4) * 4
    U = 2
    UP = U * P
    GPE = CAP // UP
    NQ = E1 * GPE
    ROW = H + 1
    FAR = 65536
    DROP = 16384
    HID = NLANG * A
    NCH = -(-HID // P)
    TAIL = HID - (NCH - 1) * P
    LASTK = TAIL + NLANG
    KROWS = [P] * (NCH - 1) + [LASTK]
    assert CAP % UP == 0 and TAIL % 32 == 0 and NG % 2 == 0 and E1 % 2 == 0 and GPE % 2 == 1

    rows0 = nc.dram_tensor("rows0", (NBLKP * P, ROW), fp32).ap()
    back0 = nc.dram_tensor("back0", (T, H), fp32).ap()
    rows1 = nc.dram_tensor("rows1", (E1 * CAP, ROW), fp32).ap()
    back1 = nc.dram_tensor("back1", (TOP_K * T, H), fp32).ap()

    x_g = x.rearrange("(g i p) h -> g p i h", p=P, i=G)
    out_g = out.rearrange("(g i p) h -> g p i h", p=P, i=G)
    back0_g = back0.rearrange("(g i p) h -> g p i h", p=P, i=G)
    back1_g = back1.rearrange("(k g i p) h -> k g p i h", p=P, i=G, k=TOP_K)
    rows0_b = rows0.rearrange("(j p) r -> j p r", p=P)
    rows1_q = rows1.rearrange("(q u p) r -> q p u r", p=P, u=U)

    ctx = ExitStack()
    with ctx:
        def sb(name, shape, dt=fp32):
            return ctx.enter_context(nc.sbuf_tensor(name, shape, dt))

        def sem(name):
            return ctx.enter_context(nc.semaphore(name))

        acc = sb("acc", [P, NT, H])
        featT = sb("featT", [P, T])
        disp = sb("disp", [P, NT, ROW])
        with ExitStack() as layer0:
            def sb0(name, shape, dt=fp32):
                return layer0.enter_context(nc.sbuf_tensor(name, shape, dt))

            c0w = sb0("c0w", [P, NSUB * H])
            w_dn = sb0("w_dn", [P, E0 * C0 * H])
            w_guh = sb0("w_guh", [P, E0 * F0x2], fp32r)
            w_gul = sb0("w_gul", [P, E0 * F0x2], fp32r)
        back = [[sb(f"back{k}_{g}", [P, G, H]) for g in range(NG)] for k in range(TOP_K)]
        y0g = [sb(f"y0g{k}", [P, G, H]) for k in range(4)]
        nrm = [sb(f"nrm{k}", [P, G, H]) for k in range(2)]
        w1r = [sb(f"w1r{k}", [P, F1]) for k in range(2)]
        w1h = [sb(f"w1h{k}", [P, F1], fp32r) for k in range(2)]
        w1l = [sb(f"w1l{k}", [P, F1], fp32r) for k in range(2)]
        w2r = [sb(f"w2r{k}", [P, C1, H]) for k in range(2)]
        NX = GPE
        grp_x = [sb(f"grp_x{k}", [P, U, ROW]) for k in range(NX)]
        grp_y = [sb(f"grp_y{k}", [P, U, H]) for k in range(2)]
        xh = [sb(f"xh{k}", [P, GP], fp32r) for k in range(2)]
        xl = [sb(f"xl{k}", [P, GP], fp32r) for k in range(2)]
        a_w1h = sb("a_w1h", [P, NCH * P], fp32r)
        a_w1l = sb("a_w1l", [P, NCH * P], fp32r)
        sw1h = sb("sw1h", [P, F1], fp32r)
        sw1l = sb("sw1l", [P, F1], fp32r)
        used = (2 * NG + 4 + 2) * GP + 10 * F1 + 2 * NX * ROW + 4 * H + 4 * GP + 2 * NCH * P
        sb("spare", [P, NSUB * H + E0 * (C0 * H + 2 * F0x2) - used])
        shg = sb("shg", [P, F0])
        shu = sb("shu", [P, F0])
        shd = sb("shd", [P, C0, H])
        rt0 = sb("rt0", [P, E0])
        rt1 = sb("rt1", [P, E1])
        c0bs = sb("c0bs", [NSUB, H])
        gam = sb("gam", [NLANG, H])
        bet = sb("bet", [NLANG, H])
        a_w1 = sb("a_w1", [P, NCH * P])
        a_w2 = sb("a_w2", [P, NCH, H])
        a_b1 = sb("a_b1", [P, NCH])
        sw1 = sb("sw1", [P, F1])
        sw2 = sb("sw2", [P, C1, H])
        sb1 = sb("sb1", [P, C1])
        sb2 = sb("sb2", [P, H])
        xT = [sb(f"xT{k}", [P, GP]) for k in range(2)]
        act = [sb(f"act{k}", [P, C1, GP]) for k in range(2)]
        sil = sb("sil", [P, C0, GP])
        b1r = [sb(f"b1r{k}", [P, C1]) for k in range(2)]
        b2r = [sb(f"b2r{k}", [P, H]) for k in range(2)]
        blk_x = [sb(f"blk_x{s}", [P, ROW]) for s in range(4)]
        act0, act1 = (a[:, C0:C1, :].rearrange("p c t -> p (c t)") for a in act)
        assert 4 * H + 2 * F0 <= (C1 - C0) * GP
        blk_y = [act0[:, s * H:(s + 1) * H] for s in range(4)]
        blk_i = [sb(f"blk_i{s}", [P, 1], i32) for s in range(8)]
        blk_xh = [sb(f"blk_xh{k}", [P, P], fp32r) for k in range(2)]
        blk_xl = [sb(f"blk_xl{k}", [P, P], fp32r) for k in range(2)]
        blk_s = [act0[:, 4 * H + k * F0:4 * H + (k + 1) * F0] for k in range(2)]
        blk_a = [act1[:, k * F0:(k + 1) * F0] for k in range(2)]
        blk_aT = [act1[:, (2 + k) * F0:(3 + k) * F0] for k in range(2)]
        grp_i = [sb(f"grp_i{k}", [P, U], i32) for k in range(NX)]
        zrow = sb("zrow", [P, 1032])
        ident = sb("ident", [P, P])
        tri = sb("tri", [P, P], bf16)
        ones_b = sb("ones_b", [P, P], bf16)
        codes = sb("codes", [P, NT])
        subjI = sb("subjI", [NSUB, B], i32)
        langI = sb("langI", [NLANG, B], i32)
        w0off = sb("w0off", [1, B], i32)
        rowI = sb("rowI", [P, 1], i32)
        rowF = sb("rowF", [P, 1])
        colL = sb("colL", [NLANG, NCH * P])
        other = sb("other", [NLANG, NCH * P], bf16)
        hot0 = sb("hot0", [NSUB, B])
        hot1 = sb("hot1", [NLANG, B])
        hot1b = sb("hot1b", [NLANG, B], bf16)
        c0bT = sb("c0bT", [P, B])
        gamT = sb("gamT", [P, B])
        betT = sb("betT", [P, B])
        RT = NT // 4
        assert RT % G == 0
        W = NT * E0
        assert W == NT * TOP_K * E1 and W == 512
        lg = sb("lg", [P, W])
        t1 = sb("t1", [P, W])
        t2 = sb("t2", [P, W])
        t3 = sb("t3", [P, W])
        condS = t3[:, :].rearrange("p (i h) -> p i h", h=H)
        mask = sb("mask", [P, W], bf16)
        seen = sb("seen", [P, W], bf16)
        before = sb("before", [P, E1], bf16)
        keep = sb("keep", [P, W])
        rst = sb("rst", [P, W])
        rst1 = sb("rst1", [P, E1 * RT])
        revE = sb("revE", [P, E0])
        baseE = sb("baseE", [P, E1])
        m1 = sb("m1", [P, NT])
        m3 = sb("m3", [P, NT])
        wk = sb("wk", [P, TOP_K, NT])
        score = sb("score", [P, NT])
        slotF = sb("slotF", [P, TOP_K, NT])
        slot = sb("slot", [P, TOP_K, NT], i32)
        padI = sb("padI", [P, E0], i32)
        padF = sb("padF", [P, E0])
        endE = sb("endE", [P, E0])
        ones_f = sb("ones_f", [P, E0])
        jrow = sb("jrow", [1, NBLKP])
        cmpj = act0[0:1, 0:NBLKP * (E0 - 1)].rearrange("o (j e) -> o j e", e=E0 - 1)
        bexp = sb("bexp", [1, NBLKP])
        w_at = sb("w_at", [1, NBLKP + 2, 2], i32)
        cnt1 = sb("cnt1", [P, E1])
        bn6 = sb("bn6", [P, G, 6])
        mv = sb("mv", [P, G, 2])
        rstd = [sb(f"rstd{k}", [P, G]) for k in range(2)]
        nmr = [sb(f"nmr{k}", [P, G]) for k in range(2)]
        epsc = sb("epsc", [P, 1])

        PS = [ctx.enter_context(nc.psum_tensor(f"PS{i}", [P, 512], fp32)) for i in range(8)]

        x_ld = [sem(f"x_ld{g}") for g in range(NG)]
        ld_small = sem("ld_small")
        ld_c0w = sem("ld_c0w")
        ld_tab = sem("ld_tab")
        ld_sh0 = sem("ld_sh0")
        g_ld = [sem(f"g_ld{k}") for k in range(2)]
        g_hi = sem("g_hi")
        g_lo = sem("g_lo")
        e_xl = sem("e_xl")
        ld_dn = sem("ld_dn")
        ld_l1 = sem("ld_l1")
        zero0 = sem("zero0")
        zero1 = sem("zero1")
        poolk = sem("poolk")
        dch = sem("dch")
        dve_ready = sem("dve_ready")
        off_ready = sem("off_ready")
        pe_tab = sem("pe_tab")
        tab_done = sem("tab_done")
        pe_xt = sem("pe_xt")
        xT_done = sem("xT_done")
        pe_c = sem("pe_c")
        condA = sem("condA")
        condD = sem("condD")
        pe_ht = sem("pe_ht")
        hT_done = sem("hT_done")
        pe_l = sem("pe_l")
        lg_done = sem("lg_done")
        pe_tok = sem("pe_tok")
        tok_done = sem("tok_done")
        mx0 = sem("mx0")
        sg0 = sem("sg0")
        mk0 = sem("mk0")
        pe_rank0 = sem("pe_rank0")
        slots0 = sem("slots0")
        blocks0 = sem("blocks0")
        scaled = sem("scaled")
        sc0 = sem("sc0")
        pe_gu = sem("pe_gu")
        sil_done = sem("sil_done")
        act_done = sem("act_done")
        pe_dn = sem("pe_dn")
        acc0 = sem("acc0")
        bx_ld = [sem(f"bx_ld{s}") for s in range(4)]
        by_st = [sem(f"by_st{s}") for s in range(4)]
        e_xt = sem("e_xt")
        e_xc = sem("e_xc")
        e_gu = sem("e_gu")
        e_sl = sem("e_sl")
        e_ac = sem("e_ac")
        e_ta = sem("e_ta")
        e_at = sem("e_at")
        e_dn = sem("e_dn")
        e_oc = sem("e_oc")
        e_ix = sem("e_ix")
        y0_ld = [sem(f"y0_ld{k}") for k in range(4)]
        x1_done = sem("x1_done")
        b_xt = sem("b_xt")
        b_xc = sem("b_xc")
        b_xl = sem("b_xl")
        b_ws = sem("b_ws")
        b_w1 = sem("b_w1")
        b_rl = sem("b_rl")
        b_w2 = sem("b_w2")
        b_var = sem("b_var")
        b_std = sem("b_std")
        b_nb = sem("b_nb")
        b_nm = sem("b_nm")
        b_nt = sem("b_nt")
        b_xn = sem("b_xn")
        b_lg = sem("b_lg")
        b_lc = sem("b_lc")
        b_rk = sem("b_rk")
        b_bt = sem("b_bt")
        b_tk = sem("b_tk")
        ex_in = sem("ex_in")
        ex_out = sem("ex_out")
        mk1 = sem("mk1")
        pe_rank1 = sem("pe_rank1")
        slots1 = sem("slots1")
        codes0 = sem("codes0")
        codes1 = sem("codes1")
        sc1 = [[sem(f"sc1_{k}{h}") for h in range(2)] for k in range(2)]
        s_sp = sem("s_sp")
        s_gu = sem("s_gu")
        s_sl = sem("s_sl")
        s_dn = sem("s_dn")
        s_ac = sem("s_ac")
        gx_ld = [sem(f"gx_ld{k}") for k in range(NX)]
        gy_st = [sem(f"gy_st{k}") for k in range(2)]
        w_ld = [sem(f"w_ld{k}") for k in range(2)]
        wb_ld = [sem(f"wb_ld{k}") for k in range(2)]
        q_xt = sem("q_xt")
        q_xc = sem("q_xc")
        q_xl = sem("q_xl")
        w_sp = sem("w_sp")
        q_gu = sem("q_gu")
        q_sl = sem("q_sl")
        q_dn = sem("q_dn")
        q_oc = sem("q_oc")
        q_ix = sem("q_ix")
        fy_ld = [sem(f"fy_ld{g}") for g in range(NG)]
        f_sc = sem("f_sc")
        f_ac = sem("f_ac")
        o_st = sem("o_st")
        pool_turn = sem("pool_turn")

        block = ctx.enter_context(nc.Block())
        mm = nc.tensor.matmul

        def at(ap, i):
            return ap[i] if isinstance(i, int) else ap[ds(i, 1)].squeeze(0)

        def residual(ops, eng, n):
            eng.wait_ge(y0_ld[n % 4], 16 * (n // 4 + 1))
            a = acc[:, n * G:(n + 1) * G, :]
            ops.tensor_tensor(a, a, y0g[n % 4][:, :, :], ALU.add).then_inc(x1_done, 1)

        def split_rounds(n):
            done = [min(m + max(m + 1 - NG // 2, 0), E0 // 2) if m > 0 else 0 for m in (n - 1, n)]
            return range(*done)

        assert split_rounds(NG - 1).stop == E0 // 2

        def tile(buf, i):
            return buf[:, i * P:(i + 1) * P]

        @block.sync
        def _(sp):
            sp.dma_start(acc[:, 0:G, :], x_g[0]).then_inc(x_ld[0], 16)
            sp.dma_start(w0off[:, :], subj).then_inc(ld_small, 16)
            sp.dma_start(acc[:, G:2 * G, :], x_g[1]).then_inc(x_ld[1], 16)
            sp.dma_start(subjI[:, :], subj.partition_broadcast(NSUB)).then_inc(ld_tab, 16)
            sp.dma_start(langI[:, :], lang.partition_broadcast(NLANG)).then_inc(ld_tab, 16)
            for dst, src in ((c0bs[:, :], c0_b), (gam[:, :], c1_gamma), (bet[:, :], c1_beta),
                             (rt0[:, :], f0_router), (rt1[:, :], f1_router)):
                sp.dma_start(dst, src).then_inc(ld_tab, 16)
            for g in range(2, NG):
                sp.dma_start(acc[:, g * G:(g + 1) * G, :], x_g[g]).then_inc(x_ld[g], 16)
            sp.dma_start(shg[:, :], f0_sh_gate).then_inc(ld_sh0, 16)
            sp.dma_start(shu[:, :], f0_sh_up).then_inc(ld_sh0, 16)
            sp.dma_start(shd[:, :, :], f0_sh_down.rearrange("(c p) h -> p c h", p=P)).then_inc(ld_sh0, 16)
            sp.wait_ge(poolk, 3)
            zw = ROW * 4
            for r in range(0, NBLKP * P, P * 4):
                sp.dma_start(rows0[r:r + P * 4, :].rearrange("(p a) r -> p (a r)", p=P),
                             zrow[:, 0:zw]).then_inc(zero0, 16)
            sp.dma_start(w_dn[:, :].rearrange("p (e c h) -> p e c h", e=E0, c=C0),
                         f0_down.rearrange("e (c p) h -> p e c h", p=P)).then_inc(ld_dn, 16)
            for r in range(0, E1 * CAP, P * 4):
                sp.dma_start(rows1[r:r + P * 4, :].rearrange("(p a) r -> p (a r)", p=P),
                             zrow[:, 0:zw]).then_inc(zero1, 16)
            for r in range(0, TOP_K * T, P * 8):
                sp.dma_start(back1[r:r + P * 8, :].rearrange("(p a) h -> p (a h)", p=P),
                             zrow[:, 0:8 * H]).then_inc(zero1, 16)
            sp.wait_ge(dve_ready, 1)
            sp.dma_start(a_w1[:, 0:HID], c1_w1).then_inc(ld_l1, 16)
            for c in range(NCH - 1):
                sp.dma_start(a_w2[:, c, :], c1_w2[c * P:(c + 1) * P, :]).then_inc(ld_l1, 16)
                sp.dma_start(a_b1[:, c:c + 1], c1_b1[c * P:(c + 1) * P, :]).then_inc(ld_l1, 16)
            c = NCH - 1
            sp.dma_start(a_w2[0:TAIL, c, :], c1_w2[c * P:HID, :]).then_inc(ld_l1, 16)
            sp.dma_start(a_w2[TAIL:LASTK, c, :], c1_b2).then_inc(ld_l1, 16)
            sp.dma_start(a_b1[0:TAIL, c:c + 1], c1_b1[c * P:HID, :]).then_inc(ld_l1, 16)
            sp.dma_start(sw1[:, :], f1_sh_w1).then_inc(ld_l1, 16)
            sp.dma_start(sw2[:, :, :], f1_sh_w2.rearrange("(c p) h -> p c h", p=P)).then_inc(ld_l1, 16)
            sp.dma_start(sb1[:, :], f1_sh_b1).then_inc(ld_l1, 16)
            sp.dma_start(sb2[:, :], f1_sh_b2.partition_broadcast(P)).then_inc(ld_l1, 16)

            sp.wait_ge(pe_c, QB * NG)
            for r in range(E0 // 2):
                if r >= 2:
                    sp.wait_ge(g_lo, 2 * (r - 1))
                sp.dma_start(c0w[:, (r % 2) * 2 * F0x2:(r % 2 + 1) * 2 * F0x2].rearrange("p (e f) -> p e f", e=2),
                             f0_gate_up[2 * r:2 * r + 2].rearrange("e p f -> p e f")).then_inc(g_ld[r % 2], 16)

            def load_block(j, s, first=False):
                if not first:
                    sp.wait_ge(e_xt, j - 3)
                    sp.wait_ge(e_ix, j - 3)
                sp.dma_start(blk_x[s][:, :], at(rows0_b, j)).then_inc(bx_ld[s], 16)

            sp.wait_ge(sc0, 16 * NT)
            for j in range(4):
                load_block(j, j, first=True)
            with sp.Fori(0, NBLKP // 4 - 1) as it:
                for s in range(4):
                    load_block(it * 4 + (4 + s), s)
            for s in range(4):
                sp.wait_ge(by_st[s], 16 * (NBLKP // 4))
            for g in range(NG):
                if g >= 4:
                    sp.wait_ge(x1_done, g - 3)
                sp.dma_start(y0g[g % 4][:, :, :], back0_g[g]).then_inc(y0_ld[g % 4], 16)

            def load_weights(e, k, split=None):
                if split is not None:
                    sp.wait_ge(w_sp, split)
                sp.dma_start(w1r[k][:, :], at(f1_w1, e)).then_inc(w_ld[k], 16)

            def load_rest(e, k, free_at=None):
                if free_at is not None:
                    sp.wait_ge(q_oc, free_at)
                sp.dma_start(w2r[k][:, :, :], at(f1_w2, e).rearrange("(c p) h -> p c h", p=P)).then_inc(wb_ld[k], 16)
                sp.dma_start(b1r[k][:, :], at(f1_b1, e)).then_inc(wb_ld[k], 16)
                sp.dma_start(b2r[k][:, :], f1_b2[ds(e, 1), :].partition_broadcast(P)).then_inc(wb_ld[k], 16)

            def load_group(m, k, first=False):
                if not first:
                    sp.wait_ge(q_xt, m - (NX - 1))
                    sp.wait_ge(q_ix, m - (NX - 1))
                sp.dma_start(grp_x[k][:, :, :], at(rows1_q, m)).then_inc(gx_ld[k], 16)

            for e in range(2):
                load_weights(e, e)
                load_rest(e, e)
            for k in range(TOP_K):
                for h in range(2):
                    sp.wait_ge(sc1[k][h], 16 * (NT // 2))
            for m in range(NX):
                load_group(m, m, first=True)
            with sp.Fori(0, E1 // 2 - 1) as it:
                for u in range(2 * GPE):
                    load_group(it * (2 * GPE) + (NX + u), u % NX)
                    if u == 0:
                        load_weights(it * 2 + 2, 0, it * 4 + 2)
                    if u == GPE:
                        load_rest(it * 2 + 2, 0, it * (2 * GPE) + GPE)
                        load_weights(it * 2 + 3, 1, it * 4 + 4)
                    if u == 2 * GPE - 1:
                        load_rest(it * 2 + 3, 1, it * (2 * GPE) + 2 * GPE)
            for m in range(NX + (E1 // 2 - 1) * 2 * GPE, NQ):
                load_group(m, m % NX)

            for k in range(2):
                sp.wait_ge(gy_st[k], 16 * U * (NQ // 2))
            for g in range(NG):
                for k in range(TOP_K):
                    sp.dma_start(back[k][g][:, :, :], back1_g[k, g]).then_inc(fy_ld[g], 16)
            for g in range(NG):
                sp.wait_ge(f_ac, g + 1)
                sp.dma_start(out_g[g], acc[:, g * G:(g + 1) * G, :]).then_inc(o_st, 16)
            sp.wait_ge(o_st, 16 * NG)

        @block.gpsimd
        def _(pool):
            gp = nc.gpsimd
            gp.memset(ident[:, :], 0.0).then_inc(poolk, 1)
            pool.wait_ge(poolk, 1)
            gp.affine_select(out=ident[:, :], in_=ident[:, :], compare_op=ALU.not_equal, fill=1.0,
                             base=0, pattern=[[-1, P]], channel_multiplier=1).then_inc(poolk, 1)
            gp.memset(zrow[:, :], 0.0).then_inc(poolk, 1)
            gp.memset(tri[:, :], -1.0).then_inc(poolk, 1)
            gp.memset(ones_b[:, :], 1.0).then_inc(poolk, 1)
            gp.memset(rst[:, :], 1.0).then_inc(poolk, 1)
            gp.memset(rst1[:, :], 1.0).then_inc(poolk, 1)
            pool.wait_ge(poolk, 7)
            gp.affine_select(out=tri[:, :], in_=tri[:, :], compare_op=ALU.is_ge, fill=0.0,
                             base=0, pattern=[[-1, P]], channel_multiplier=1).then_inc(poolk, 1)
            gp.memset(rst[:, :].rearrange("p (e i) -> p e i", i=NT)[:, :, 0:1], 0.0).then_inc(poolk, 1)
            gp.memset(rst1[:, :].rearrange("p (e i) -> p e i", i=RT)[:, :, 0:1], 0.0).then_inc(poolk, 1)
            gp.iota(rowI[:, :], pattern=[[1, 1]], base=0, channel_multiplier=1).then_inc(poolk, 1)
            gp.iota(codes[:, :], pattern=[[-P, NT]], base=FAR, channel_multiplier=-1,
                    allow_small_or_imprecise_dtypes=True).then_inc(poolk, 1)
            gp.iota(revE[:, :], pattern=[[-1, E0]], base=E0, channel_multiplier=0,
                    allow_small_or_imprecise_dtypes=True).then_inc(poolk, 1)
            gp.iota(baseE[:, :], pattern=[[CAP, E1]], base=-DROP, channel_multiplier=0,
                    allow_small_or_imprecise_dtypes=True).then_inc(poolk, 1)
            gp.iota(jrow[:, :], pattern=[[P, NBLKP]], base=0, channel_multiplier=0,
                    allow_small_or_imprecise_dtypes=True).then_inc(poolk, 1)
            gp.iota(colL[:, 0:HID], pattern=[[1, NLANG], [0, A]], base=0, channel_multiplier=0,
                    allow_small_or_imprecise_dtypes=True).then_inc(poolk, 1)
            gp.iota(colL[:, HID:NCH * P], pattern=[[1, NCH * P - HID]], base=0, channel_multiplier=0,
                    allow_small_or_imprecise_dtypes=True).then_inc(poolk, 1)
            gp.memset(ones_f[:, :], 1.0).then_inc(poolk, 1)
            gp.memset(epsc[:, :], LN_EPS).then_inc(poolk, 1)
            pool.wait_ge(poolk, 19)
            gp.tensor_copy(disp[:, :, H:ROW], codes[:, :].unsqueeze(2)).then_inc(codes0, 1)

            pool.wait_ge(zero0, 16 * (NBLKP // 4))
            pool.wait_ge(codes0, 1)
            for t in range(NT):
                if t % (NT // 2) == 0:
                    pool.wait_ge(slots0, t // (NT // 2) + 1)
                if t % G == 0:
                    pool.wait_ge(scaled, t + G)
                gp.indirect_dma_start(rows0, bass.IndirectOffsetOnAxis(ap=slot[:, 0, t:t + 1], axis=0),
                                      disp[:, t, :], None, bounds_check=NBLKP * P - 1,
                                      oob_is_err=False).then_inc(sc0, 16)

            last_token = pool.to_reg(T - 1)
            with pool.Fori(0, NBLKP // 8) as it:
                for c in range(8):
                    s = c % 4
                    pool.wait_ge(e_oc, it * 8 + (c + 1))
                    pool.sem_inc(pool_turn)
                    gp.indirect_dma_start(back0, bass.IndirectOffsetOnAxis(ap=blk_i[c][:, 0:1], axis=0),
                                          blk_y[s][:, :], None, bounds_check=last_token,
                                          oob_is_err=False).then_inc(by_st[s], 16)

            pool.wait_ge(acc0, NG)
            pool.wait_ge(x1_done, 2)
            for n in range(2, NG):
                residual(gp, pool, n)

            pool.wait_ge(zero1, 16 * (E1 * CAP // (4 * P) + TOP_K * T // (8 * P)))
            HT = NT // 2
            for k in range(TOP_K):
                for t in range(NT):
                    if k == 0 and t % RT == 0:
                        pool.wait_ge(slots1, t // RT + 1)
                        pool.wait_ge(b_tk, (t + RT) // G)
                    if k == 1 and t == 0:
                        pool.wait_ge(slots1, NT // RT + 1)
                    gp.indirect_dma_start(rows1, bass.IndirectOffsetOnAxis(ap=slot[:, k, t:t + 1], axis=0),
                                          disp[:, t, :], None, bounds_check=E1 * CAP - 1,
                                          oob_is_err=False).then_inc(sc1[k][t // HT], 16)
                    if (k, t) in ((0, NT - 8), (1, HT - 8)):
                        h = k
                        pool.wait_ge(sc1[0][h], 16 * HT)
                        half = slice(h * HT, (h + 1) * HT)
                        gp.tensor_scalar(disp[:, half, H:ROW], codes[:, half].unsqueeze(2), float(-T), None,
                                         ALU.add).then_inc(codes1, 1)
                        pool.wait_ge(codes1, h + 1)
            last_row = pool.to_reg(TOP_K * T - 1)
            with pool.Fori(0, E1 // 2) as it:
                for v in range(2 * GPE):
                    k = v % 2
                    pool.wait_ge(q_oc, it * (2 * GPE) + (v + 1))
                    pool.sem_inc(pool_turn)
                    for u in range(U):
                        gp.indirect_dma_start(back1, bass.IndirectOffsetOnAxis(ap=grp_i[v % NX][:, u:u + 1], axis=0),
                                              grp_y[k][:, u, :], None, bounds_check=last_row,
                                              oob_is_err=False).then_inc(gy_st[k], 16)

        @block.scalar
        def _(eng):
            sc = nc.scalar

            def cp(dst, src):
                return sc.activation(dst, src, ACT.Copy)

            eng.dma_start(c0w[:, :].rearrange("p (s h) -> p s h", s=NSUB),
                          c0_w.rearrange("s p h -> p s h")).then_inc(ld_c0w, 16)
            eng.preload_act_table(ACT.Sigmoid)
            def copy_x(n):
                eng.wait_ge(pe_xt, n + 1)
                cp(xT[n % 2][:, :], PS[0][:, :]).then_inc(xT_done, 1)

            copy_x(0)
            for n in range(NG + 1):
                if n < NG:
                    if n + 1 < NG:
                        copy_x(n + 1)
                    for b in range(2):
                        eng.wait_ge(pe_c, QB * n + b + 1)
                        cp(condS[b * S:(b + 1) * S, :, :],
                           PS[1 + b][0:S, :].rearrange("p (i h) -> p i h", h=H)).then_inc(condA, 1)
                if n >= 1:
                    eng.wait_ge(pe_tok, n)
                    cp(disp[:, (n - 1) * G:n * G, 0:H],
                       PS[7][:, :].rearrange("p (i h) -> p i h", h=H)).then_inc(tok_done, 1)
            eng.wait_ge(mx0, 1)
            sc.activation(score[:, :], m1[:, :], ACT.Sigmoid).then_inc(sg0, 1)
            eng.preload_act_table(ACT.Silu)
            eng.wait_ge(sg0, 1)
            eng.wait_ge(tok_done, NG)
            for n in range(NG):
                for c in range(C0):
                    eng.wait_ge(pe_gu, 2 * C0 * n + 2 * c + 1)
                    if n >= 1:
                        eng.wait_ge(act_done, C0 * (n - 1) + c + 1)
                    sc.activation(sil[:, c, :], PS[2 * c][:, :], ACT.Silu).then_inc(sil_done, 1)
                for t in range(n * 2 * G, min((n + 1) * 2 * G, NT)):
                    sc.activation(disp[:, t, 0:H], disp[:, t, 0:H], ACT.Copy,
                                  scale=score[:, t:t + 1]).then_inc(scaled, 1)

                for r in split_rounds(n):
                    eng.wait_ge(g_ld[r % 2], 16 * (r // 2 + 1))
                    for e in (2 * r, 2 * r + 1):
                        cp(w_guh[:, e * F0x2:(e + 1) * F0x2],
                           c0w[:, e % 4 * F0x2:(e % 4 + 1) * F0x2]).then_inc(g_hi, 1)

            def copy_xT(j, k):
                eng.wait_ge(e_xt, j + 1)
                cp(blk_xh[k][:, :], PS[5 + k][:, 0:P]).then_inc(e_xc, 1)

            def silu(j, k):
                eng.wait_ge(e_gu, j + 1)
                sc.activation(blk_s[k][:, :], PS[k][:, 0:F0], ACT.Silu).then_inc(e_sl, 1)

            def copy_aT(j, k):
                eng.wait_ge(e_ta, j + 1)
                cp(blk_aT[k][:, :], PS[2 + k][:, 0:F0]).then_inc(e_at, 1)

            def act_stage(j, k, first=False, last=False):
                if not last:
                    copy_xT(j + 1, 1 - k)
                silu(j, k)
                if not first:
                    copy_aT(j - 1, 1 - k)

            copy_xT(0, 0)
            for j in range(4):
                act_stage(j, j % 2, first=j == 0)
            with eng.Fori(0, NBLKP // 4 - 2) as it:
                for s in range(4):
                    act_stage(it * 4 + (4 + s), s % 2)
            for j in range(NBLKP - 4, NBLKP):
                act_stage(j, j % 2, last=j == NBLKP - 1)
            copy_aT(NBLKP - 1, (NBLKP - 1) % 2)

            eng.wait_ge(ld_l1, 16 * (2 * (NCH - 1) + 8))
            def copy_x1(n):
                eng.wait_ge(b_xt, n + 1)
                cp(xh[n % 2][:, :], PS[0][:, :]).then_inc(b_xc, 1)

            def copy_rows(m):
                eng.wait_ge(b_bt, m + 1)
                cp(disp[:, m * G:(m + 1) * G, 0:H],
                   PS[6][:, :].rearrange("p (i h) -> p i h", h=H)).then_inc(b_tk, 1)

            def shared1_silu(n):
                for c in range(C1):
                    eng.wait_ge(s_gu, C1 * n + c + 1)
                    eng.wait_ge(b_w2, NG)
                    if n >= 2:
                        eng.wait_ge(s_dn, n - 1)
                    sc.activation(act[n % 2][:, c, :], PS[c][:, :], ACT.Silu,
                                  bias=sb1[:, c:c + 1]).then_inc(s_sl, 1)

            copy_x1(0)
            for n in range(NG + 2):
                if n + 1 < NG:
                    copy_x1(n + 1)
                if n < NG:
                    for c in range(NCH):
                        eng.wait_ge(b_w1, NCH * n + c + 1)
                        if n >= 2:
                            eng.wait_ge(b_w2, n - 1)
                        sc.activation(act[n % 2][0:KROWS[c], c, :], PS[1 + c][0:KROWS[c], :], ACT.Relu,
                                      bias=a_b1[0:KROWS[c], c:c + 1]).then_inc(b_rl, 1)
                if 1 <= n < NG + 1:
                    k = (n - 1) % 2
                    eng.wait_ge(b_var, n)
                    sc.activation(rstd[k][:, :], mv[:, :, 1], ACT.Sqrt, bias=epsc[:, :]).then_inc(b_std, 1)
                if n == NG + 1:
                    shared1_silu(0)
                if 3 <= n:
                    copy_rows(n - 3)
                if 1 <= n < NG + 1:
                    eng.wait_ge(b_nb, n)
                    for i in range(G):
                        ins = sc.activation(nrm[k][:, i, :], nrm[k][:, i, :], ACT.Identity,
                                            scale=rstd[k][:, i:i + 1], bias=nmr[k][:, i:i + 1])
                    ins.then_inc(b_nm, 1)
                if n == NG:
                    eng.preload_act_table(ACT.Silu)
            copy_rows(NG - 1)
            eng.wait_ge(ex_in, 1)
            sc.activation(t1[:, 0:NT * E1], t1[:, 0:NT * E1], ACT.Exp).then_inc(ex_out, 1)
            eng.preload_act_table(ACT.Silu)
            for n in range(1, NG):
                shared1_silu(n)

            def q_copy(q, k):
                eng.wait_ge(q_xt, q + 1)
                cp(xh[k][:, 0:UP], PS[0][:, 0:UP]).then_inc(q_xc, 1)

            def q_silu(q, k, e, biases=None):
                if biases is not None:
                    eng.wait_ge(wb_ld[e], biases)
                for c in range(C1):
                    if c % 2 == 0:
                        eng.wait_ge(q_gu, q * (C1 // 2) + (c // 2 + 1))
                    sc.activation(act[k][:, c, 0:UP], PS[1 + k * (C1 // 2) + c // 2][:, (c % 2) * UP:(c % 2 + 1) * UP],
                                  ACT.Silu, bias=b1r[e][:, c:c + 1]).then_inc(q_sl, 1)

            def q_stage(q, b, it48=0, last=False):
                if not last:
                    q_copy(q + 1, (b + 1) % 2)
                q_silu(q, b % 2, b // GPE % 2,
                       it48 + (b // (2 * GPE) + 1) * 48 if b % GPE == 0 else None)

            q_copy(0, 0)
            q_stage(0, 0)
            with eng.Fori(0, E1 // 2 - 1) as it:
                for u in range(2 * GPE):
                    q_stage(it * (2 * GPE) + (1 + u), 1 + u, it * 48)
            for q in range(1 + (E1 // 2 - 1) * 2 * GPE, NQ):
                q_stage(q, q, last=q == NQ - 1)

            for g in range(NG):
                eng.wait_ge(fy_ld[g], 16 * TOP_K)
                for i in range(G):
                    ins = sc.activation(back[1][g][:, i, :], back[1][g][:, i, :], ACT.Copy,
                                        scale=wk[:, 1, g * G + i:g * G + i + 1])
                ins.then_inc(f_sc, 1)

        @block.vector
        def _(dve):
            v = nc.vector
            chain = [0]

            def link(ins):
                chain[0] += 1
                ins.then_inc(dch, 1)
                dve.wait_ge(dch, chain[0])

            def bc(ap, shape):
                return ap.to_broadcast(shape)

            v.memset(a_w1[:, HID:NCH * P], 0.0)
            link(v.memset(w_at[:, :, :], 0))
            v.memset(a_b1[TAIL:LASTK, NCH - 1:NCH], 1.0).then_inc(dve_ready, 1)
            dve.wait_ge(ld_small, 16)
            v.tensor_scalar(w0off[:, :], w0off[:, :], float(H), None, ALU.mult).then_inc(off_ready, 1)
            dve.wait_ge(poolk, 19)
            link(v.tensor_copy(rowF[:, :], rowI[:, :]))
            link(v.tensor_scalar(other[:, :], colL[:, :], rowF[0:NLANG, :], -BIG, ALU.not_equal, ALU.mult))
            dve.wait_ge(ld_tab, 16 * 7)
            link(v.tensor_scalar(hot0[:, :], subjI[:, :], rowF[0:NSUB, :], None, ALU.is_equal))
            link(v.tensor_scalar(hot1[:, :], langI[:, :], rowF[0:NLANG, :], None, ALU.is_equal))
            link(v.tensor_copy(hot1b[:, :], hot1[:, :]))
            v.engine_nop().then_inc(dve_ready, 1)

            def first_max(vals, ne, keys, out, i0, n):
                shape = [P, n, ne]
                w3 = lambda a: a[:, i0 * ne:(i0 + n) * ne].rearrange("p (i e) -> p i e", e=ne)
                top, best = m1[:, i0:i0 + n], m3[:, i0:i0 + n]
                link(v.tensor_reduce(top, w3(vals), AX.X, ALU.max))
                link(v.tensor_tensor(w3(keys), w3(vals), bc(top.unsqueeze(2), shape), ALU.is_equal))
                link(v.tensor_tensor(w3(keys), w3(keys), bc(revE[:, E0 - ne:E0].unsqueeze(1), shape), ALU.mult))
                link(v.tensor_reduce(best, w3(keys), AX.X, ALU.max))
                link(v.tensor_tensor(out, w3(keys), bc(best.unsqueeze(2), shape), ALU.is_equal))

            te = lambda a, ne: a.rearrange("p (i e) -> p i e", e=ne)
            et = lambda a, n: a.rearrange("p (e i) -> p e i", i=n)
            by_t = lambda a, n: a.rearrange("p (e i) -> p i e", i=n)

            for n in range(NG + 1):
                if n >= 1:
                    m = n - 1
                    dve.wait_ge(pe_ht, n)
                    v.tensor_tensor(featT[:, m * GP:n * GP].rearrange("p (b s) -> p b s", s=S),
                                    PS[5][:, :].rearrange("p (b s) -> p b s", s=S),
                                    bc(c0bT[:, m * GB:n * GB].unsqueeze(2), [P, GB, S]),
                                    ALU.add).then_inc(hT_done, 1)
                if n < NG:
                    for b in range(2, 4):
                        dve.wait_ge(pe_c, QB * n + b + 1)
                        v.tensor_copy(condS[b * S:(b + 1) * S, :, :],
                                      PS[1 + b][0:S, :].rearrange("p (i h) -> p i h", h=H)).then_inc(condD, 1)
                if n == 0:
                    dve.wait_ge(pe_tab, 1)
                    link(v.tensor_copy(c0bT[:, :], PS[6][:, 0:B]))
                    link(v.tensor_copy(gamT[:, :], PS[6][:, B:2 * B]))
                    link(v.tensor_copy(betT[:, :], PS[6][:, 2 * B:3 * B]))
                    v.engine_nop().then_inc(tab_done, 1)
                if n >= 1:
                    dve.wait_ge(pe_l, n)
                    v.tensor_copy(lg[:, m * G * E0:n * G * E0], PS[6][:, 0:G * E0]).then_inc(lg_done, 1)
                    if n * G % RT == 0:
                        dve.wait_ge(lg_done, n)
                        first_max(lg, E0, t1, by_t(mask[:, :], NT)[:, n * G - RT:n * G, :], n * G - RT, RT)

            def glu0(n):
                for c in range(C0):
                    dve.wait_ge(sil_done, C0 * n + c + 1)
                    dve.wait_ge(pe_gu, 2 * C0 * n + 2 * c + 2)
                    if n >= 2:
                        dve.wait_ge(pe_dn, n - 1)
                    v.tensor_tensor(act[n % 2][:, c, :], PS[2 * c + 1][:, :], sil[:, c, :],
                                    ALU.mult).then_inc(act_done, 1)

            def add0(n):
                dve.wait_ge(pe_dn, n + 1)
                a = acc[:, n * G:(n + 1) * G, :]
                v.tensor_tensor(a, a, PS[4][:, :].rearrange("p (i h) -> p i h", h=H), ALU.add).then_inc(acc0, 1)

            v.engine_nop().then_inc(mx0, 1)
            link(v.tensor_tensor_scan(seen[:, :], rst[:, :], mask[:, :], 0.0, ALU.mult, ALU.add))
            v.engine_nop().then_inc(mk0, 1)
            glu0(0)
            dve.wait_ge(pe_rank0, 1)
            link(v.tensor_scalar(padI[:, :], PS[6][:, 0:E0], float(P - 1), None, ALU.add))
            link(v.tensor_scalar(padI[:, :], padI[:, :], P.bit_length() - 1, P.bit_length() - 1,
                                 ALU.arith_shift_right, ALU.arith_shift_left))
            link(v.tensor_copy(padF[:, :], padI[:, :]))
            link(v.tensor_tensor_scan(endE[:, :], ones_f[:, :], padF[:, :], 0.0, ALU.mult, ALU.add))
            link(v.tensor_tensor(padF[:, :], endE[:, :], padF[:, :], ALU.subtract))
            dve.wait_ge(pe_rank0, 2)
            HN = NT // 2
            for h in range(2):
                own = lambda a: et(a, NT)[:, :, h * HN:(h + 1) * HN]
                link(v.tensor_tensor(own(t3[:, :]), own(PS[5][:, :]), bc(padF[:, :].unsqueeze(2), [P, E0, HN]),
                                     ALU.add))
                link(v.tensor_tensor(own(t3[:, :]), own(t3[:, :]), own(mask[:, :]), ALU.mult))
                link(v.tensor_reduce(slotF[:, 0, h * HN:(h + 1) * HN], own(t3[:, :]).rearrange("p e i -> p i e"),
                                     AX.X, ALU.add))
                v.tensor_copy(slot[:, 0, h * HN:(h + 1) * HN], slotF[:, 0, h * HN:(h + 1) * HN]).then_inc(slots0, 1)

            def split_gate_up(r):
                for e in (2 * r, 2 * r + 1):
                    w = c0w[:, e % 4 * F0x2:(e % 4 + 1) * F0x2]
                    high, low = (a[:, e * F0x2:(e + 1) * F0x2] for a in (w_guh, w_gul))
                    dve.wait_ge(g_hi, e + 1)
                    v.tensor_tensor(low, w, high.bitcast(fp32), ALU.subtract).then_inc(g_lo, 1)

            for n in range(1, NG + 1):
                if n < NG:
                    glu0(n)
                    for r in split_rounds(n):
                        split_gate_up(r)
                add0(n - 1)
                if n == 1:
                    link(v.tensor_tensor(cmpj[:, :, :], bc(jrow[:, :].unsqueeze(2), [1, NBLKP, E0 - 1]),
                                         bc(endE[0:1, 0:E0 - 1].unsqueeze(1), [1, NBLKP, E0 - 1]), ALU.is_ge))
                    link(v.tensor_reduce(bexp[:, :], cmpj[:, :, :], AX.X, ALU.add))
                    v.tensor_scalar(w_at[:, 0:NBLKP, 0], bexp[:, :], float(F0x2), None, ALU.mult)
                    v.tensor_scalar(w_at[:, 2:NBLKP + 2, 1], bexp[:, :], float(C0 * H), None,
                                    ALU.mult).then_inc(blocks0, 1)

            def index(c, turn):
                dve.wait_ge(bx_ld[c % 4], turn * 32 + (c // 4 + 1) * 16)
                v.tensor_scalar(blk_i[c][:, :], blk_x[c % 4][:, H:ROW], -1.0, float(FAR), ALU.mult,
                                ALU.add).then_inc(e_ix, 1)

            def low(j, k):
                dve.wait_ge(e_xc, j + 1)
                v.tensor_tensor(blk_xl[k][:, :], PS[5 + k][:, 0:P], blk_xh[k][:, :].bitcast(fp32),
                                ALU.subtract).then_inc(e_xl, 1)

            def glu(j, k):
                dve.wait_ge(e_sl, j + 1)
                v.tensor_tensor(blk_a[k][:, :], PS[k][:, F0:F0x2], blk_s[k][:, :], ALU.mult).then_inc(e_ac, 1)

            def result(j, s, stored=None):
                dve.wait_ge(e_dn, j + 1)
                if stored is not None:
                    dve.wait_ge(by_st[s], stored)
                v.tensor_copy(blk_y[s][:, :], PS[4 if s % 2 == 0 else 7][:, 0:H]).then_inc(e_oc, 1)

            def dve_stage(j, c, turn=0, stored=None):
                if not (isinstance(j, int) and j + 1 == NBLKP):
                    low(j + 1, (c + 1) % 2)
                index(c, turn)
                glu(j, c % 2)
                if not (isinstance(j, int) and j < 2):
                    result(j - 2, (c - 2) % 4, stored)

            low(0, 0)
            for j in range(8):
                dve_stage(j, j, stored=16 if j >= 6 else None)
            with dve.Fori(0, NBLKP // 8 - 2) as it:
                for c in range(8):
                    dve_stage(it * 8 + (8 + c), c, it + 1, it * 32 + 16 * ((c + 2) // 4 + 1))
            for j in range(NBLKP - 8, NBLKP):
                dve_stage(j, j % 8, NBLKP // 8 - 1, 16 * ((j - 2) // 4))
            for j in range(NBLKP - 2, NBLKP):
                result(j, j % 4, 16 * (j // 4))

            dve.wait_ge(acc0, NG)

            WE = NT * E1
            L3 = [P, NT, E1]

            def choice_slots(k, i0, n, pos):
                cols = slice(k * WE + i0 * E1, k * WE + (i0 + n) * E1)
                link(v.scalar_tensor_tensor(out=keep[:, cols], in0=pos, scalar=float(CAP), in1=mask[:, cols],
                                            op0=ALU.is_lt, op1=ALU.mult))
                link(v.tensor_tensor(et(t3[:, cols], n), et(pos, n), bc(baseE[:, :].unsqueeze(2), [P, E1, n]),
                                     ALU.add))
                if k == 0:
                    v.engine_nop().then_inc(b_rk, 1)
                link(v.tensor_tensor(t3[:, cols], t3[:, cols], keep[:, cols], ALU.mult))
                link(v.tensor_reduce(slotF[:, k, i0:i0 + n], by_t(t3[:, cols], n), AX.X, ALU.add))
                v.tensor_scalar(slot[:, k, i0:i0 + n], slotF[:, k, i0:i0 + n], float(DROP), None,
                                ALU.add).then_inc(slots1, 1)

            def first_choices(r):
                cols = slice(r * RT * E1, (r + 1) * RT * E1)
                first_max(lg, E1, t2, by_t(mask[:, cols], RT), r * RT, RT)
                link(v.tensor_tensor_scan(seen[:, cols], rst1[:, :], mask[:, cols], 0.0, ALU.mult, ALU.add))
                v.engine_nop().then_inc(mk1, 1)

            def first_slots(r):
                dve.wait_ge(pe_rank1, r + 1)
                last = et(seen[:, r * RT * E1:(r + 1) * RT * E1], RT)[:, :, RT - 1]
                if r == 0:
                    link(v.tensor_copy(before[:, :], last))
                else:
                    link(v.tensor_tensor(before[:, :], before[:, :], last, ALU.add))
                choice_slots(0, r * RT, RT, PS[7][:, WE:WE + RT * E1])

            def x1_low(n):
                dve.wait_ge(b_xc, n + 1)
                if n >= 2:
                    dve.wait_ge(b_w1, NCH * (n - 1))
                v.tensor_tensor(xl[n % 2][:, :], PS[0][:, :], xh[n % 2][:, :].bitcast(fp32),
                                ALU.subtract).then_inc(b_xl, 1)

            dve.wait_ge(ld_l1, 16 * (2 * (NCH - 1) + 8))
            link(v.tensor_copy(a_w1h[:, :], a_w1[:, :]))
            v.tensor_tensor(a_w1l[:, :], a_w1[:, :], a_w1h[:, :].bitcast(fp32), ALU.subtract).then_inc(b_ws, 1)
            link(v.tensor_copy(sw1h[:, :], sw1[:, :]))
            v.tensor_tensor(sw1l[:, :], sw1[:, :], sw1h[:, :].bitcast(fp32), ALU.subtract).then_inc(b_ws, 1)
            def split_features(n):
                dve.wait_ge(b_w1, NCH * min(NG - 1 + n, NG))
                if n >= 2:
                    dve.wait_ge(s_gu, C1 * (n - 1))
                f = featT[:, n * GP:(n + 1) * GP]
                link(v.tensor_copy(xh[n % 2][:, :], f))
                v.tensor_tensor(xl[n % 2][:, :], f, xh[n % 2][:, :].bitcast(fp32), ALU.subtract).then_inc(s_sp, 1)

            for n in range(2):
                residual(v, dve, n)
            x1_low(0)
            for n in range(NG + 3):
                if n == NG:
                    split_features(0)
                if n + 1 < NG:
                    x1_low(n + 1)
                if (n - 3) * G % RT == 0 and n > 3:
                    first_slots((n - 3) * G // RT - 1)
                if 1 <= n < NG + 1:
                    m = n - 1
                    k = m % 2
                    dve.wait_ge(b_w2, n)
                    dve.wait_ge(x1_done, n)
                    if m >= 2:
                        dve.wait_ge(b_nt, m - 1)
                    link(v.tensor_tensor(nrm[k][:, :, :], PS[4][:, :].rearrange("p (i h) -> p i h", h=H),
                                         acc[:, m * G:(m + 1) * G, :], ALU.add))
                    for i in range(G):
                        ins = v.bn_stats(bn6[:, i, :], nrm[k][:, i, :])
                    link(ins)
                    for i in range(G):
                        ins = v.bn_aggr(mv[:, i, :], bn6[:, i, :])
                    ins.then_inc(b_var, 1)
                if 2 <= n < NG + 2:
                    g = n - 2
                    dve.wait_ge(b_nt, g + 1)
                    f3 = featT[:, g * GP:(g + 1) * GP].rearrange("p (b s) -> p b s", s=S)
                    link(v.tensor_tensor(f3, PS[5][:, :].rearrange("p (b s) -> p b s", s=S),
                                         bc(gamT[:, g * GB:(g + 1) * GB].unsqueeze(2), [P, GB, S]), ALU.mult))
                    v.tensor_tensor(f3, f3, bc(betT[:, g * GB:(g + 1) * GB].unsqueeze(2), [P, GB, S]),
                                    ALU.add).then_inc(b_xn, 1)
                if 1 <= n < NG + 1:
                    dve.wait_ge(b_std, n)
                    link(v.reciprocal(rstd[k][:, :], rstd[k][:, :]))
                    v.scalar_tensor_tensor(out=nmr[k][:, :], in0=mv[:, :, 0], scalar=-1.0, in1=rstd[k][:, :],
                                           op0=ALU.mult, op1=ALU.mult).then_inc(b_nb, 1)
                if n >= 3:
                    m = n - 3
                    dve.wait_ge(b_lg, m + 1)
                    v.tensor_copy(lg[:, m * G * E1:(m + 1) * G * E1], PS[7][:, 0:G * E1]).then_inc(b_lc, 1)
                    if (m + 1) * G % RT == 0:
                        dve.wait_ge(b_lc, m + 1)
                        first_choices((m + 1) * G // RT - 1)

            def add1(n):
                dve.wait_ge(s_dn, n + 1)
                a = acc[:, n * G:(n + 1) * G, :]
                link(v.scalar_tensor_tensor(out=a, in0=PS[4][:, :].rearrange("p (i h) -> p i h", h=H),
                                            scalar=SHARED_SCALE, in1=a, op0=ALU.mult, op1=ALU.add))
                v.tensor_tensor(a, a, bc(sb2[:, :].unsqueeze(1), [P, G, H]), ALU.add).then_inc(s_ac, 1)

            link(v.tensor_reduce(m1[:, :], te(lg[:, 0:WE], E1), AX.X, ALU.max))
            v.tensor_tensor(te(t1[:, 0:WE], E1), te(lg[:, 0:WE], E1), bc(m1[:, :].unsqueeze(2), L3),
                            ALU.subtract).then_inc(ex_in, 1)
            first_slots(NT // RT - 1)
            split_features(1)
            split_features(2)
            dve.wait_ge(ex_out, 1)
            link(v.tensor_reduce(m1[:, :], te(t1[:, 0:WE], E1), AX.X, ALU.add))
            link(v.reciprocal(m1[:, :], m1[:, :]))
            link(v.tensor_tensor(te(lg[:, 0:WE], E1), te(t1[:, 0:WE], E1), bc(m1[:, :].unsqueeze(2), L3), ALU.mult))
            parts = lambda a: a.rearrange("p (r e i) -> p r i e", e=E1, i=RT)
            rie = lambda a: a.rearrange("p (r i e) -> p r i e", e=E1, i=RT)
            link(v.tensor_scalar(rie(t2[:, 0:WE]), parts(mask[:, 0:WE]), -1.0, 1.0, ALU.mult, ALU.add))
            link(v.tensor_tensor(t2[:, 0:WE], lg[:, 0:WE], t2[:, 0:WE], ALU.mult))
            first_max(t2, E1, t1, by_t(mask[:, WE:2 * WE], NT), 0, NT)
            link(v.tensor_tensor_scan(seen[:, WE:2 * WE], rst[:, 0:WE], mask[:, WE:2 * WE], 0.0, ALU.mult, ALU.add))
            v.engine_nop().then_inc(mk1, 1)
            link(v.tensor_scalar(sb2[:, :], sb2[:, :], SHARED_SCALE, None, ALU.mult))
            dve.wait_ge(pe_rank1, NT // RT + 1)
            link(v.tensor_scalar(cnt1[:, :], PS[6][:, 0:E1], float(CAP), None, ALU.min))
            link(v.tensor_tensor(et(t1[:, 0:WE], NT), et(PS[5][:, 0:WE], NT), bc(cnt1[:, :].unsqueeze(2), [P, E1, NT]),
                                 ALU.add))
            choice_slots(1, 0, NT, t1[:, 0:WE])
            for n in range(3):
                add1(n)
                split_features(n + 3)
            link(v.tensor_tensor(rie(t2[:, 0:WE]), parts(keep[:, 0:WE]), rie(lg[:, 0:WE]), ALU.mult))
            link(v.tensor_tensor(te(t2[:, WE:2 * WE], E1), by_t(keep[:, WE:2 * WE], NT), te(lg[:, 0:WE], E1), ALU.mult))
            link(v.tensor_reduce(wk[:, :, :], t2[:, :].rearrange("p (k i e) -> p k i e", k=TOP_K, e=E1), AX.X, ALU.add))
            link(v.tensor_tensor(m1[:, :], wk[:, 0, :], wk[:, 1, :], ALU.add))
            link(v.tensor_scalar(m1[:, :], m1[:, :], TINY, None, ALU.max))
            link(v.reciprocal(m1[:, :], m1[:, :]))
            link(v.tensor_tensor(wk[:, :, :], wk[:, :, :], bc(m1[:, :].unsqueeze(1), [P, TOP_K, NT]), ALU.mult))
            for n in range(3, NG - 1):
                add1(n)
                if n + 3 < NG:
                    split_features(n + 3)

            def q_index(k, turn):
                dve.wait_ge(gx_ld[k], turn * 16 + 16)
                v.tensor_scalar(grp_i[k][:, :], grp_x[k][:, :, H], -1.0, float(FAR), ALU.mult,
                                ALU.add).then_inc(q_ix, 1)

            def q_low(q, k):
                dve.wait_ge(q_xc, q + 1)
                v.tensor_tensor(xl[k][:, 0:UP], PS[0][:, 0:UP], xh[k][:, 0:UP].bitcast(fp32),
                                ALU.subtract).then_inc(q_xl, 1)

            def split_weights(k, loaded, e2):
                dve.wait_ge(w_ld[k], loaded)
                v.tensor_copy(w1h[k][:, :], w1r[k][:, :]).then_inc(w_sp, 1)
                dve.wait_ge(w_sp, e2 + 1)
                v.tensor_tensor(w1l[k][:, :], w1r[k][:, :], w1h[k][:, :].bitcast(fp32), ALU.subtract).then_inc(w_sp, 1)

            def q_result(q, k, e, turn=None):
                dve.wait_ge(q_dn, q + 1)
                if turn is not None:
                    dve.wait_ge(gy_st[k], turn * (16 * U))
                v.tensor_tensor(grp_y[k][:, :, :], PS[5 + k][:, 0:UP].rearrange("p (u h) -> p u h", h=H),
                                bc(b2r[e][:, :].unsqueeze(1), [P, U, H]), ALU.add).then_inc(q_oc, 1)

            def q_stage(q, b, it2=0, itg=0, it4=0, it16=0):
                if not (isinstance(q, int) and q + 2 >= NQ):
                    q_index((b + 2) % NX, it2 + (b + 2) // NX)
                    q_low(q + 2, b % 2)
                q_result(q, b % 2, b // GPE % 2, itg + b // 2 if b >= 2 else None)
                if b % (2 * GPE) == 1:
                    split_weights(1, it16 + 16 * (b // (2 * GPE) + 1), it4 + (b // (2 * GPE) * 4 + 2))
                if b % (2 * GPE) == GPE + 1 and not (isinstance(q, int) and q + GPE >= NQ):
                    split_weights(0, it16 + 16 * (b // (2 * GPE) + 2), it4 + (b // (2 * GPE) * 4 + 4))

            split_weights(0, 16, 0)
            q_index(0, 0)
            q_low(0, 0)
            add1(NG - 1)
            q_index(1, 0)
            q_low(1, 1)
            for q in range(2):
                q_stage(q, q)
            with dve.Fori(0, E1 // 2 - 1) as it:
                for u in range(2 * GPE):
                    q_stage(it * (2 * GPE) + (2 + u), 2 + u, it * 2, it * GPE, it * 4, it * 16)
            for q in range(2 + (E1 // 2 - 1) * 2 * GPE, NQ):
                q_stage(q, q)

            for g in range(NG):
                dve.wait_ge(fy_ld[g], 16 * TOP_K)
                for i in range(G):
                    t = g * G + i
                    ins = v.scalar_tensor_tensor(out=acc[:, t, :], in0=back[0][g][:, i, :], scalar=wk[:, 0, t:t + 1],
                                                 in1=acc[:, t, :], op0=ALU.mult, op1=ALU.add)
                link(ins)
                dve.wait_ge(f_sc, g + 1)
                a = acc[:, g * G:(g + 1) * G, :]
                v.tensor_tensor(a, a, back[1][g][:, :, :], ALU.add).then_inc(f_ac, 1)

        @block.tensor
        def _(pe):
            def tr(dst, src, k=P):
                return nc.tensor.transpose(dst, src, ident[0:k, 0:k])

            def x_in(n):
                pe.wait_ge(x_ld[n], 16)
                if n >= 1:
                    pe.wait_ge(xT_done, n)
                for i in range(G):
                    last = tr(tile(PS[0], i), acc[:, n * G + i, :])
                last.then_inc(pe_xt, 1)

            def keep_busy(bank, n):
                for _ in range(n):
                    mm(bank[:, :], ident[:, :], zrow[:, 0:512], start=True, stop=True)

            pe.wait_ge(poolk, 3)
            keep_busy(PS[7], 1)
            x_in(0)
            keep_busy(PS[7], 1)
            for n in range(NG + 1):
                if n + 1 < NG:
                    x_in(n + 1)
                if n >= 1:
                    pe.wait_ge(condA, 2 * n)
                    pe.wait_ge(condD, 2 * n)
                    if n == 1:
                        pe.wait_ge(tab_done, 1)
                    else:
                        pe.wait_ge(hT_done, n - 1)
                    for i in range(G):
                        last = tr(tile(PS[5], i), condS[:, i, :])
                    last.then_inc(pe_ht, 1)
                if n < NG:
                    pe.wait_ge(xT_done, n + 1)
                    if n == 0:
                        pe.wait_ge(ld_c0w, 16)
                        pe.wait_ge(off_ready, 1)
                    _, offs = nc.values_load_multi_w_load_instructions(
                        w0off[0:1, n * GB:(n + 1) * GB], engines=(mybir.EngineType.PE,), min_val=0,
                        max_val=(NSUB - 1) * H, skip_runtime_bounds_check_because="subjects are under NSUB")
                    for b in range(QB):
                        for i in range(G):
                            t = i * QB + b
                            last = mm(PS[1 + b][0:S, i * H:(i + 1) * H],
                                      xT[n % 2][:, t * S:(t + 1) * S], c0w[:, ds(offs[t], H)],
                                      start=True, stop=True)
                        last.then_inc(pe_c, 1)
                if n == 0:
                    pe.wait_ge(dve_ready, 2)
                    pe.wait_ge(ld_tab, 16 * 7)
                    mm(PS[6][:, 0:B], c0bs[:, :], hot0[:, :], start=True, stop=True)
                    mm(PS[6][:, B:2 * B], gam[:, :], hot1[:, :], start=True, stop=True)
                    mm(PS[6][:, 2 * B:3 * B], bet[:, :], hot1[:, :], start=True, stop=True).then_inc(pe_tab, 1)
                if n >= 1:
                    m = n - 1
                    pe.wait_ge(hT_done, n)
                    if m >= 1:
                        pe.wait_ge(lg_done, m)
                        pe.wait_ge(tok_done, m)
                    for i in range(G):
                        last = mm(PS[6][:, i * E0:(i + 1) * E0], tile(featT, m * G + i), rt0[:, :],
                                  start=True, stop=True)
                    last.then_inc(pe_l, 1)
                    for i in range(G):
                        last = tr(tile(PS[7], i), tile(featT, m * G + i))
                    last.then_inc(pe_tok, 1)

            def shared0_up(n):
                for c in range(C0):
                    for w, b in ((shg, 2 * c), (shu, 2 * c + 1)):
                        if n >= 1:
                            pe.wait_ge(act_done, C0 * (n - 1) + c + 1)
                        mm(PS[b][:, :], w[:, c * P:(c + 1) * P], featT[:, n * GP:(n + 1) * GP],
                           start=True, stop=True).then_inc(pe_gu, 1)

            def shared0_down(n):
                pe.wait_ge(act_done, C0 * (n + 1))
                if n >= 1:
                    pe.wait_ge(acc0, n)
                for i in range(G):
                    for c in range(C0):
                        last = mm(tile(PS[4], i), tile(act[n % 2][:, c, :], i), shd[:, c, :],
                                  start=c == 0, stop=c == C0 - 1)
                last.then_inc(pe_dn, 1)

            pe.wait_ge(ld_sh0, 48)
            shared0_up(0)
            pe.wait_ge(mk0, 1)
            pe.wait_ge(poolk, 19)
            mm(PS[6][:, 0:E0], ones_b[:, :], seen[:, :].rearrange("p (e i) -> p e i", i=NT)[:, :, NT - 1],
               start=True, stop=True).then_inc(pe_rank0, 1)
            mm(PS[5][:, :], tri[:, :], mask[:, :], start=True, stop=False)
            mm(PS[5][:, :], ones_b[:, :], seen[:, :], start=False, stop=True).then_inc(pe_rank0, 1)
            for n in range(1, NG):
                shared0_up(n)
                shared0_down(n - 1)
            shared0_down(NG - 1)

            def x_tr(j, s, turn, k):
                pe.wait_ge(bx_ld[s], turn * 16 + 16)
                tr(PS[5 + k][:, 0:P], blk_x[s][:, 0:H]).then_inc(e_xt, 1)

            def gate_up(j, k, off):
                pe.wait_ge(e_xl, j + 1)
                high, low = (w[:, ds(off, F0x2)] for w in (w_guh, w_gul))
                mm(PS[k][:, :], blk_xh[k][:, :], high, start=True, stop=False)
                mm(PS[k][:, :], blk_xh[k][:, :], low, start=False, stop=False)
                mm(PS[k][:, :], blk_xl[k][:, :], high, start=False, stop=True).then_inc(e_gu, 1)

            def a_tr(j, k):
                pe.wait_ge(e_ac, j + 1)
                for c in range(C0):
                    last = tr(tile(PS[2 + k], c), tile(blk_a[k], c))
                last.then_inc(e_ta, 1)

            def down(j, k, off, first=False):
                pe.wait_ge(e_at, j + 1)
                if not first:
                    pe.wait_ge(e_oc, j - 1)
                for c in range(C0):
                    last = mm(PS[4 if k == 0 else 7][:, 0:H], blk_aT[k][:, c * P:(c + 1) * P],
                              w_dn[:, ds(off + c * H, H)], start=c == 0, stop=c == C0 - 1)
                last.then_inc(e_dn, 1)

            def offsets(j, n):
                _, vals = nc.values_load_multi_w_load_instructions(
                    w_at[0:1, ds(j, n), :].rearrange("o j k -> o (j k)"), engines=(mybir.EngineType.PE,), min_val=0,
                    max_val=(E0 - 1) * max(F0x2, C0 * H),
                    skip_runtime_bounds_check_because="a count of at most E0 - 1, times the stride")
                return vals[0::2], [nc.s_assert_within(
                    v, 0, (E0 - 1) * C0 * H, skip_runtime_bounds_check_because="the down weights' stride")
                    for v in vals[1::2]]

            pe.wait_ge(acc0, NG)
            pe.wait_ge(blocks0, 1)
            pe.wait_ge(slots0, 2)
            pe.wait_ge(tok_done, NG)
            pe.wait_ge(g_lo, E0)
            pe.wait_ge(ld_dn, 16)

            def pe_stages(j0, turn, offs_g, offs_d):
                for i in range(len(offs_g)):
                    j = j0 + i
                    static = isinstance(j, int)
                    if not (static and j == NBLKP - 1):
                        x_tr(j + 1, (i + 1) % 4, turn + (i + 1) // 4, (i + 1) % 2)
                    gate_up(j, i % 2, offs_g[i])
                    if not (static and j < 2):
                        down(j - 2, i % 2, offs_d[i], first=static and j < 4)
                    if not (static and j < 1):
                        a_tr(j - 1, (i + 1) % 2)

            x_tr(0, 0, 0, 0)
            pe_stages(0, 0, *offsets(0, 4))
            with pe.Fori(0, (NBLKP - 8) // 8) as it:
                pe_stages(it * 8 + 4, it * 2 + 1, *offsets(it * 8 + 4, 8))
            og, od = offsets(NBLKP - 4, 6)
            pe_stages(NBLKP - 4, NBLKP // 4 - 1, og[:4], od[:4])
            down(NBLKP - 2, 0, od[4])
            a_tr(NBLKP - 1, 1)
            down(NBLKP - 1, 1, od[5])

            pe.wait_ge(e_oc, NBLKP)
            pe.wait_ge(ld_l1, 16 * (2 * (NCH - 1) + 8))
            def x1_in(n):
                pe.wait_ge(x1_done, n + 1)
                if n >= 1:
                    pe.wait_ge(b_xl, n)
                for i in range(G):
                    last = tr(tile(PS[0], i), acc[:, n * G + i, :])
                last.then_inc(b_xt, 1)

            WE = NT * E1

            def rank1(r):
                cols = slice(r * RT * E1, (r + 1) * RT * E1)
                pos = PS[7][:, WE:WE + RT * E1]
                pe.wait_ge(mk1, r + 1)
                pe.wait_ge(b_lc, (r + 1) * RT // G)
                mm(pos, tri[:, :], mask[:, cols], start=True, stop=False)
                last = mm(pos, ones_b[:, :], seen[:, cols], start=False, stop=r == 0)
                if r:
                    last = mm(pos.rearrange("p (e i) -> p e i", i=RT), ones_b[:, :],
                              before[:, :].unsqueeze(2).to_broadcast([P, E1, RT]), start=False, stop=True)
                last.then_inc(pe_rank1, 1)

            def shared1_up(n, chunks=range(C1)):
                pe.wait_ge(s_sp, n + 1)
                for c in chunks:
                    if n >= 1:
                        pe.wait_ge(s_sl, C1 * (n - 1) + c + 1)
                    high, low = sw1h[:, c * P:(c + 1) * P], sw1l[:, c * P:(c + 1) * P]
                    mm(PS[c][:, :], high, xh[n % 2][:, :], start=True, stop=False)
                    mm(PS[c][:, :], high, xl[n % 2][:, :], start=False, stop=False)
                    mm(PS[c][:, :], low, xh[n % 2][:, :], start=False, stop=True).then_inc(s_gu, 1)

            keep_busy(PS[1], 7)
            pe.wait_ge(b_ws, 2)
            x1_in(0)
            for n in range(NG + 3):
                if n == NG + 1:
                    pe.wait_ge(b_xl, NG)
                    pe.wait_ge(b_rl, NCH * NG)
                    pe.wait_ge(b_var, NG)
                    shared1_up(0)
                if n + 1 < NG:
                    x1_in(n + 1)
                if n < NG:
                    pe.wait_ge(b_xc, n + 1)
                    if n >= 1:
                        pe.wait_ge(b_rl, NCH * n)
                    for c in range(NCH):
                        cols = slice(c * P, (c + 1) * P)
                        mm(PS[1 + c][:, :], a_w1h[:, cols], xh[n % 2][:, :], start=True, stop=False)
                        mm(PS[1 + c][:, :], a_w1l[:, cols], xh[n % 2][:, :], start=False, stop=False)
                    pe.wait_ge(b_xl, n + 1)
                    for c in range(NCH):
                        cols = slice(c * P, (c + 1) * P)
                        mm(PS[1 + c][:, :], a_w1h[:, cols], xl[n % 2][:, :], start=False, stop=False)
                        mm(PS[1 + c][:, :].rearrange("p (b s) -> p b s", s=S), other[:, cols],
                           hot1b[:, n * GB:(n + 1) * GB].unsqueeze(2).to_broadcast([NLANG, GB, S]),
                           start=False, stop=True).then_inc(b_w1, 1)
                if 1 <= n < NG + 1:
                    m = n - 1
                    pe.wait_ge(b_rl, NCH * n)
                    if m >= 1:
                        pe.wait_ge(b_var, m)
                    for i in range(G):
                        if i == 2 and (n - 3) * G % RT == 0 and n > 3:
                            rank1((n - 3) * G // RT - 1)
                        for c in range(NCH):
                            last = mm(tile(PS[4], i), tile(act[m % 2][0:KROWS[c], c, :], i),
                                      a_w2[0:KROWS[c], c, :], start=c == 0, stop=c == NCH - 1)
                    last.then_inc(b_w2, 1)
                elif (n - 3) * G % RT == 0 and n > 3:
                    rank1((n - 3) * G // RT - 1)
                if 2 <= n < NG + 2:
                    m = n - 2
                    pe.wait_ge(b_nm, m + 1)
                    if m >= 1:
                        pe.wait_ge(b_xn, m)
                    for i in range(G):
                        last = tr(tile(PS[5], i), nrm[m % 2][:, i, :])
                    last.then_inc(b_nt, 1)
                if n >= 3:
                    m = n - 3
                    pe.wait_ge(b_xn, m + 1)
                    if m >= 1:
                        pe.wait_ge(b_lc, m)
                        if m * G >= RT:
                            pe.wait_ge(b_rk, m * G // RT)
                        pe.wait_ge(b_tk, m)
                    for i in range(G):
                        last = mm(PS[7][:, i * E1:(i + 1) * E1], tile(featT, m * G + i), rt1[:, :],
                                  start=True, stop=True)
                    last.then_inc(b_lg, 1)
                    for i in range(G):
                        last = tr(tile(PS[6], i), tile(featT, m * G + i))
                    last.then_inc(b_bt, 1)

            def shared1_down(n):
                pe.wait_ge(s_sl, C1 * (n + 1))
                if n >= 1:
                    pe.wait_ge(s_ac, n)
                for i in range(G):
                    for c in range(C1):
                        last = mm(tile(PS[4], i), tile(act[n % 2][:, c, :], i), sw2[:, c, :],
                                  start=c == 0, stop=c == C1 - 1)
                last.then_inc(s_dn, 1)

            rank1(NT // RT - 1)
            shared1_down(0)
            shared1_up(1)
            shared1_up(2, range(C1 // 2))
            pe.wait_ge(b_tk, NG)
            pe.wait_ge(mk1, NT // RT + 1)
            mm(PS[6][:, 0:E1], ones_b[:, :], before[:, :], start=True, stop=True)
            mm(PS[5][:, 0:WE], tri[:, :], mask[:, WE:2 * WE], start=True, stop=False)
            mm(PS[5][:, 0:WE], ones_b[:, :], seen[:, WE:2 * WE], start=False, stop=True).then_inc(pe_rank1, 1)
            shared1_up(2, range(C1 // 2, C1))
            shared1_down(1)
            for n in range(3, NG):
                shared1_up(n)
                shared1_down(n - 1)

            def q_tr(k, turn):
                pe.wait_ge(gx_ld[k], turn * 16 + 16)
                for u in range(U):
                    last = tr(tile(PS[0], u), grp_x[k][:, u, 0:H])
                last.then_inc(q_xt, 1)

            def q_up(q, k, e):
                for c in range(C1):
                    y = PS[1 + k * (C1 // 2) + c // 2][:, (c % 2) * UP:(c % 2 + 1) * UP]
                    high, low = (w[e][:, c * P:(c + 1) * P] for w in (w1h, w1l))
                    mm(y, high, xh[k][:, 0:UP], start=True, stop=False)
                    mm(y, high, xl[k][:, 0:UP], start=False, stop=False)
                    last = mm(y, low, xh[k][:, 0:UP], start=False, stop=True)
                    if c % 2 == 1:
                        last.then_inc(q_gu, 1)

            def q_down(q, k, e, first=False):
                pe.wait_ge(q_sl, q * C1 + C1)
                if not first:
                    pe.wait_ge(q_oc, q - 1)
                for u in range(U):
                    for c in range(C1):
                        last = mm(PS[5 + k][:, u * P:(u + 1) * P], act[k][:, c, u * P:(u + 1) * P],
                                  w2r[e][:, c, :], start=c == 0, stop=c == C1 - 1)
                last.then_inc(q_dn, 1)

            def q_stage(q, w, e, we, k, turn, weights=None, first=False, last=False):
                pe.wait_ge(q_xl, q + 1)
                if not last:
                    q_tr(k, turn)
                if weights is not None:
                    pe.wait_ge(w_sp, weights)
                q_up(q, w, e)
                if not (isinstance(q, int) and q == 0):
                    q_down(q - 1, 1 - w, we, first=first)

            def q_args(b, it2=0, it4=0):
                return (b % 2, b // GPE % 2, (b - 1) // GPE % 2, (b + 1) % NX, it2 + (b + 1) // NX,
                        it4 + 2 * (b // GPE + 1) if b % GPE == 0 else None)

            pe.wait_ge(s_sl, C1 * (NG - 1) + 1)
            q_tr(0, 0)
            shared1_down(NG - 1)
            q_stage(0, *q_args(0), first=True)
            pe.wait_ge(s_ac, NG)
            for q in range(1, 3):
                q_stage(q, *q_args(q), first=True)
            with pe.Fori(0, E1 // 2 - 1) as it:
                for u in range(2 * GPE):
                    q_stage(it * (2 * GPE) + (3 + u), *q_args(3 + u, it * 2, it * 4))
            for q in range(3 + (E1 // 2 - 1) * 2 * GPE, NQ):
                q_stage(q, *q_args(q), last=q == NQ - 1)
            q_down(NQ - 1, (NQ - 1) % 2, (E1 - 1) % 2)


def kernel(**inputs):
    import numpy as np
    import concourse.bacc as bacc
    from concourse import mybir
    from concourse.bass_utils import run_bass_kernel_spmd

    i = {k: np.asarray(a) for k, a in inputs.items()}
    x = i["x"]
    nb, ns, h = x.shape
    lw1 = i["L1_cond_W1"]
    nl, _, na = lw1.shape
    e1, f1 = i["L1_ffn_b1"].shape
    arrays = {
        "x": x.reshape(nb * ns, h),
        "subj": i["itok_B_0_15"].reshape(1, nb),
        "lang": i["itok_B_0_8"].reshape(1, nb),
        "c0_w": i["L0_cond_weights"],
        "c0_b": i["L0_cond_b"],
        "f0_router": i["L0_ffn_w_router"].T,
        "f0_gate_up": i["L0_ffn_gate_up_proj"],
        "f0_down": i["L0_ffn_down_proj"],
        "f0_sh_gate": i["L0_ffn_w_gate"].T,
        "f0_sh_up": i["L0_ffn_w_up"].T,
        "f0_sh_down": i["L0_ffn_w_down"].T,
        "c1_w1": lw1.transpose(1, 0, 2).reshape(h, nl * na),
        "c1_b1": i["L1_cond_b1"].reshape(nl * na, 1),
        "c1_w2": i["L1_cond_W2"].reshape(nl * na, h),
        "c1_b2": i["L1_cond_b2"],
        "c1_gamma": i["L1_cond_gamma"],
        "c1_beta": i["L1_cond_beta"],
        "f1_router": i["L1_ffn_router_w"],
        "f1_w1": i["L1_ffn_w1"],
        "f1_b1": i["L1_ffn_b1"].reshape(e1, f1 // 128, 128).transpose(0, 2, 1),
        "f1_w2": i["L1_ffn_w2"],
        "f1_b2": i["L1_ffn_b2"],
        "f1_sh_w1": i["L1_ffn_sw1"],
        "f1_sh_b1": i["L1_ffn_sb1"].reshape(f1 // 128, 128).T,
        "f1_sh_w2": i["L1_ffn_sw2"],
        "f1_sh_b2": i["L1_ffn_sb2"].reshape(1, h),
    }
    arrays = {k: np.ascontiguousarray(a) for k, a in arrays.items()}
    nc = bacc.Bacc("TRN2", target_bir_lowering=False, num_devices=1)
    args = [nc.dram_tensor(f"in_{k}", a.shape, mybir.dt.from_np(a.dtype), kind="ExternalInput").ap()
            for k, a in arrays.items()]
    res = nc.dram_tensor("out_x", (nb * ns, h), mybir.dt.float32, kind="ExternalOutput").ap()
    adaln_moe_two_layers(nc, *args, res)
    r = run_bass_kernel_spmd(nc, [{f"in_{k}": a for k, a in arrays.items()}], core_ids=[0])
    return r.results[0]["out_x"].reshape(nb, ns, h)
```
